# Optimizing a Trainium2 kernel written in Bass

```python
import numpy as np
import jax
import jax.numpy as jnp

def _softmax(x, axis=-1):
    return jax.nn.softmax(x, axis=axis)

def _gelu(x):
    return jax.nn.gelu(x, approximate=True)

def _silu(x):
    return jax.nn.silu(x)

def _sigmoid(x):
    return jax.nn.sigmoid(x)

def _layernorm(x, axis=-1, eps=1e-05):
    m = jnp.mean(x, axis=axis, keepdims=True)
    v = jnp.var(x, axis=axis, keepdims=True)
    return (x - m) / jnp.sqrt(v + eps)

def _scatter_add(tgt, idx, src, axis=0):
    return tgt.at[idx].add(src)

def _segment_sum(src, seg, n):
    return jax.ops.segment_sum(src, seg, n)
kernel_name = 'mk_sandwich_d1_jaxref_r4_9d0476'

def setup_inputs(seed: int=0):
    np.random.seed(seed)
    _w = jnp.asarray

    def _L0_attn_setup():
        import math
        import jax, jax.numpy as jnp
        import numpy as np
        N_HEAD = 16

        def _reference_tuple_inner(x, W_dq, W_uq, W_dkv, W_uk, W_uv, W_o):
            B, T, C = x.shape
            nh = N_HEAD
            hs = C // nh
            kvl = W_dkv.shape[0]
            k_eff = (W_dq.T @ W_uq.T @ W_uk).reshape(nh, hs, kvl)
            v_eff = (W_uv.T @ W_o.T).reshape(kvl, nh, hs).transpose(1, 0, 2)
            c_kv = x @ W_dkv.T
            q = (x @ W_dq.T @ W_uq.T).reshape(B, T, nh, hs).transpose(0, 2, 1, 3)
            q_lat = jnp.einsum('bhtd,hdl->bhtl', q, k_eff)
            attn = jnp.einsum('bhtl,bsl->bhts', q_lat, c_kv) / math.sqrt(hs)
            causal_mask = jnp.triu(jnp.ones((T, T), bool), k=1)
            attn = jnp.where(causal_mask[None, None], -jnp.inf, attn)
            attn = jax.nn.softmax(attn, axis=-1)
            ctx = jnp.einsum('bhts,bsl->bhtl', attn, c_kv)
            y = jnp.einsum('bhtl,hld->bhtd', ctx, v_eff).transpose(0, 2, 1, 3).reshape(B, T, C)
            return (y, c_kv)
        key = jax.random.key(seed)
        ks = jax.random.split(key, 7)
        B, T, C = (4, 512, 256)
        QL, KVL = (64, 64)
        s = 0.02
        return {'x': jax.random.normal(ks[0], (B, T, C), jnp.float32), 'W_dq': jax.random.normal(ks[1], (QL, C), jnp.float32) * s, 'W_uq': jax.random.normal(ks[2], (C, QL), jnp.float32) * s, 'W_dkv': jax.random.normal(ks[3], (KVL, C), jnp.float32) * s, 'W_uk': jax.random.normal(ks[4], (C, KVL), jnp.float32) * s, 'W_uv': jax.random.normal(ks[5], (C, KVL), jnp.float32) * s, 'W_o': jax.random.normal(ks[6], (C, C), jnp.float32) * s}
    _L0_attn_in = _L0_attn_setup()

    def _L0_ffn_setup():
        import jax, jax.numpy as jnp
        import numpy as np
        E, K, D, F = (8, 2, 256, 1024)
        EPS = 1e-06
        B, S = (2, 256)
        key = jax.random.key(seed)
        ks = jax.random.split(key, 6)
        s_in = 1.0 / np.sqrt(D)
        s_mid = 1.0 / np.sqrt(F)
        return {'x': jax.random.normal(ks[0], (B, S, D), dtype=jnp.float32), 'Wg': jax.random.normal(ks[1], (D, E), dtype=jnp.float32) * s_in, 'gamma': jnp.ones((E, D), dtype=jnp.float32), 'beta': jnp.zeros((E, D), dtype=jnp.float32), 'W1': jax.random.normal(ks[2], (E, D, F), dtype=jnp.float32) * s_in, 'b1': jnp.zeros((E, F), dtype=jnp.float32), 'W2': jax.random.normal(ks[3], (E, F, D), dtype=jnp.float32) * s_mid, 'b2': jnp.zeros((E, D), dtype=jnp.float32)}
    _L0_ffn_in = _L0_ffn_setup()
    _d = {'L0_attn_x': _L0_attn_in['x'], 'L0_attn_W_dq': _L0_attn_in['W_dq'], 'L0_attn_W_uq': _L0_attn_in['W_uq'], 'L0_attn_W_dkv': _L0_attn_in['W_dkv'], 'L0_attn_W_uk': _L0_attn_in['W_uk'], 'L0_attn_W_uv': _L0_attn_in['W_uv'], 'L0_attn_W_o': _L0_attn_in['W_o'], 'L0_ffn_Wg': _L0_ffn_in['Wg'], 'L0_ffn_gamma': _L0_ffn_in['gamma'], 'L0_ffn_beta': _L0_ffn_in['beta'], 'L0_ffn_W1': _L0_ffn_in['W1'], 'L0_ffn_b1': _L0_ffn_in['b1'], 'L0_ffn_W2': _L0_ffn_in['W2'], 'L0_ffn_b2': _L0_ffn_in['b2']}
    _x0 = _d['L0_attn_x']
    _d['L0_attn_x'] = jax.random.normal(jax.random.fold_in(jax.random.key(seed), 1), (4, 1024, 256), dtype=_x0.dtype)
    del _x0
    return _d

def reference(L0_attn_x, L0_attn_W_dq, L0_attn_W_uq, L0_attn_W_dkv, L0_attn_W_uk, L0_attn_W_uv, L0_attn_W_o, L0_ffn_Wg, L0_ffn_gamma, L0_ffn_beta, L0_ffn_W1, L0_ffn_b1, L0_ffn_W2, L0_ffn_b2):

    def _L0_attn_ref(x, W_dq, W_uq, W_dkv, W_uk, W_uv, W_o):
        import math
        import jax, jax.numpy as jnp
        import numpy as np
        N_HEAD = 16

        def _reference_tuple_inner(x, W_dq, W_uq, W_dkv, W_uk, W_uv, W_o):
            B, T, C = x.shape
            nh = N_HEAD
            hs = C // nh
            kvl = W_dkv.shape[0]
            k_eff = (W_dq.T @ W_uq.T @ W_uk).reshape(nh, hs, kvl)
            v_eff = (W_uv.T @ W_o.T).reshape(kvl, nh, hs).transpose(1, 0, 2)
            c_kv = x @ W_dkv.T
            q = (x @ W_dq.T @ W_uq.T).reshape(B, T, nh, hs).transpose(0, 2, 1, 3)
            q_lat = jnp.einsum('bhtd,hdl->bhtl', q, k_eff)
            attn = jnp.einsum('bhtl,bsl->bhts', q_lat, c_kv) / math.sqrt(hs)
            causal_mask = jnp.triu(jnp.ones((T, T), bool), k=1)
            attn = jnp.where(causal_mask[None, None], -jnp.inf, attn)
            attn = jax.nn.softmax(attn, axis=-1)
            ctx = jnp.einsum('bhts,bsl->bhtl', attn, c_kv)
            y = jnp.einsum('bhtl,hld->bhtd', ctx, v_eff).transpose(0, 2, 1, 3).reshape(B, T, C)
            return (y, c_kv)
        return _reference_tuple_inner(x, W_dq, W_uq, W_dkv, W_uk, W_uv, W_o)[0]

    def _L0_ffn_ref(x, Wg, gamma, beta, W1, b1, W2, b2):
        import jax, jax.numpy as jnp
        import numpy as np
        E, K, D, F = (8, 2, 256, 1024)
        EPS = 1e-06
        B, S = (2, 256)
        orig_shape = x.shape
        xf = x.reshape(-1, orig_shape[-1])
        scores = xf @ Wg
        w, idx = jax.lax.top_k(scores, K)
        w = jax.nn.softmax(w, axis=-1)
        mu = jnp.mean(xf, axis=-1, keepdims=True)
        var = jnp.var(xf, axis=-1, keepdims=True)
        xhat = (xf - mu) * jax.lax.rsqrt(var + EPS)
        normed = xhat[None, :, :] * gamma[:, None, :] + beta[:, None, :]
        h = jax.nn.relu(jnp.einsum('end,edf->enf', normed, W1) + b1[:, None, :])
        out = jnp.einsum('enf,efd->end', h, W2) + b2[:, None, :] + xf[None, :, :]
        cw = jnp.sum(w[..., None] * jax.nn.one_hot(idx, E, dtype=w.dtype), axis=1)
        y = jnp.einsum('ne,end->nd', cw, out)
        return y.reshape(orig_shape)
    x = L0_attn_x
    x = x + _layernorm(_L0_attn_ref(_layernorm(x, axis=-1), L0_attn_W_dq, L0_attn_W_uq, L0_attn_W_dkv, L0_attn_W_uk, L0_attn_W_uv, L0_attn_W_o), axis=-1)
    x = x + _layernorm(_L0_ffn_ref(_layernorm(x, axis=-1), L0_ffn_Wg, L0_ffn_gamma, L0_ffn_beta, L0_ffn_W1, L0_ffn_b1, L0_ffn_W2, L0_ffn_b2), axis=-1)
    return x

_drawn_inputs = setup_inputs


def setup_inputs(seed=0):
    import zlib

    import numpy as np

    out = dict(_drawn_inputs(seed))
    spreads = {'L0_ffn_gamma': (1.0, 0.2),
     'L0_ffn_beta': (0.0, 0.348),
     'L0_ffn_b1': (0.0, 0.338),
     'L0_ffn_b2': (0.0, 0.289)}
    factors = {'L0_attn_W_dq': 8.0, 'L0_attn_W_uq': 8.0, 'L0_attn_W_uk': 8.0}
    for name, (base, spread) in spreads.items():
        noise = np.random.default_rng([zlib.crc32(name.encode()), seed]).standard_normal(out[name].shape)
        drawn = base * np.exp(spread * noise) if base else spread * noise
        out[name] = jnp.asarray(drawn.astype(out[name].dtype))
    for name, factor in factors.items():
        out[name] = (out[name] * factor).astype(out[name].dtype)
    return out
```

```python
from contextlib import ExitStack

import numpy as np

import concourse.bass as bass
from concourse import mybir

F32 = mybir.dt.float32
F32R = mybir.dt.float32r
BF16 = mybir.dt.bfloat16
ALU = mybir.AluOpType
ACT = mybir.ActivationFunctionType
AX = mybir.AxisListType

P = 128
B, T, C = 4, 1024, 256
N = B * T
NH, HS, KVL = 16, 16, 64
CT = C // P
CH = 512
NCH = T // CH
TC = CH // P
TB = T // P
GH = 4
NG = NH // GH
KR = 3 * HS
KM = KR + 2
VW = HS + 1
LN_EPS = 1e-5
SCRATCH = "Internal"


def settle(eng, passed):
    eng.sem_inc(passed, 1)


class Store:

    def __init__(self, nc, ctx, tag):
        self.nc, self.ctx, self.tag = nc, ctx, tag

    def sb(self, name, shape, dt=F32):
        return self.ctx.enter_context(self.nc.sbuf_tensor(f"{self.tag}_{name}", shape, dt))

    def ps(self, name, shape, dt=F32):
        return self.ctx.enter_context(self.nc.psum_tensor(f"{self.tag}_{name}", shape, dt))

    def sem(self, name):
        return self.ctx.enter_context(self.nc.semaphore(f"{self.tag}_{name}"))


def project(nc, d, keep):
    with ExitStack() as ctx:
        s = Store(nc, ctx, "proj")
        ident = keep["ident"]
        wz = s.sb("wz", [P, CT, P])
        wdq = s.sb("wdq", [KVL, C])
        wuqT = s.sb("wuqT", [KVL, C])
        wuq = s.sb("wuq", [P, CT, KVL])
        wuk = s.sb("wuk", [P, CT, KVL])
        wuv = s.sb("wuv", [P, CT, KVL])
        woT = s.sb("woT", [P, CT, C])
        amat = s.sb("amat", [KVL, KVL])
        kvw = s.sb("kvw", [P, 2, C])
        x = s.sb("x", [P, 2, TC, C])
        xn = s.sb("xn", [P, 2, TC, C])
        stats = s.sb("stats", [P, 2, TC, 6])
        mv = s.sb("mv", [P, 2, TC, 2])
        veps = s.sb("veps", [P, 2, TC])
        rstd = s.sb("rstd", [P, 2, TC])
        mhalf = s.sb("mhalf", [P, TC])
        ones = s.sb("ones", [P, T], F32R)
        zeros = s.sb("zeros", [P, T])
        xnT = s.sb("xnT", [P, CT, CH])
        z = s.sb("z", [P, CH])
        hi = s.sb("hi", [P, 2, 4, CH], F32R)
        lo = s.sb("lo", [P, 2, 4, CH], F32R)
        v = s.sb("v", [P, 2, TC, NH, VW])

        psX = s.ps("psX", [P, CT, CH])
        psZ = s.ps("psZ", [P, CH])
        psQ = s.ps("psQ", [P, 2, CH])
        psV = s.ps("psV", [P, TC, C])

        w_in = s.sem("w_in")
        x_in = [s.sem(f"x_in{u}") for u in range(2)]
        a_made, a_kept, kv_made, kv_kept = (s.sem(n) for n in ("a_made", "a_kept", "kv_made", "kv_kept"))
        stats_done, mv_done, veps_done, rstd_done, xn_done = (
            s.sem(n) for n in ("stats_done", "mv_done", "veps_done", "rstd_done", "xn_done"))
        consts = s.sem("consts")
        xT_made, xT_kept, z_made, z_kept = (s.sem(n) for n in ("xT_made", "xT_kept", "z_made", "z_kept"))
        qk_made, hi_done, lo_done = (s.sem(n) for n in ("qk_made", "hi_done", "lo_done"))
        v_made, v_kept = s.sem("v_made"), s.sem("v_kept")
        stored = [s.sem(f"stored{u}") for u in range(2)]
        ones_stored, blank = s.sem("ones_stored"), s.sem("blank")

        PER = 16 * (6 + 6 + NG)

        with nc.Block() as block:
            @block.sync
            def _(sp):
                for dst, src in ((ident[:], d["ident"]), (keep["identb"][:], d["identb"]), (keep["mask_ts"][:], d["mask_ts"]),
                                 (keep["mask_st"][:], d["mask_st"]),
                                 (wz[:], d["wz"].rearrange("(k p) m -> p k m", p=P)),
                                 (wdq[:], d["wdq"]), (wuqT[:], d["wuqT"]),
                                 (wuq[:], d["wuq"].rearrange("(k p) m -> p k m", p=P)),
                                 (wuk[:], d["wuk"].rearrange("(k p) m -> p k m", p=P)),
                                 (wuv[:], d["wuv"].rearrange("(k p) m -> p k m", p=P)),
                                 (woT[:], d["woT"].rearrange("(k p) m -> p k m", p=P))):
                    sp.dma_start(dst, src).then_inc(w_in, 16)
                with sp.Fori(0, B) as b:
                    for u in range(2):
                        sp.wait_ge(xn_done, b * 2 + u + 1)
                        sp.dma_start(x[:, u], d["x"][bass.ds(b * T + u * CH, CH), :].rearrange("(k p) c -> p k c", p=P)
                                     ).then_inc(x_in[u], 16)
                rows = (NT + 1) * XT // P
                for r in range(0, rows, 8):
                    n = min(8, rows - r)
                    sp.dma_start(d["xs"][r * P:(r + n) * P, :].rearrange("(p k) c -> p k c", p=P),
                                 zeros[:, 0:C].unsqueeze(1).to_broadcast([P, n, C])).then_inc(blank, 16)
                sp.wait_ge(blank, 16 * -(-rows // 8))

            @block.gpsimd
            def _(pool):
                pool.memset(mhalf[:], -0.5).then_inc(consts, 1)
                pool.memset(zeros[:], 0.0).then_inc(consts, 1)
                pool.memset(ones[:].bitcast(F32), 1.0).then_inc(consts, 1)
                pool.memset(v[:, :, :, :, HS:VW], 1.0).then_inc(consts, 1)
                pool.wait_ge(consts, 4)
                with pool.Fori(0, B) as b:
                    for u in range(2):
                        pool.wait_ge(mv_done, b * 2 * TC + (u + 1) * TC)
                        settle(pool, keep["passed"])
                        pool.tensor_scalar(veps[:, u], mv[:, u, :, 1], LN_EPS, None, ALU.add).then_inc(veps_done, 1)
                        pool.wait_ge(veps_done, b * 2 + u + 1)
                        pool.tensor_tensor(rstd[:, u], veps[:, u], mhalf[:], ALU.pow).then_inc(rstd_done, 1)

            @block.vector
            def _(dve):
                dve.nop().then_inc(xn_done, 2)
                dve.nop().then_inc(lo_done, 2)
                dve.nop().then_inc(v_kept, 2)
                dve.wait_ge(a_made, 1)
                dve.tensor_copy(amat[:], psZ[0:KVL, 0:KVL]).then_inc(a_kept, 1)
                dve.wait_ge(kv_made, 1)
                dve.tensor_copy(kvw[KVL:P], psQ[KVL:P, :, 0:C]).then_inc(kv_kept, 1)
                dve.wait_ge(consts, 4)
                with dve.Fori(0, B) as b:
                    for u in range(2):
                        dve.wait_ge(x_in[u], b * 16 + 16)
                        for t in range(TC):
                            dve.bn_stats(stats[:, u, t], x[:, u, t]).then_inc(stats_done, 1)
                        dve.wait_ge(stats_done, b * 8 + (u * TC + TC))
                        settle(dve, keep["passed"])
                        for t in range(TC):
                            dve.bn_aggr(mv[:, u, t], stats[:, u, t]).then_inc(mv_done, 1)
                        dve.wait_ge(rstd_done, b * 2 + u + 1)
                        dve.wait_ge(xT_made, b * 2 + u + 1)
                        for t in range(TC):
                            ins = dve.tensor_scalar(xn[:, u, t], x[:, u, t], mv[:, u, t, 0:1], rstd[:, u, t:t + 1],
                                                    ALU.subtract, ALU.mult)
                        ins.then_inc(xn_done, 1)
                        dve.wait_ge(stored[u], b * PER + 1)
                        for m in range(4):
                            dve.wait_ge(hi_done, b * 8 + u * 4 + m + 1 + 2)
                            dve.tensor_tensor(lo[:, u, m], psQ[:, m % 2], hi[:, u, m], ALU.subtract).then_inc(lo_done, 1)
                        for t in range(0, TC, 2):
                            dve.wait_ge(v_made, b * 8 + u * 4 + t + 2)
                            dve.tensor_copy(v[:, u, t:t + 2, :, 0:HS],
                                            psV[:, t:t + 2].rearrange("p k (h w) -> p k h w", h=NH)
                                            ).then_inc(v_kept, 1)

            @block.scalar
            def _(act):
                act.nop().then_inc(hi_done, 2)
                act.nop().then_inc(xT_kept, 1)
                act.nop().then_inc(z_kept, 1)
                for u in range(2):
                    act.nop().then_inc(stored[u], 1)
                act.wait_ge(consts, 4)
                for r in range(KR, KM):
                    act.dma_start(d["ks"][:, :, r, :].rearrange("g h t -> (g h) t"), ones[0:B * NH, :].bitcast(F32)
                                  ).then_inc(ones_stored, 16)
                    act.dma_start(d["qs"][:, :, r, :].rearrange("g h t -> (g h) t"), zeros[0:B * NH, :]
                                  ).then_inc(ones_stored, 16)
                with act.Fori(0, B) as b:
                    for u in range(2):
                        act.wait_ge(xT_made, b * 2 + u + 1 + 1)
                        act.activation(xnT[:], psX[:], ACT.Copy).then_inc(xT_kept, 1)
                        act.wait_ge(z_made, b * 2 + u + 1)
                        act.activation(z[:], psZ[:], ACT.Copy).then_inc(z_kept, 1)
                        act.wait_ge(stored[u], b * PER + 1)
                        for m in range(4):
                            act.wait_ge(qk_made, b * 8 + u * 4 + m + 1)
                            act.activation(hi[:, u, m], psQ[:, m % 2], ACT.Copy).then_inc(hi_done, 1)
                        act.wait_ge(hi_done, b * 8 + u * 4 + 4 + 2)
                        act.wait_ge(lo_done, b * 8 + u * 4 + 4 + 2)
                        cols = slice(u * CH, (u + 1) * CH)
                        for m in range(2):
                            q = d["qs"][bass.ds(b * NG + m * 2, 2)].rearrange("g h r t -> (g h) r t")
                            k = d["ks"][bass.ds(b * NG + m * 2, 2)].rearrange("g h r t -> (g h) r t")
                            for part, src in enumerate((hi, hi, lo)):
                                act.dma_start(q[:, part * HS:(part + 1) * HS, cols], src[:, u, m].bitcast(F32)).then_inc(stored[u], 16)
                            for part, src in enumerate((hi, lo, hi)):
                                act.dma_start(k[:, part * HS:(part + 1) * HS, cols], src[:, u, 2 + m].bitcast(F32)
                                             ).then_inc(stored[u], 16)
                        act.wait_ge(v_kept, b * 4 + u * 2 + 2 + 2)
                        for g in range(NG):
                            vs = d["vs"][bass.ds(b * NG + g, 1)].rearrange("o (k p) w -> (o p) k w", p=P)
                            act.dma_start(vs[:, u * TC:(u + 1) * TC, :],
                                         v[:, u, :, g * GH:(g + 1) * GH, :].rearrange("p k h w -> p k (h w)")
                                         ).then_inc(stored[u], 16)
                for u in range(2):
                    act.wait_ge(stored[u], PER * B + 1)
                act.wait_ge(ones_stored, 64)

            @block.tensor
            def _(pe):
                pe.wait_ge(w_in, 16 * 11)
                for k in range(CT):
                    ins = pe.matmul(psZ[0:KVL, 0:KVL], wuq[:, k], wuk[:, k], start=(k == 0), stop=(k == CT - 1))
                ins.then_inc(a_made, 1)
                for k in range(CT):
                    pe.matmul(psQ[KVL:P, 1, 0:C], wuv[:, k], woT[:, k], start=(k == 0), stop=(k == CT - 1))
                pe.wait_ge(a_kept, 1)
                pe.matmul(psQ[KVL:P, 0, 0:C], amat[:], wdq[:], start=True, stop=True).then_inc(kv_made, 1)
                pe.wait_ge(kv_kept, 1)
                pe.nop().then_inc(xT_made, 1)
                with pe.Fori(0, B) as b:
                    for u in range(2):
                        pe.wait_ge(xn_done, b * 2 + u + 1 + 2)
                        pe.wait_ge(xT_kept, b * 2 + u + 1)
                        for t in range(TC):
                            for k in range(CT):
                                ins = pe.transpose(psX[:, k, t * P:(t + 1) * P], xn[:, u, t, k * P:(k + 1) * P], ident[:])
                        ins.then_inc(xT_made, 1)
                        pe.wait_ge(xT_kept, b * 2 + u + 1 + 1)
                        pe.wait_ge(z_kept, b * 2 + u + 1)
                        for k in range(CT):
                            ins = pe.matmul(psZ[:], wz[:, k], xnT[:, k], start=(k == 0), stop=(k == CT - 1))
                        ins.then_inc(z_made, 1)
                        pe.wait_ge(z_kept, b * 2 + u + 1 + 1)
                        for m in range(4):
                            pe.wait_ge(lo_done, b * 8 + u * 4 + m + 1)
                            r, w = ((slice(0, KVL), wuqT[:, m * P:(m + 1) * P]) if m < 2 else
                                    (slice(KVL, P), kvw[KVL:P, 0, (m - 2) * P:(m - 1) * P]))
                            pe.matmul(psQ[:, m % 2], w, z[r], start=True, stop=True).then_inc(qk_made, 1)
                        for t in range(TC):
                            pe.wait_ge(v_kept, b * 4 + u * 2 + 2)
                            pe.matmul(psV[:, t], z[KVL:P, t * P:(t + 1) * P], kvw[KVL:P, 1], start=True, stop=True
                                      ).then_inc(v_made, 1)


BLOCKS = [(c, j) for c in range(NCH) for j in range((c + 1) * TC)]
STEPS = [(c, j, p) for c, j in BLOCKS for p in range(2)]
NB, NS = len(BLOCKS), len(STEPS)


def max_units():
    out = []
    for i in range(TB):
        keys = (i + 1) * P
        if 2 * keys <= CH:
            out += [(i, 0, (e, e + 2), 0, keys) for e in range(2)]
        else:
            out += [(i, k, (h,), k * CH, min(CH, keys - k * CH)) for k in range(-(-keys // CH)) for h in range(GH)]
    return out


UNITS = max_units()
NU = len(UNITS)
HALF = NU // 2
TURN = 12
AFTER = [[] for _ in STEPS]
for m in range(HALF):
    AFTER[m * (TURN - 1) // HALF].append((1, HALF + m))
    AFTER[TURN + 2 + m * (NS - TURN - 2) // HALF].append((2, m))
assert NU % 4 == 0 and NB % 3 == 0
NSL = NG


def attend(nc, d, keep):
    with ExitStack() as ctx:
        s = Store(nc, ctx, "att")
        ident, identb = keep["ident"], keep["identb"]
        y = keep["y"]
        qg = [s.sb(f"q{g}", [P, 2, T], F32R) for g in range(NSL)]
        kg = [s.sb(f"k{g}", [P, GH, T], F32R) for g in range(NSL)]
        vg = [s.sb(f"v{g}", [P, TB, GH * VW]) for g in range(NSL)]
        pt = s.sb("pt", [P, 3, GH, CH])
        pm = s.sb("pm", [P, 2, TB, 2, GH])
        nh = s.sb("nh", [P, TB, 2 * GH], F32R)
        mt = s.sb("mt", [2 * GH, T], F32R)
        ot = s.sb("ot", [P, CH])
        rec = s.sb("rec", [P, TC, GH])
        onesb = s.sb("onesb", [1, CH], BF16)

        ps_s = [s.ps(f"ps_s{i}", [P, 2, CH]) for i in range(2)]
        ps_m = [s.ps(f"ps_m{i}", [P, CH]) for i in range(2)]
        ps_o = s.ps("ps_o", [P, CH])
        ps_t = s.ps("ps_t", [P, TC, P])

        loaded = [s.sem(f"loaded{g}") for g in range(NSL)]
        m_in = [s.sem(f"m_in{g}") for g in range(NSL)]
        init, st_made, ex_done, pv_done, ot_done, tb_made, y_rec, y_done = (
            s.sem(n) for n in ("init", "st_made", "ex_done", "pv_done", "ot_done", "tb_made", "y_rec", "y_done"))
        mx_made, mx_read, pm_done, nh_hi, nh_done, mtp_made, mt_done = (
            s.sem(n) for n in ("mx_made", "mx_read", "pm_done", "nh_hi", "nh_done", "mtp_made", "mt_done"))

        def at(b, g, per, more):
            return b * (NG * per) + (g * per + more)

        def ahead(b, g, n):
            if isinstance(b, int) and b * NG + g + n >= B * NG:
                return None
            return ((b if isinstance(b, int) else b), g + n)

        with nc.Block() as block:
            @block.sync
            def _(sp):
                def loads(b, g):
                    slot = g % NSL
                    for h in range(GH):
                        r = slice(64 * (h % 2), 64 * (h % 2) + KM)
                        sp.dma_start(qg[slot][r, h // 2, :].bitcast(F32),
                                     d["qs"][bass.ds(b * NG + g, 1), h].rearrange("o r t -> (o r) t")
                                     ).then_inc(loaded[slot], 16)
                        sp.dma_start(kg[slot][r, h, :].bitcast(F32),
                                     d["ks"][bass.ds(b * NG + g, 1), h].rearrange("o r t -> (o r) t")
                                     ).then_inc(loaded[slot], 16)
                    sp.dma_start(vg[slot][:], d["vs"][bass.ds(b * NG + g, 1)].rearrange("o (k p) w -> (o p) k w", p=P)
                                 ).then_inc(loaded[slot], 16)

                def max_rows(b, g):
                    sp.wait_ge(mt_done, at(b, g, 1, 1))
                    slot = g % NSL
                    for h in range(GH):
                        for part in range(2):
                            r = 64 * (h % 2) + KR + part
                            sp.dma_start(qg[slot][r:r + 1, h // 2, :].bitcast(F32),
                                         mt[part * GH + h:part * GH + h + 1, :].bitcast(F32)).then_inc(m_in[slot], 16)

                sp.wait_ge(init, 1 + 2 * NSL)
                for g in range(3):
                    loads(0, g)
                max_rows(0, 0)

                def body(b):
                    for g in range(NG):
                        if ahead(b, g, 3):
                            sp.wait_ge(pv_done, at(b, g, NB, 3))
                            loads(b, g + 3)
                        if ahead(b, g, 1):
                            max_rows(b, g + 1)

                with sp.Fori(0, B - 1) as b:
                    body(b)
                body(B - 1)

            @block.gpsimd
            def _(pool):
                pool.memset(onesb[:], 1.0).then_inc(init, 1)
                for g in range(NSL):
                    pool.memset(qg[g][:].bitcast(F32), 0.0).then_inc(init, 1)
                    pool.memset(kg[g][:].bitcast(F32), 0.0).then_inc(init, 1)

            @block.tensor
            def _(pe):
                pe.nop().then_inc(pv_done, 3)
                pe.nop().then_inc(tb_made, 1)
                pe.wait_ge(init, 1)
                pe.matmul(ps_o[:], onesb[:, 0:P], onesb[:], start=True, stop=True)

                def unit(b, g, m):
                    i, piece, heads, k0, keys = UNITS[m]
                    slot, out = g % NSL, ps_m[m % 2]
                    if m == 0:
                        pe.wait_ge(loaded[slot], at(b, g // NSL * NSL, 36, 144))
                    pe.wait_ge(mx_read, at(b, g, NU, m + 1))
                    for n, h in enumerate(heads):
                        diag = k0 + keys == (i + 1) * P
                        ins = pe.matmul(out[:, n * keys:(n + 1) * keys], qg[slot][:, h // 2, i * P:(i + 1) * P],
                                        kg[slot][:, h, k0:k0 + keys], start=True, stop=not diag)
                        if diag:
                            ins = pe.matmul(out[:, (n + 1) * keys - P:(n + 1) * keys], identb[:], keep["mask_ts"][:],
                                            start=False, stop=True)
                    ins.then_inc(mx_made, 1)

                def max_turn(b, g):
                    pe.wait_ge(nh_done, at(b, g, 1, 1))
                    for i in range(TB):
                        ins = pe.transpose(ps_m[i // TC][0:2 * GH, (i % TC) * P:(i % TC + 1) * P],
                                           nh[:, i, :].bitcast(F32), ident[:])
                    ins.then_inc(mtp_made, 1)

                def scores(b, g, k):
                    c, j, p = STEPS[k]
                    slot, out = g % NSL, ps_s[k % 2]
                    if k == 0:
                        pe.wait_ge(m_in[slot], at(b, g // NSL * NSL, 32, 128))
                    pe.wait_ge(ex_done, at(b, g, NS, k + 1))
                    off = max(0, (j - c * TC) * P)
                    diag = j >= c * TC
                    for e in range(2):
                        ins = pe.matmul(out[:, e, off:CH], kg[slot][:, 2 * p + e, j * P:(j + 1) * P],
                                        qg[slot][:, p, c * CH + off:(c + 1) * CH], start=True, stop=not diag)
                    if diag:
                        for e in range(2):
                            ins = pe.matmul(out[:, e, off:off + P], identb[:], keep["mask_st"][:], start=False, stop=True)
                    ins.then_inc(st_made, 1)

                def values(b, g, blk):
                    c, j = BLOCKS[blk]
                    slot = g % NSL
                    pe.wait_ge(ex_done, at(b, g, NS, 2 * blk + 2 + 2))
                    if j == 0:
                        pe.wait_ge(ot_done, at(b, g, 2, 1 + c))
                    off = max(0, (j - c * TC) * P)
                    for h in range(GH):
                        ins = pe.matmul(ps_o[32 * h:32 * h + VW, off:CH], vg[slot][:, j, h * VW:(h + 1) * VW],
                                        pt[:, blk % 3, h, off:CH], start=(j == 0), stop=(j == (c + 1) * TC - 1))
                    ins.then_inc(pv_done, 1)

                def turn_out(b, g, c):
                    pe.wait_ge(ot_done, at(b, g, 2, c + 1))
                    pe.wait_ge(y_done, at(b, g, 2, c + 1))
                    for t in range(TC):
                        ins = pe.transpose(ps_t[:, t, :], ot[:, t * P:(t + 1) * P], ident[:])
                    ins.then_inc(tb_made, 1)

                for m in range(NU):
                    unit(0, 0, m)
                max_turn(0, 0)
                pe.wait_ge(mt_done, 1)
                for m in range(HALF):
                    unit(0, 1, m)

                def body(b):
                    for g in range(NG):
                        for k in range(NS):
                            scores(b, g, k)
                            if k == 4:
                                turn_out(b, g, 0)
                            if k == 14:
                                turn_out(b, g, 1)
                            if k == TURN and ahead(b, g, 1):
                                max_turn(b, g + 1)
                            for n, m in AFTER[k]:
                                if ahead(b, g, n):
                                    if (n, m) == (2, 0):
                                        pe.wait_ge(mt_done, at(b, g + 1, 1, 1))
                                    unit(b, g + n, m)
                            if k % 2 == 1 and k >= 3:
                                values(b, g, k // 2 - 1)
                        values(b, g, NB - 1)

                with pe.Fori(0, B - 1) as b:
                    body(b)
                body(B - 1)
                turn_out(B, 0, 0)

            @block.scalar
            def _(act):
                act.nop().then_inc(ex_done, 2)

                def fill_mt(b, g):
                    act.wait_ge(mtp_made, at(b, g, 1, 1))
                    for i in range(2):
                        ins = act.activation(mt[:, i * CH:(i + 1) * CH], ps_m[i][0:2 * GH, :], ACT.Copy)
                    ins.then_inc(mt_done, 1)

                def keep_out(b, g, c):
                    act.wait_ge(pv_done, at(b, g, NB, 3 + TC * c))
                    act.wait_ge(tb_made, at(b, g, 2, c + 1))
                    act.activation(ot[:], ps_o[:], ACT.Copy).then_inc(ot_done, 1)

                fill_mt(0, 0)

                def body(b):
                    for g in range(NG):
                        for k, (c, j, p) in enumerate(STEPS):
                            blk = k // 2
                            act.wait_ge(st_made, at(b, g, NS, k + 1))
                            act.wait_ge(pv_done, at(b, g, NB, blk + 1))
                            off = max(0, (j - c * TC) * P)
                            act.activation(pt[:, blk % 3, 2 * p:2 * p + 2, off:CH], ps_s[k % 2][:, :, off:CH],
                                           ACT.Exp, scale=HS ** -0.5).then_inc(ex_done, 1)
                            if k == 1:
                                keep_out(b, g, 0)
                            if k == 11:
                                keep_out(b, g, 1)
                            if k == TURN and ahead(b, g, 1):
                                act.wait_ge(m_in[g % NSL], at(b, g // NSL * NSL, 32, 128))
                                fill_mt(b, g + 1)

                with act.Fori(0, B - 1) as b:
                    body(b)
                body(B - 1)
                keep_out(B, 0, 0)

            @block.vector
            def _(dve):
                dve.nop().then_inc(mx_read, 2)
                dve.nop().then_inc(y_done, 1)

                def unit(b, g, m):
                    i, piece, heads, k0, keys = UNITS[m]
                    dve.wait_ge(mx_made, at(b, g, NU, m + 1))
                    src = ps_m[m % 2][:, 0:len(heads) * keys]
                    if len(heads) > 1:
                        src = src.rearrange("p (h k) -> p h k", k=keys)
                    h = heads[0]
                    dve.tensor_reduce(pm[:, g % 2, i, piece, h:h + 3:2] if len(heads) > 1 else pm[:, g % 2, i, piece, h:h + 1],
                                      src, AX.X, ALU.max).then_inc(mx_read, 1)

                def negate(b, g):
                    q = pm[:, g % 2]
                    dve.wait_ge(mx_read, at(b, g, NU, NU + 2))
                    dve.tensor_tensor(q[:, TC:TB, 0], q[:, TC:TB, 0], q[:, TC:TB, 1], ALU.max).then_inc(pm_done, 1)
                    dve.wait_ge(pm_done, at(b, g, 1, 1))
                    if not (isinstance(b, int) and b * NG + g == 0):
                        dve.wait_ge(mtp_made, at(b, g, 1, 0))
                    dve.tensor_scalar(nh[:, :, 0:GH], q[:, :, 0], -1.0, None, ALU.mult).then_inc(nh_hi, 1)
                    dve.wait_ge(nh_hi, at(b, g, 1, 1))
                    dve.scalar_tensor_tensor(nh[:, :, GH:2 * GH], q[:, :, 0], -1.0, nh[:, :, 0:GH],
                                             ALU.mult, ALU.subtract).then_inc(nh_done, 1)
                    dve.wait_ge(nh_done, at(b, g, 1, 1))

                def normalise(b, g, c):
                    dve.wait_ge(tb_made, at(b, g, 2, c + 2))
                    o = ps_t[:].rearrange("p t (h w) -> p t h w", h=GH)
                    dve.reciprocal(rec[:], o[:, :, :, HS]).then_inc(y_rec, 1)
                    dve.wait_ge(y_rec, at(b, g, 2, c + 1))
                    place = b * NG + (g + c)
                    half = 1 - c
                    dst = y[:, bass.ds(place, 1), half * TC:(half + 1) * TC, :].rearrange("p o t (h w) -> p (o t) h w", h=GH)
                    dve.tensor_tensor(dst, o[:, :, :, 0:HS], rec[:].unsqueeze(3).to_broadcast([P, TC, GH, HS]), ALU.mult
                                      ).then_inc(y_done, 1)

                for m in range(NU):
                    unit(0, 0, m)
                negate(0, 0)
                for m in range(HALF):
                    unit(0, 1, m)

                def body(b):
                    for g in range(NG):
                        for m in range(NU):
                            if m == 10:
                                normalise(b, g, 0)
                            if m == 30:
                                normalise(b, g, 1)
                            if m < HALF and ahead(b, g, 1):
                                unit(b, g + 1, HALF + m)
                            elif HALF <= m < NU:
                                if m == HALF and ahead(b, g, 1):
                                    negate(b, g + 1)
                                if ahead(b, g, 2):
                                    unit(b, g + 2, m - HALF)

                with dve.Fori(0, B - 1) as b:
                    body(b)
                body(B - 1)
                normalise(B, 0, 0)


E, K, F = 8, 2, 1024
FT = F // P
XT = 256
NT = K * N // XT + E
MOE_EPS = 1e-6
TILES = N // P


def route(nc, d, keep):
    with ExitStack() as ctx:
        s = Store(nc, ctx, "route")
        ident = keep["ident"]
        y, xf = keep["y"], keep["xf"]
        wgt, slot, base = keep["wgt"], keep["slot"], keep["base"]
        gb = keep["gb"]
        xh = s.sb("xh", [P, TILES, C])
        yn = s.sb("yn", [P, TB, C])
        xb = s.sb("xb", [P, TB, C])
        stats = s.sb("stats", [P, 3, TB, 6])
        mv = s.sb("mv", [P, 3, TB, 2])
        veps = s.sb("veps", [P, 3, TB])
        rstd = s.sb("rstd", [P, 3, TB])
        mhalf = s.sb("mhalf", [P, TB])
        xfT = s.sb("xfT", [P, 2, CT, P])
        wg = s.sb("wg", [P, CT, E])
        before = s.sb("before", [P, P])
        ones = s.sb("ones", [P, TILES])
        ones_sq = s.sb("ones_sq", [P, P])
        ei = s.sb("ei", [P, E])
        ti = s.sb("ti", [E, NT + 1])
        gam = s.sb("gam", [E, 2, C])
        best = s.sb("best", [P, TILES, 8])
        order = s.sb("order", [P, TILES, 8], mybir.dt.uint32)
        which = s.sb("which", [P, K, TILES])
        pick = s.sb("pick", [P, K, TILES, E])
        taken = s.sb("taken", [P, TILES, E])
        upto = s.sb("upto", [P, E, TILES])
        place = s.sb("place", [P, TILES, E])
        tiles_i = s.sb("tiles_i", [P, E], mybir.dt.int32)
        tiles_f = s.sb("tiles_f", [P, E])
        base_f = s.sb("base_f", [P, E + 1])
        hit = s.sb("hit", [P, TILES, E])
        slot_f = s.sb("slot_f", [P, TILES])
        de = s.sb("de", [P, TILES])
        edge = s.sb("edge", [E, 2, E])
        edges = s.sb("edges", [E, 2])
        own = s.sb("own", [E, 2, NT + 1])

        ps_x = [s.ps(f"ps_x{i}", [P, CT, P]) for i in range(2)]
        ps_g = s.ps("ps_g", [P, TILES, E])
        ps_r = s.ps("ps_r", [P, TILES, E])
        ps_n = s.ps("ps_n", [P, TILES, E])
        ps_b = s.ps("ps_b", [P, 2, CT, NT + 1])

        x_in, c_in, consts = s.sem("x_in"), s.sem("c_in"), s.sem("consts")
        stat, aggr, rs, step = s.sem("stat"), s.sem("aggr"), s.sem("rs"), s.sem("step")
        ve_done, yn_done, x1_done, xf_done, xh_done = (
            s.sem(n) for n in ("ve_done", "yn_done", "x1_done", "xf_done", "xh_done"))
        turned, turn_kept, gated, ranked, weights_in, slots_in, gb_made = (
            s.sem(n) for n in ("turned", "turn_kept", "gated", "ranked", "weights_in", "slots_in", "gb_made"))
        exp_done, scattered, picked, owned, xf_kept = (
            s.sem(n) for n in ("exp_done", "scattered", "picked", "owned", "xf_kept"))

        with nc.Block() as block:
            @block.sync
            def _(sp):
                for b in range(B):
                    sp.dma_start(xf[:, b * TB:(b + 1) * TB], d["x"][b * T:(b + 1) * T, :].rearrange("(k p) c -> p k c", p=P)
                                 ).then_inc(x_in, 16)
                for dst, src in ((wg[:], d["wg"].rearrange("(k p) e -> p k e", p=P)), (before[:], d["before"]),
                                 (ei[:], d["ei"]), (ti[:], d["ti"]), (gam[:, 0], d["gamma"]), (gam[:, 1], d["beta"])):
                    sp.dma_start(dst, src).then_inc(c_in, 16)

            @block.gpsimd
            def _(pool):
                pool.memset(mhalf[:], -0.5).then_inc(consts, 1)
                pool.memset(ones[:], 1.0).then_inc(consts, 1)
                pool.memset(ones_sq[:], 1.0).then_inc(consts, 1)
                pool.wait_ge(consts, 3)
                with pool.Fori(0, B) as b:
                    for n in range(3):
                        pool.wait_ge(aggr, b * (3 * TB) + (n + 1) * TB)
                        settle(pool, keep["passed"])
                        pool.tensor_scalar(veps[:, n], mv[:, n, :, 1], MOE_EPS if n == 2 else LN_EPS, None, ALU.add
                                           ).then_inc(ve_done, 1)
                        pool.wait_ge(ve_done, b * 3 + n + 1)
                        pool.tensor_tensor(rstd[:, n], veps[:, n], mhalf[:], ALU.pow).then_inc(rs, 1)
                pool.wait_ge(slots_in, 1)
                pool.wait_ge(xh_done, B)
                for k in range(K):
                    for t in range(TILES):
                        pool.indirect_dma_start(d["xs"], bass.IndirectOffsetOnAxis(ap=slot[:, k, t:t + 1], axis=0),
                                                xh[:, t, :], None).then_inc(scattered, 16)
                pool.wait_ge(scattered, 16 * K * TILES)

            @block.vector
            def _(dve):
                dve.wait_ge(consts, 3)
                with dve.Fori(0, B) as b:
                    def moments(n, src):
                        settle(dve, keep["passed"])
                        for t in range(TB):
                            dve.bn_stats(stats[:, n, t], src(t)).then_inc(stat, 1)
                        dve.wait_ge(stat, b * (3 * TB) + (n * TB + TB))
                        settle(dve, keep["passed"])
                        for t in range(TB):
                            dve.bn_aggr(mv[:, n, t], stats[:, n, t]).then_inc(aggr, 1)
                        dve.wait_ge(rs, b * 3 + n + 1)

                    def tile(buf, t):
                        return buf[:, bass.ds(b * TB + t, 1), :].rearrange("p o c -> p (o c)")

                    def head_tile(t):
                        return y[:, bass.ds(b * NG + 1, NG), t, :]

                    moments(0, head_tile)
                    for t in range(TB):
                        dve.tensor_scalar(yn[:, t].rearrange("p (g w) -> p g w", g=NG), head_tile(t), mv[:, 0, t, 0:1],
                                          rstd[:, 0, t:t + 1], ALU.subtract, ALU.mult).then_inc(yn_done, 1)
                    dve.wait_ge(x_in, 16 * B)
                    for t in range(TB):
                        dve.wait_ge(yn_done, b * TB + t + 1)
                        dve.tensor_tensor(head_tile(t), tile(xf, t).rearrange("p (g w) -> p g w", g=NG),
                                          yn[:, t].rearrange("p (g w) -> p g w", g=NG), ALU.add).then_inc(x1_done, 1)
                    dve.wait_ge(x1_done, b * TB + TB)
                    moments(1, head_tile)
                    dve.wait_ge(xf_kept, b + 1)
                    for t in range(TB):
                        dve.tensor_scalar(xb[:, t].rearrange("p (g w) -> p g w", g=NG), head_tile(t), mv[:, 1, t, 0:1], rstd[:, 1, t:t + 1],
                                          ALU.subtract, ALU.mult).then_inc(xf_done, 1)
                    dve.wait_ge(xf_done, b * TB + TB)
                    moments(2, lambda t: xb[:, t])
                    for t in range(TB):
                        ins = dve.tensor_scalar(tile(xh, t), xb[:, t], mv[:, 2, t, 0:1], rstd[:, 2, t:t + 1],
                                                ALU.subtract, ALU.mult)
                    ins.then_inc(xh_done, 1)

                n = 0

                def then(ins):
                    nonlocal n
                    n += 1
                    ins.then_inc(step, 1)
                    dve.wait_ge(step, n)

                dve.wait_ge(gated, TILES + 2)
                dve.wait_ge(c_in, 16 * 6)
                for t in range(TILES):
                    ins = dve.max(best[:, t], ps_g[:, t])
                then(ins)
                for t in range(TILES):
                    ins = dve.max_index(order[:, t], best[:, t], ps_g[:, t])
                then(ins)
                then(dve.tensor_copy(which[:], order[:, :, 0:K].rearrange("p t k -> p k t")))
                for k in range(K):
                    ins = dve.tensor_tensor(pick[:, k], ei[:].unsqueeze(1).to_broadcast([P, TILES, E]),
                                            which[:, k].unsqueeze(2).to_broadcast([P, TILES, E]), ALU.is_equal)
                then(ins)
                dve.tensor_tensor(taken[:], pick[:, 0], pick[:, 1], ALU.add).then_inc(picked, 1)
                then(dve.tensor_tensor(de[:], best[:, :, 1], best[:, :, 0], ALU.subtract))
                dve.nop().then_inc(weights_in, 1)
                dve.wait_ge(exp_done, 1)
                then(dve.tensor_scalar(de[:], wgt[:, 1], 1.0, None, ALU.add))
                then(dve.reciprocal(wgt[:, 0], de[:]))
                then(dve.tensor_tensor(wgt[:, 1], wgt[:, 1], wgt[:, 0], ALU.mult))
                then(dve.tensor_tensor(wgt[:, 2], wgt[:, 1], wgt[:, 0], ALU.add))
                dve.wait_ge(ranked, 1)
                for e in range(E):
                    ins = dve.tensor_tensor_scan(upto[:, e], ones[:], ps_n[:, :, e], 0.0, ALU.mult, ALU.add)
                then(ins)
                then(dve.tensor_scalar(tiles_f[:], upto[:, :, TILES - 1], float(XT - 1), float(XT), ALU.add, ALU.max))
                then(dve.tensor_copy(tiles_i[:], tiles_f[:]))
                then(dve.tensor_scalar(tiles_i[:], tiles_i[:], XT.bit_length() - 1, None, ALU.logical_shift_right))
                then(dve.tensor_copy(tiles_f[:], tiles_i[:]))
                then(dve.memset(base_f[:, 0:1], 0.0))
                then(dve.tensor_tensor_scan(base_f[:, 1:E + 1], ones[:, 0:E], tiles_f[:], 0.0, ALU.mult, ALU.add))
                then(dve.tensor_copy(base[:], base_f[:]))
                then(dve.tensor_copy(place[:], ps_r[:]))
                then(dve.tensor_tensor(place[:], place[:], upto[:].rearrange("p e t -> p t e"), ALU.add))
                then(dve.tensor_tensor(place[:], place[:], ps_n[:], ALU.subtract))
                then(dve.scalar_tensor_tensor(place[:], base_f[:, 0:E].unsqueeze(1).to_broadcast([P, TILES, E]), float(XT),
                                              place[:], ALU.mult, ALU.add))
                for k in range(K):
                    then(dve.tensor_tensor(hit[:], pick[:, k], place[:], ALU.mult))
                    then(dve.tensor_reduce(slot_f[:], hit[:], AX.X, ALU.add))
                    then(dve.tensor_copy(slot[:, k], slot_f[:]))
                dve.nop().then_inc(slots_in, 1)
                for k in range(2):
                    ins = dve.tensor_tensor(edge[:, k], ident[0:E, 0:E], base_f[0:E, k:k + E], ALU.mult)
                then(ins)
                then(dve.tensor_reduce(edges[:], edge[:], AX.X, ALU.add))
                dve.tensor_scalar(own[:, 0], ti[:], edges[:, 0:1], None, ALU.is_ge)
                then(dve.tensor_scalar(own[:, 1], ti[:], edges[:, 1:2], None, ALU.is_lt))
                dve.tensor_tensor(own[:, 0], own[:, 0], own[:, 1], ALU.mult).then_inc(owned, 1)
                dve.wait_ge(gb_made, 1)
                then(dve.tensor_copy(gb[:], ps_b[:]))

            @block.scalar
            def _(act):
                act.nop().then_inc(turn_kept, 2)
                act.nop().then_inc(xf_kept, 1)
                with act.Fori(0, B) as b:
                    for t in range(TB):
                        act.wait_ge(turned, b * TB + t + 1)
                        act.wait_ge(gated, b * TB + t + 1)
                        act.activation(xfT[:, t % 2], ps_x[t % 2][:], ACT.Copy).then_inc(turn_kept, 1)
                    act.wait_ge(xh_done, b + 1)
                    act.activation(xf[:, bass.ds(b * TB, TB), :], xb[:], ACT.Copy).then_inc(xf_kept, 1)
                act.wait_ge(weights_in, 1)
                act.activation(wgt[:, 1], de[:], ACT.Exp).then_inc(exp_done, 1)

            @block.tensor
            def _(pe):
                pe.wait_ge(c_in, 16 * 6)
                pe.nop().then_inc(gated, 2)
                with pe.Fori(0, B) as b:
                    for t in range(TB + 1):
                        if t < TB:
                            pe.wait_ge(xf_done, b * TB + t + 1)
                            pe.wait_ge(turn_kept, b * TB + t + 1)
                            for k in range(CT):
                                ins = pe.transpose(ps_x[t % 2][:, k], xb[:, t, k * P:(k + 1) * P], ident[:])
                            ins.then_inc(turned, 1)
                        if t > 0:
                            pe.wait_ge(turn_kept, b * TB + (t - 1) + 1 + 2)
                            for k in range(CT):
                                ins = pe.matmul(ps_g[:, bass.ds(b * TB + (t - 1), 1), :].rearrange("p o e -> p (o e)"),
                                                xfT[:, (t - 1) % 2, k], wg[:, k], start=(k == 0), stop=(k == CT - 1))
                            ins.then_inc(gated, 1)
                pe.wait_ge(picked, 1)
                pe.matmul(ps_r[:].rearrange("p t e -> p (t e)"), before[:], taken[:].rearrange("p t e -> p (t e)"),
                          start=True, stop=True)
                pe.matmul(ps_n[:].rearrange("p t e -> p (t e)"), ones_sq[:], taken[:].rearrange("p t e -> p (t e)"),
                          start=True, stop=True).then_inc(ranked, 1)
                pe.wait_ge(owned, 1)
                for n in range(2):
                    for k in range(CT):
                        ins = pe.matmul(ps_b[:, n, k], gam[:, n, k * P:(k + 1) * P], own[:, 0], start=True, stop=True)
                ins.then_inc(gb_made, 1)


def experts(nc, d, keep):
    with ExitStack() as ctx:
        s = Store(nc, ctx, "moe")
        ident, base, gb = keep["ident"], keep["base"], keep["gb"]
        raw1 = s.sb("raw1", [P, CT, F])
        raw2 = s.sb("raw2", [P, FT, C])
        w1 = [[s.sb(f"w1{r}{p}", [P, CT, F], F32R) for p in "hl"] for r in range(2)]
        w2 = [[s.sb(f"w2{r}{p}", [P, FT, C], F32R) for p in "hl"] for r in range(2)]
        b1 = [s.sb(f"b1{r}", [P, FT]) for r in range(2)]
        b2 = [s.sb(f"b2{r}", [P, C]) for r in range(2)]
        rows = s.sb("rows", [P, 2, C])
        xg = s.sb("xg", [P, CT, XT])
        xT = [s.sb(f"xT{p}", [P, CT, XT], F32R) for p in "hl"]
        hf = s.sb("hf", [P, 4, XT])
        hT = [s.sb(f"hT{p}", [P, FT, XT], F32R) for p in "hl"]
        o = s.sb("o", [P, 2, C])

        ps_x = s.ps("ps_x", [P, CT, XT])
        ps_h = [s.ps(f"ps_h{i}", [P, XT]) for i in range(4)]
        ps_o = [s.ps(f"ps_o{i}", [P, C]) for i in range(2)]
        NHB = len(ps_h)

        raw_in, raw_used, w_made, w_used = s.sem("raw_in"), s.sem("raw_used"), s.sem("w_made"), s.sem("w_used")
        b_in = [s.sem(f"b_in{r}") for r in range(2)]
        rows_in, turned, xg_done, xh_done, xl_done, h_made, hf_done, hh_done, hl_done, up_done, out_made, o_done, stored = (
            s.sem(n) for n in ("rows_in", "turned", "xg_done", "xh_done", "xl_done", "h_made", "hf_done", "hh_done", "hl_done",
                               "up_done", "out_made", "o_done", "stored"))
        bv, b_used = s.sem("bv"), s.sem("b_used")
        pieces = ((0, 0), (0, 1), (1, 0))

        def each(eng, expert, tile, late=None):
            with eng.Fori(0, E // 2) as q:
                for r in range(2):
                    expert(q, r)
                    first = eng.value_load(base[0:1, bass.ds(q * 2 + r, 1)], min_val=0, max_val=NT - 1)
                    last = eng.value_load(base[0:1, bass.ds(q * 2 + (r + 1), 1)], min_val=1, max_val=NT)
                    with eng.Fori(first, last) as i:
                        tile(r, i)
                    if late:
                        late(last)

        with nc.Block() as block:
            @block.sync
            def _(sp):
                def fetch(i):
                    sp.dma_start(rows[:], d["xs"][bass.ds(i * XT, XT), :].rearrange("(k p) c -> p k c", p=P)
                                 ).then_inc(rows_in, 16)

                fetch(0)
                sp.nop().then_inc(stored, 1)

                def tile(r, i):
                    sp.wait_ge(turned, i + 1)
                    fetch(i + 1)
                    sp.wait_ge(o_done, i * 2 + 4)
                    sp.dma_start(d["xs"][bass.ds(i * XT, XT), :].rearrange("(k p) c -> p k c", p=P), o[:]
                                 ).then_inc(stored, 16)

                each(sp, lambda q, r: None, tile)
                total = sp.value_load(base[0:1, E:E + 1], min_val=1, max_val=NT)
                sp.wait_ge(stored, total * 16 + 1)
                settle(sp, keep["passed"])

            @block.gpsimd
            def _(pool):
                with pool.Fori(0, E // 2) as q:
                    for r in range(2):
                        e = q * 2 + r
                        pool.dma_start(raw1[:], d["w1"][bass.ds(q * 2 + r, 1)].rearrange("o (k p) f -> (o p) k f", p=P)
                                       ).then_inc(raw_in, 16)
                        pool.dma_start(raw2[:], d["w2"][bass.ds(q * 2 + r, 1)].rearrange("o (k p) c -> (o p) k c", p=P)
                                       ).then_inc(raw_in, 16)
                        pool.wait_ge(w_used, q * 2 + r + 1)
                        pool.wait_ge(b_used, q * 2 + r + 1)
                        pool.dma_start(b1[r][:], d["b1"][:, bass.ds(q * 2 + r, 1), :].rearrange("p o f -> p (o f)")
                                       ).then_inc(b_in[r], 16)
                        pool.dma_start(b2[r][:], d["b2"][bass.ds(q * 2 + r, 1), :].rearrange("o c -> (o c)").partition_broadcast(P)
                                       ).then_inc(b_in[r], 16)
                        pool.wait_ge(raw_in, q * 64 + (r + 1) * 32)
                        settle(pool, keep["passed"])
                        pool.tensor_copy(w1[r][0][:], raw1[:]).then_inc(bv, 1)
                        pool.tensor_copy(w2[r][0][:], raw2[:]).then_inc(bv, 1)
                        pool.wait_ge(bv, q * 4 + r * 2 + 2)
                        pool.tensor_tensor(w1[r][1][:], raw1[:], w1[r][0][:], ALU.subtract).then_inc(w_made, 1)
                        pool.tensor_tensor(w2[r][1][:], raw2[:], w2[r][0][:], ALU.subtract).then_inc(w_made, 1)
                        pool.wait_ge(w_made, q * 4 + r * 2 + 2)

            @block.tensor
            def _(pe):
                pe.nop().then_inc(w_used, 2)
                pe.nop().then_inc(up_done, 1)
                def turn(n):
                    pe.wait_ge(rows_in, n * 16)
                    pe.wait_ge(xg_done, n)
                    for t in range(XT // P):
                        for k in range(CT):
                            ins = pe.transpose(ps_x[:, k, t * P:(t + 1) * P], rows[:, t, k * P:(k + 1) * P], ident[:])
                    ins.then_inc(turned, 1)

                turn(1)

                def tile(r, i):
                    pe.wait_ge(xl_done, i + 1)
                    for f in range(FT):
                        pe.wait_ge(hf_done, i * FT + (f + 1))
                        n = 0
                        for k in range(CT):
                            for a, m in pieces:
                                ins = pe.matmul(ps_h[f % NHB][:], w1[r][a][:, k, f * P:(f + 1) * P], xT[m][:, k],
                                                start=(n == 0), stop=(n == 3 * CT - 1))
                                n += 1
                        ins.then_inc(h_made, 1)
                    turn(i + 2)
                    pe.wait_ge(o_done, i * 2 + 2)
                    for f in range(FT):
                        pe.wait_ge(hl_done, i * FT + (f + 1 + NHB))
                        for t in range(XT // P):
                            for a, m in pieces:
                                ins = pe.matmul(ps_o[t][:], hT[a][:, f, t * P:(t + 1) * P], w2[r][m][:, f],
                                                start=(f == 0 and (a, m) == pieces[0]),
                                                stop=(f == FT - 1 and (a, m) == pieces[-1]))
                    ins.then_inc(out_made, 1)

                def expert(q, r):
                    pe.wait_ge(w_made, q * 4 + r * 2 + 2)
                    settle(pe, keep["passed"])

                def leave(last):
                    pe.wait_ge(out_made, last)
                    pe.nop().then_inc(w_used, 1)

                each(pe, expert, tile, leave)

            @block.scalar
            def _(act):
                act.nop().then_inc(hf_done, NHB)
                act.nop().then_inc(xg_done, 1)

                def feed(i, n):
                    act.wait_ge(turned, n)
                    for k in range(CT):
                        ins = act.activation(xg[:, k], ps_x[:, k], ACT.Identity, scale=gb[:, 0, k, i], bias=gb[:, 1, k, i])
                    ins.then_inc(xg_done, 1)
                    act.wait_ge(xg_done, n + 1)
                    act.activation(xT[0][:], xg[:], ACT.Copy).then_inc(xh_done, 1)

                feed(slice(0, 1), 1)

                def tile(r, i):
                    for f in range(FT):
                        act.wait_ge(h_made, i * FT + (f + 1))
                        act.wait_ge(hl_done, i * FT + (f + 1))
                        act.activation(hf[:, f % NHB], ps_h[f % NHB][:], ACT.Relu, bias=b1[r][:, f:f + 1]).then_inc(hf_done, 1)
                    feed(bass.ds(i + 1, 1), i + 2)

                def expert(q, r):
                    act.wait_ge(b_in[r], q * 32 + 32)
                    settle(act, keep["passed"])

                each(act, expert, tile)

            @block.vector
            def _(dve):
                dve.nop().then_inc(hl_done, NHB)
                dve.nop().then_inc(o_done, 2)
                dve.nop().then_inc(b_used, 2)

                def feed(n):
                    dve.wait_ge(xh_done, n)
                    dve.tensor_tensor(xT[1][:], xg[:], xT[0][:], ALU.subtract).then_inc(xl_done, 1)

                feed(1)

                def tile(r, i):
                    for f in range(FT):
                        dve.wait_ge(hf_done, i * FT + (f + 1 + NHB))
                        dve.tensor_copy(hT[0][:, f], hf[:, f % NHB]).then_inc(hh_done, 1)
                        dve.wait_ge(hh_done, i * FT + (f + 1))
                        dve.tensor_tensor(hT[1][:, f], hf[:, f % NHB], hT[0][:, f], ALU.subtract).then_inc(hl_done, 1)
                    feed(i + 2)
                    dve.wait_ge(out_made, i + 1)
                    dve.wait_ge(stored, i * 16 + 1)
                    for t in range(XT // P):
                        dve.tensor_tensor(o[:, t], ps_o[t][:], b2[r][:], ALU.add).then_inc(o_done, 1)

                def leave(last):
                    dve.wait_ge(o_done, last * 2 + 2)
                    dve.nop().then_inc(b_used, 1)

                def expert(q, r):
                    dve.wait_ge(b_in[r], q * 32 + 32)
                    settle(dve, keep["passed"])

                each(dve, expert, tile, leave)


def combine(nc, d, keep):
    with ExitStack() as ctx:
        s = Store(nc, ctx, "comb")
        y, xf, wgt, slot = keep["y"], keep["xf"], keep["wgt"], keep["slot"]
        g = s.sb("g", [P, TILES, K, C])
        acc = s.sb("acc", [P, TILES, C])
        stats = s.sb("stats", [P, TILES, 6])
        mv = s.sb("mv", [P, TILES, 2])
        veps = s.sb("veps", [P, TILES])
        rstd = s.sb("rstd", [P, TILES])
        mhalf = s.sb("mhalf", [P, TB])
        zn = s.sb("zn", [P, TILES, C])
        gathered = [s.sem(f"gathered{i}") for i in range(4)]
        consts, w0, w1, w2, st, ag, ve, rs, zd, done, stored = (
            s.sem(n) for n in ("consts", "w0", "w1", "w2", "st", "ag", "ve", "rs", "zd", "done", "stored"))

        with nc.Block() as block:
            @block.gpsimd
            def _(pool):
                pool.memset(mhalf[:], -0.5).then_inc(consts, 1)
                pool.wait_ge(consts, 1)

                def roots(q):
                    tiles = slice(q * TB, (q + 1) * TB)
                    pool.wait_ge(ag, (q + 1) * TB)
                    pool.tensor_scalar(veps[:, tiles], mv[:, tiles, 1], LN_EPS, None, ALU.add).then_inc(ve, 1)
                    pool.wait_ge(ve, q + 1)
                    pool.tensor_tensor(rstd[:, tiles], veps[:, tiles], mhalf[:], ALU.pow).then_inc(rs, 1)

                for q in range(B):
                    for t in range(q * TB, (q + 1) * TB):
                        for k in range(K):
                            pool.indirect_dma_start(g[:, t, k], None, d["xs"],
                                                    bass.IndirectOffsetOnAxis(ap=slot[:, k, t:t + 1], axis=0)
                                                    ).then_inc(gathered[q], 16)
                    if q:
                        roots(q - 1)
                roots(B - 1)

            @block.vector
            def _(dve):
                for q in range(B):
                    tiles = range(q * TB, (q + 1) * TB)
                    for t in tiles:
                        dve.tensor_scalar(acc[:, t], xf[:, t], wgt[:, 2, t:t + 1], None, ALU.mult).then_inc(w0, 1)
                    dve.wait_ge(gathered[q], 16 * K * TB)
                    for t in tiles:
                        dve.wait_ge(w0, t + 1)
                        dve.scalar_tensor_tensor(acc[:, t], g[:, t, 0], wgt[:, 0, t:t + 1], acc[:, t], ALU.mult, ALU.add
                                                 ).then_inc(w1, 1)
                    for t in tiles:
                        dve.wait_ge(w1, t + 1)
                        dve.scalar_tensor_tensor(acc[:, t], g[:, t, 1], wgt[:, 1, t:t + 1], acc[:, t], ALU.mult, ALU.add
                                                 ).then_inc(w2, 1)
                    for t in tiles:
                        dve.wait_ge(w2, t + 1)
                        dve.bn_stats(stats[:, t], acc[:, t]).then_inc(st, 1)
                    for t in tiles:
                        dve.wait_ge(st, t + 1)
                        dve.bn_aggr(mv[:, t], stats[:, t]).then_inc(ag, 1)
                    dve.wait_ge(rs, q + 1)
                    for t in tiles:
                        dve.tensor_scalar(zn[:, t], acc[:, t], mv[:, t, 0:1], rstd[:, t:t + 1], ALU.subtract, ALU.mult
                                          ).then_inc(zd, 1)
                    for t in tiles:
                        dve.wait_ge(zd, t + 1)
                        z = zn[:, t].rearrange("p (g w) -> p g w", g=NG)
                        dve.tensor_tensor(z, z, y[:, q * NG + 1:(q + 1) * NG + 1, t % TB, :], ALU.add).then_inc(done, 1)

            @block.sync
            def _(sp):
                for q in range(B):
                    sp.wait_ge(done, (q + 1) * TB)
                    sp.dma_start(d["out"][q * T:(q + 1) * T, :].rearrange("(k p) c -> p k c", p=P),
                                 zn[:, q * TB:(q + 1) * TB]).then_inc(stored, 16)
                sp.wait_ge(stored, 16 * B)


_INS = ["x", "wz", "wdq", "wuqT", "wuq", "wuk", "wuv", "woT", "ident", "identb", "mask_ts", "mask_st",
        "wg", "before", "ei", "ti", "gamma", "beta", "w1", "w2", "b1", "b2"]


def build(nc, d):
    with ExitStack() as ctx:
        s = Store(nc, ctx, "keep")
        keep = {"ident": s.sb("ident", [P, P]), "identb": s.sb("identb", [P, P], BF16),
                "passed": s.sem("passed"),
                "mask_ts": s.sb("mask_ts", [P, P], BF16), "mask_st": s.sb("mask_st", [P, P], BF16)}
        project(nc, d, keep)
        keep["y"] = s.sb("y", [P, B * NG + 1, TB, GH * HS])
        attend(nc, d, keep)
        keep["xf"] = s.sb("xf", [P, TILES, C])
        keep["wgt"] = s.sb("wgt", [P, 3, TILES])
        keep["slot"] = s.sb("slot", [P, K, TILES], mybir.dt.uint32)
        keep["base"] = s.sb("base", [P, E + 1], mybir.dt.int32)
        keep["gb"] = s.sb("gb", [P, 2, CT, NT + 1])
        route(nc, d, keep)
        experts(nc, d, keep)
        combine(nc, d, keep)


def kernel(**inputs):
    import concourse.bacc as bacc
    import ml_dtypes
    from concourse.bass_utils import run_bass_kernel_spmd

    w = {k.replace("L0_attn_", "").replace("L0_ffn_", ""): np.asarray(a) for k, a in inputs.items()}
    future = np.triu(np.full((P, P), -1e30, np.float32), 1)
    arrays = {
        "x": w["x"].reshape(N, C),
        "wz": np.concatenate([w["W_dq"].T, w["W_dkv"].T], axis=1),
        "wdq": w["W_dq"], "wuqT": w["W_uq"].T, "wuq": w["W_uq"], "wuk": w["W_uk"], "wuv": w["W_uv"], "woT": w["W_o"].T,
        "ident": np.eye(P, dtype=np.float32), "identb": np.eye(P).astype(ml_dtypes.bfloat16),
        "mask_ts": future.astype(ml_dtypes.bfloat16), "mask_st": future.T.astype(ml_dtypes.bfloat16),
        "wg": w["Wg"], "before": np.triu(np.ones((P, P), np.float32), 1),
        "ei": np.tile(np.arange(E, dtype=np.float32), (P, 1)),
        "ti": np.tile(np.arange(NT + 1, dtype=np.float32), (E, 1)),
        "gamma": w["gamma"], "beta": w["beta"], "w1": w["W1"], "w2": w["W2"],
        "b1": w["b1"].reshape(E, FT, P).transpose(2, 0, 1), "b2": w["b2"],
    }
    nc = bacc.Bacc("TRN2", target_bir_lowering=False, num_devices=1)
    d = {}
    for name in _INS:
        arrays[name] = np.ascontiguousarray(arrays[name])
        d[name] = nc.dram_tensor(f"in_{name}", arrays[name].shape, mybir.dt.from_np(arrays[name].dtype),
                                 kind="ExternalInput").ap()
    d["qs"] = nc.dram_tensor("qs", (B * NG, GH, KM, T), F32, kind=SCRATCH).ap()
    d["ks"] = nc.dram_tensor("ks", (B * NG, GH, KM, T), F32, kind=SCRATCH).ap()
    d["vs"] = nc.dram_tensor("vs", (B * NG, T, GH * VW), F32, kind=SCRATCH).ap()
    d["xs"] = nc.dram_tensor("xs", ((NT + 1) * XT, C), F32, kind=SCRATCH).ap()
    d["out"] = nc.dram_tensor("out_0", (N, C), F32, kind="ExternalOutput").ap()
    build(nc, d)
    r = run_bass_kernel_spmd(nc, [{f"in_{name}": arrays[name] for name in _INS}], core_ids=[0])
    return r.results[0]["out_0"].reshape(B, T, C)
```

```python
from contextlib import ExitStack

import numpy as np

import concourse.bass as bass
from concourse import mybir

F32 = mybir.dt.float32
F32R = mybir.dt.float32r
BF16 = mybir.dt.bfloat16
ALU = mybir.AluOpType
ACT = mybir.ActivationFunctionType
AX = mybir.AxisListType

P = 128
B, T, C = 4, 1024, 256
N = B * T
NH, HS, KVL = 16, 16, 64
CT = C // P
CH = 512
NCH = T // CH
TC = CH // P
TB = T // P
GH = 4
NG = NH // GH
KR = 3 * HS
KM = KR + 2
VW = HS + 1
LN_EPS = 1e-5
SCRATCH = "Internal"


def settle(eng, passed):
    eng.sem_inc(passed, 1)


class Store:

    def __init__(self, nc, ctx, tag):
        self.nc, self.ctx, self.tag = nc, ctx, tag

    def sb(self, name, shape, dt=F32):
        return self.ctx.enter_context(self.nc.sbuf_tensor(f"{self.tag}_{name}", shape, dt))

    def ps(self, name, shape, dt=F32):
        return self.ctx.enter_context(self.nc.psum_tensor(f"{self.tag}_{name}", shape, dt))

    def sem(self, name):
        return self.ctx.enter_context(self.nc.semaphore(f"{self.tag}_{name}"))


def project(nc, d, keep):
    with ExitStack() as ctx:
        s = Store(nc, ctx, "proj")
        ident = keep["ident"]
        wz = s.sb("wz", [P, CT, P])
        wdq = s.sb("wdq", [KVL, C])
        wuqT = s.sb("wuqT", [P, C])
        wuq = s.sb("wuq", [P, CT, KVL])
        wuk = s.sb("wuk", [P, CT, KVL])
        wuv = s.sb("wuv", [P, CT, KVL])
        woT = s.sb("woT", [P, CT, C])
        amat = s.sb("amat", [KVL, KVL])
        kvw = s.sb("kvw", [P, 2, C])
        x = s.sb("x", [P, 2, TC, C])
        xn = s.sb("xn", [P, 2, TC, C])
        stats = s.sb("stats", [P, 2, TC, 6])
        mv = s.sb("mv", [P, 2, TC, 2])
        veps = s.sb("veps", [P, 2, TC])
        rstd = s.sb("rstd", [P, 2, TC])
        mhalf = s.sb("mhalf", [P, TC])
        xnT = s.sb("xnT", [P, 2, CT, CH])
        z = s.sb("z", [P, 2, CH])
        hi = s.sb("hi", [P, 2, 4, CH], F32R)
        lo = s.sb("lo", [P, 2, 4, CH], F32R)
        v = s.sb("v", [P, 2, TC, NH, VW])

        rows01 = s.sb("rows01", [2, 2, 2 * T], F32R)

        psX = s.ps("psX", [P, CT, CH])
        psZ = s.ps("psZ", [P, CH])
        psQ = s.ps("psQ", [P, 4, CH])
        psV = s.ps("psV", [P, 2, C])

        w_in = s.sem("w_in")
        x_in = [s.sem(f"x_in{u}") for u in range(2)]
        a_made, a_kept, kv_made, kv_kept = (s.sem(n) for n in ("a_made", "a_kept", "kv_made", "kv_kept"))
        stats_done, mv_done, veps_done, rstd_done, xn_done = (
            s.sem(n) for n in ("stats_done", "mv_done", "veps_done", "rstd_done", "xn_done"))
        consts = s.sem("consts")
        xT_made, xT_kept, z_made, z_kept = (s.sem(n) for n in ("xT_made", "xT_kept", "z_made", "z_kept"))
        qk_made, hi_done, lo_done = (s.sem(n) for n in ("qk_made", "hi_done", "lo_done"))
        v_made, v_kept = s.sem("v_made"), s.sem("v_kept")
        rows_made, rows_stored = s.sem("rows_made"), s.sem("rows_stored")
        stored = [s.sem(f"stored{u}") for u in range(2)]

        PER = 16 * (4 + NG)
        NC = B * NCH

        def exists(c):
            return not isinstance(c, int) or c < NC

        with nc.Block() as block:
            @block.sync
            def _(sp):
                for dst, src in ((ident[:], d["ident"]),
                                 (wuq[:], d["wuq"].rearrange("(k p) m -> p k m", p=P)),
                                 (wuk[:], d["wuk"].rearrange("(k p) m -> p k m", p=P)),
                                 (wuv[:], d["wuv"].rearrange("(k p) m -> p k m", p=P)),
                                 (woT[:], d["woT"].rearrange("(k p) m -> p k m", p=P)),
                                 (wdq[:], d["wdq"]),
                                 (wz[:], d["wz"].rearrange("(k p) m -> p k m", p=P)),
                                 (wuqT[0:KVL], d["wuqT"]), (keep["identb"][:], d["identb"]),
                                 (keep["mask_ts"][:], d["mask_ts"]), (keep["mask_st"][:], d["mask_st"])):
                    sp.dma_start(dst, src).then_inc(w_in, 16)

                with sp.Fori(0, B) as b:
                    for u in range(2):
                        c = b * 2 + u
                        cols = slice(u * CH, (u + 1) * CH)
                        for m, name in ((0, "qs"), (2, "ks")):
                            dst = d[name][bass.ds(b, 1)].rearrange("o k (m p) t -> (o k) p m t", p=P)
                            sp.wait_ge(hi_done, c * 4 + m + 2)
                            sp.dma_start(dst[0, :, :, cols], hi[:, u, m:m + 2].bitcast(F32)).then_inc(stored[u], 16)
                            sp.wait_ge(lo_done, c * 4 + m + 2 + 4)
                            sp.dma_start(dst[1, :, :, cols], lo[:, u, m:m + 2].bitcast(F32)).then_inc(stored[u], 16)
                        sp.wait_ge(v_kept, c * 4 + 4 + 2)
                        for g in range(NG):
                            vs = d["vs"][bass.ds(b * NG + g, 1)].rearrange("o p k w -> (o p) k w")
                            sp.dma_start(vs[:, u * TC:(u + 1) * TC, :],
                                         v[:, u, :, g * GH:(g + 1) * GH, :].rearrange("p k h w -> p k (h w)")
                                         ).then_inc(stored[u], 16)
                sp.wait_ge(rows_made, 2)
                for k in range(2):
                    sp.dma_start(d["rows01"][k].rearrange("p h t -> p (h t)"), rows01[:, k].bitcast(F32)
                                 ).then_inc(rows_stored, 16)
                for u in range(2):
                    sp.wait_ge(stored[u], PER * B + 1)
                sp.wait_ge(rows_stored, 32)

            @block.gpsimd
            def _(pool):
                def load(c, u):
                    pool.dma_start(x[:, u], d["x"][bass.ds(c * CH, CH), :].rearrange("(k p) c -> p k c", p=P)
                                   ).then_inc(x_in[u], 16)

                def deviation(c, u):
                    pool.wait_ge(mv_done, c * TC + TC)
                    settle(pool, keep["passed"])
                    pool.tensor_scalar(veps[:, u], mv[:, u, :, 1], LN_EPS, None, ALU.add).then_inc(veps_done, 1)
                    pool.wait_ge(veps_done, c + 1)
                    pool.tensor_tensor(rstd[:, u], veps[:, u], mhalf[:], ALU.pow).then_inc(rstd_done, 1)

                load(0, 0)
                load(1, 1)
                for n, (dst, value) in enumerate(((mhalf[:], -0.5), (kvw[0:KVL], 0.0), (wuqT[KVL:P], 0.0),
                                                  (v[:, :, :, :, HS:VW], 1.0))):
                    pool.memset(dst, value).then_inc(consts, 1)
                    pool.wait_ge(consts, n + 1)
                deviation(0, 0)
                pool.memset(rows01[:, 0].bitcast(F32), 0.0).then_inc(rows_made, 1)
                pool.memset(rows01[:, 1].bitcast(F32), 1.0).then_inc(rows_made, 1)
                with pool.Fori(0, B - 1) as b:
                    for u in range(2):
                        pool.wait_ge(xn_done, b * 2 + u + 1)
                        load(b * 2 + u + 2, u)
                        deviation(b * 2 + u + 1, 1 - u)
                deviation(NC - 1, 1)

            @block.vector
            def _(dve):
                def moments(c, u, n):
                    dve.wait_ge(x_in[u], n * 16)
                    settle(dve, keep["passed"])
                    for t in range(TC):
                        dve.bn_stats(stats[:, u, t], x[:, u, t]).then_inc(stats_done, 1)
                    dve.wait_ge(stats_done, c * TC + TC)
                    settle(dve, keep["passed"])
                    for t in range(TC):
                        dve.bn_aggr(mv[:, u, t], stats[:, u, t]).then_inc(mv_done, 1)

                def normalise(c, u):
                    dve.wait_ge(rstd_done, c + 1)
                    if not (isinstance(c, int) and c < 2):
                        dve.wait_ge(xT_made, c - 1)
                    for t in range(TC):
                        ins = dve.tensor_scalar(xn[:, u, t], x[:, u, t], mv[:, u, t, 0:1], rstd[:, u, t:t + 1],
                                                ALU.subtract, ALU.mult)
                    ins.then_inc(xn_done, 1)

                dve.nop().then_inc(lo_done, 4)
                moments(0, 0, 1)
                moments(1, 1, 1)
                normalise(0, 0)
                dve.wait_ge(a_made, 1)
                dve.tensor_copy(amat[:], psZ[0:KVL, 0:KVL]).then_inc(a_kept, 1)
                normalise(1, 1)
                dve.wait_ge(kv_made, 1)
                dve.tensor_copy(kvw[KVL:P], psQ[KVL:P, 0:2, 0:C]).then_inc(kv_kept, 1)

                def body(b):
                    for u in range(2):
                        c = b * 2 + u
                        if exists(c + 2):
                            moments(c + 2, u, b + 2)
                        dve.wait_ge(stored[u], b * PER + 1)
                        for m in range(4):
                            dve.wait_ge(hi_done, c * 4 + m + 1)
                            dve.tensor_tensor(lo[:, u, m], psQ[:, m], hi[:, u, m], ALU.subtract).then_inc(lo_done, 1)
                        if exists(c + 2):
                            normalise(c + 2, u)

                with dve.Fori(0, B - 1) as b:
                    body(b)
                body(B - 1)

            @block.scalar
            def _(act):
                act.nop().then_inc(z_kept, 1)
                act.nop().then_inc(v_kept, 2)
                for u in range(2):
                    act.nop().then_inc(stored[u], 1)

                def keep_xT(c, u):
                    act.wait_ge(xT_made, c + 1)
                    act.activation(xnT[:, u], psX[:], ACT.Copy).then_inc(xT_kept, 1)

                act.wait_ge(consts, 4)
                keep_xT(0, 0)

                def body(b):
                    for u in range(2):
                        c = b * 2 + u
                        act.wait_ge(z_made, c + 1)
                        act.activation(z[:, u], psZ[:], ACT.Copy).then_inc(z_kept, 1)
                        if exists(c + 1):
                            keep_xT(c + 1, 1 - u)
                        act.wait_ge(stored[u], b * PER + 1)
                        for m in range(4):
                            act.wait_ge(qk_made, c * 4 + m + 1)
                            act.activation(hi[:, u, m], psQ[:, m], ACT.Copy).then_inc(hi_done, 1)
                            if m % 2 == 1:
                                act.wait_ge(v_made, c * 2 + m // 2 + 1)
                                for t in range(m - 1, m + 1):
                                    act.activation(v[:, u, t, :, 0:HS], psV[:, t % 2].rearrange("p (h w) -> p h w", h=NH),
                                                   ACT.Copy).then_inc(v_kept, 1)

                with act.Fori(0, B - 1) as b:
                    body(b)
                body(B - 1)

            @block.tensor
            def _(pe):
                def turn(c, u):
                    pe.wait_ge(xn_done, c + 1)
                    if not (isinstance(c, int) and c == 0):
                        pe.wait_ge(xT_kept, c)
                    for t in range(TC):
                        for k in range(CT):
                            ins = pe.transpose(psX[:, k, t * P:(t + 1) * P], xn[:, u, t, k * P:(k + 1) * P], ident[:])
                    ins.then_inc(xT_made, 1)

                pe.wait_ge(w_in, 16 * 11)
                pe.wait_ge(consts, 4)
                for k in range(CT):
                    ins = pe.matmul(psZ[0:KVL, 0:KVL], wuq[:, k], wuk[:, k], start=(k == 0), stop=(k == CT - 1))
                ins.then_inc(a_made, 1)
                for k in range(CT):
                    pe.matmul(psQ[KVL:P, 1, 0:C], wuv[:, k], woT[:, k], start=(k == 0), stop=(k == CT - 1))
                pe.wait_ge(a_kept, 1)
                pe.matmul(psQ[KVL:P, 0, 0:C], amat[:], wdq[:], start=True, stop=True).then_inc(kv_made, 1)
                turn(0, 0)
                pe.wait_ge(kv_kept, 1)

                def body(b):
                    for u in range(2):
                        c = b * 2 + u
                        pe.wait_ge(xT_kept, c + 1)
                        pe.wait_ge(z_kept, c + 1)
                        for k in range(CT):
                            ins = pe.matmul(psZ[:], wz[:, k], xnT[:, u, k], start=(k == 0), stop=(k == CT - 1))
                        ins.then_inc(z_made, 1)
                        if exists(c + 1):
                            turn(c + 1, 1 - u)
                        pe.wait_ge(z_kept, c + 2)
                        for m in range(4):
                            pe.wait_ge(lo_done, c * 4 + m + 1)
                            w = wuqT[:, m * P:(m + 1) * P] if m < 2 else kvw[:, 0, (m - 2) * P:(m - 1) * P]
                            pe.matmul(psQ[:, m], w, z[:, u], start=True, stop=True).then_inc(qk_made, 1)
                            if m % 2 == 1:
                                pe.wait_ge(v_kept, c * 4 + (m - 1) + 2)
                                for t in range(m - 1, m + 1):
                                    ins = pe.matmul(psV[:, t % 2], z[:, u, t * P:(t + 1) * P], kvw[:, 1], start=True, stop=True)
                                ins.then_inc(v_made, 1)

                with pe.Fori(0, B - 1) as b:
                    body(b)
                body(B - 1)


BLOCKS = [(c, j) for c in range(NCH) for j in range((c + 1) * TC)]
STEPS = [(c, j, p) for c, j in BLOCKS for p in range(2)]
NB, NS = len(BLOCKS), len(STEPS)


def max_units():
    out = []
    for i in range(TB):
        keys = (i + 1) * P
        if 2 * keys <= CH:
            out += [(i, 0, (e, e + 2), 0, keys) for e in range(2)]
        else:
            out += [(i, k, (h,), k * CH, min(CH, keys - k * CH)) for k in range(-(-keys // CH)) for h in range(GH)]
    return out


UNITS = max_units()
NU = len(UNITS)
HALF = NU // 2
NBK = 3


def bank_jobs():
    work = [("unit", 1, m) for m in range(HALF, NU)] + [("unit", 2, m) for m in range(HALF)]
    cost = [len(UNITS[m][2]) * UNITS[m][4] + 64 for _, _, m in work]
    width = [CH - max(0, (j - c * TC) * P) + 96 for c, j, _ in STEPS]
    out, step, done = [[] for _ in STEPS], 0, 0
    for job, c in zip(work, cost):
        while step < NS - 1 and (done + c / 2) / sum(cost) > sum(width[:step + 1]) / sum(width):
            step += 1
        out[step].append(job)
        done += c
    out[4].insert(0, ("out", 0, 0))
    out[13].insert(0, ("out", 0, 1))
    out[15].insert(0, ("turn", 1, 0))
    out[17].insert(0, ("turn", 1, 1))
    return out


AFTER = bank_jobs()
JOBS = sum(len(x) for x in AFTER)
assert JOBS % NBK == 0 and NB % 3 == 0
NSL = NG


def attend(nc, d, keep):
    with ExitStack() as ctx:
        s = Store(nc, ctx, "att")
        ident, identb = keep["ident"], keep["identb"]
        y = keep["y"]
        qg = [s.sb(f"q{g}", [P, 2, T], F32R) for g in range(NSL)]
        kg = [s.sb(f"k{g}", [P, GH, T], F32R) for g in range(NSL)]
        vg = [s.sb(f"v{g}", [P, TB, GH * VW]) for g in range(NSL)]
        pt = s.sb("pt", [P, 3, GH, CH])
        pm = s.sb("pm", [P, 2, TB, 2, GH])
        nh = s.sb("nh", [P, TB, GH, 2], F32R)
        mt = s.sb("mt", [2 * GH, T], F32R)
        ot = s.sb("ot", [P, CH])
        rec = s.sb("rec", [P, TC, GH])
        onesb = s.sb("onesb", [1, CH], BF16)
        zeros = s.sb("zeros", [P, C])

        ps_s = [s.ps(f"ps_s{i}", [P, 2, CH]) for i in range(2)]
        ps_m = [s.ps(f"ps_m{i}", [P, CH]) for i in range(NBK)]
        ps_o = s.ps("ps_o", [P, CH])

        loaded = [s.sem(f"loaded{g}") for g in range(NSL)]
        LOADS = 16 * (4 * GH + 3) // NSL
        m_in = [s.sem(f"m_in{g}") for g in range(NSL)]
        init = [s.sem(f"init{g}") for g in range(NSL)]
        started, blank, blank_made = s.sem("started"), s.sem("blank"), s.sem("blank_made")
        st_made, ex_done, pv_done, ot_done, y_rec, y_done = (
            s.sem(n) for n in ("st_made", "ex_done", "pv_done", "ot_done", "y_rec", "y_done"))
        bank_made = [s.sem(f"bank_made{i}") for i in range(NBK)]
        bank_read = [s.sem(f"bank_read{i}") for i in range(NBK)]
        pm_done, nh_hi, nh_done, mtp_made, mt_done = (
            s.sem(n) for n in ("pm_done", "nh_hi", "nh_done", "mtp_made", "mt_done"))

        def at(b, g, per, more):
            return b * (NG * per) + (g * per + more)

        def ahead(b, g, n):
            return not isinstance(b, int) or b * NG + g + n < B * NG

        first = [("unit", 0, m) for m in range(NU)] + [("unit", 1, m) for m in range(HALF)]
        first[NU + 5:NU + 5] = [("turn", 0, 0), ("turn", 0, 1)]

        def numbered(b):
            out, n = [], len(first)
            for g in range(NG):
                steps = []
                for k in range(NS):
                    here = [j for j in AFTER[k] if ahead(b, g, j[1])]
                    steps.append([(j, n + i) for i, j in enumerate(here)])
                    n += len(here)
                out.append(steps)
            return out, n

        def turns(b, n):
            return b * (JOBS * NG // NBK) + n // NBK

        with nc.Block() as block:
            @block.sync
            def _(sp):
                def loads(b, g):
                    slot = g % NSL
                    qs, ks = (d[n][bass.ds(b + g // NG, 1)].rearrange("o k c t -> (o k) c t") for n in ("qs", "ks"))
                    for h in range(GH):
                        head = g % NG * GH + h
                        r, c = 64 * (h % 2), slice(head * HS, (head + 1) * HS)
                        for dst, src in ((qg[slot][r:r + HS, h // 2, :], qs[0, c]),
                                         (qg[slot][r + HS:r + KR, h // 2, :], qs[:, c]),
                                         (kg[slot][r:r + 2 * HS, h, :], ks[:, c]),
                                         (kg[slot][r + 2 * HS:r + KR, h, :], ks[0, c])):
                            sp.dma_start(dst.bitcast(F32), src).then_inc(loaded[slot], 16)
                    for e in range(2):
                        sp.dma_start(qg[slot][64 * e + KR:64 * e + KM].bitcast(F32), d["rows01"][0]
                                     ).then_inc(loaded[slot], 16)
                    sp.dma_start(vg[slot][:], d["vs"][bass.ds(b * NG + g, 1)].rearrange("o p k w -> (o p) k w")
                                 ).then_inc(loaded[slot], 16)

                def max_rows(b, g):
                    sp.wait_ge(mt_done, at(b, g, 1, 1))
                    slot = g % NSL
                    for h in range(GH):
                        r = 64 * (h % 2) + KR
                        sp.dma_start(qg[slot][r:r + 2, h // 2, :].bitcast(F32), mt[2 * h:2 * h + 2, :].bitcast(F32)
                                     ).then_inc(m_in[slot], 16)

                for g in range(NSL):
                    sp.wait_ge(init[g], 2)
                    for e in range(2):
                        sp.dma_start(kg[g][64 * e + KR:64 * e + KM, e::2, :].bitcast(F32), d["rows01"][1]
                                     ).then_inc(loaded[g], 16)
                    if g < 3:
                        loads(0, g)
                max_rows(0, 0)

                def body(b):
                    for g in range(NG):
                        if ahead(b, g, 3):
                            sp.wait_ge(pv_done, at(b, g, NB, 3))
                            loads(b, g + 3)
                        if ahead(b, g, 1):
                            max_rows(b, g + 1)

                with sp.Fori(0, B - 1) as b:
                    body(b)
                body(B - 1)

            @block.gpsimd
            def _(pool):
                pool.memset(onesb[:], 1.0).then_inc(started, 1)
                for g in range(NSL):
                    pool.memset(qg[g][:].bitcast(F32), 0.0).then_inc(init[g], 1)
                    if g > 0:
                        pool.memset(kg[g][:].bitcast(F32), 0.0).then_inc(init[g], 1)
                pool.memset(zeros[:], 0.0).then_inc(blank_made, 1)
                pool.wait_ge(blank_made, 1)
                pool.wait_ge(pv_done, 3 + 2)
                rows = (NT + 1) * XT // P
                for r in range(0, rows, 8):
                    n = min(8, rows - r)
                    pool.dma_start(d["xs"][r * P:(r + n) * P, :].rearrange("(p k) c -> p k c", p=P),
                                   zeros[:].unsqueeze(1).to_broadcast([P, n, C])).then_inc(blank, 16)
                pool.wait_ge(blank, 16 * -(-rows // 8))

            @block.tensor
            def _(pe):
                pe.nop().then_inc(pv_done, 3)
                pe.wait_ge(started, 1)
                pe.matmul(ps_o[:], onesb[:, 0:P], onesb[:], start=True, stop=True)

                def unit(b, g, m, out):
                    i, piece, heads, k0, keys = UNITS[m]
                    slot = g % NSL
                    if m == 0:
                        pe.wait_ge(loaded[slot], at(b, g // NSL * NSL, LOADS, 4 * LOADS + 32))
                    for n, h in enumerate(heads):
                        diag = k0 + keys == (i + 1) * P
                        ins = pe.matmul(out[:, n * keys:(n + 1) * keys], qg[slot][:, h // 2, i * P:(i + 1) * P],
                                        kg[slot][:, h, k0:k0 + keys], start=True, stop=not diag)
                        if diag:
                            ins = pe.matmul(out[:, (n + 1) * keys - P:(n + 1) * keys], identb[:], keep["mask_ts"][:],
                                            start=False, stop=True)
                    return ins

                def max_turn(b, g, half, out):
                    pe.wait_ge(nh_done, at(b, g, 1, 1))
                    for i in range(TC):
                        ins = pe.transpose(out[0:2 * GH, i * P:(i + 1) * P], nh[:, half * TC + i].rearrange("p h k -> p (h k)").bitcast(F32), ident[:])
                    return ins

                def turn_out(b, g, c, out):
                    pe.wait_ge(ot_done, at(b, g, 2, c + 1))
                    for t in range(TC):
                        ins = pe.transpose(out[:, t * P:(t + 1) * P], ot[:, t * P:(t + 1) * P], ident[:])
                    return ins

                def job(b, g, what, n):
                    kind, more, m = what
                    bank = n % NBK
                    if not (isinstance(b, int) and n < NBK):
                        pe.wait_ge(bank_read[bank], turns(b, n))
                    do = {"unit": unit, "turn": max_turn, "out": turn_out}[kind]
                    do(b, g + more, m, ps_m[bank]).then_inc(bank_made[bank], 1)

                def scores(b, g, k):
                    c, j, p = STEPS[k]
                    slot, out = g % NSL, ps_s[k % 2]
                    if k == 0:
                        pe.wait_ge(m_in[slot], at(b, g // NSL * NSL, 16, 64))
                    pe.wait_ge(ex_done, at(b, g, NS, k + 1))
                    off = max(0, (j - c * TC) * P)
                    diag = j >= c * TC
                    for e in range(2):
                        ins = pe.matmul(out[:, e, off:CH], kg[slot][:, 2 * p + e, j * P:(j + 1) * P],
                                        qg[slot][:, p, c * CH + off:(c + 1) * CH], start=True, stop=not diag)
                    if diag:
                        for e in range(2):
                            ins = pe.matmul(out[:, e, off:off + P], identb[:], keep["mask_st"][:], start=False, stop=True)
                    ins.then_inc(st_made, 1)

                def values(b, g, blk):
                    c, j = BLOCKS[blk]
                    slot = g % NSL
                    pe.wait_ge(ex_done, at(b, g, NS, 2 * blk + 2 + 2))
                    if j == 0:
                        pe.wait_ge(ot_done, at(b, g, 2, 1 + c))
                    off = max(0, (j - c * TC) * P)
                    for h in range(GH):
                        ins = pe.matmul(ps_o[32 * h:32 * h + VW, off:CH], vg[slot][:, j, h * VW:(h + 1) * VW],
                                        pt[:, blk % 3, h, off:CH], start=(j == 0), stop=(j == (c + 1) * TC - 1))
                    ins.then_inc(pv_done, 1)

                for n, what in enumerate(first):
                    job(0, 0, what, n)

                def body(b):
                    for g, steps in enumerate(numbered(b)[0]):
                        for k in range(NS):
                            scores(b, g, k)
                            jobs = list(steps[k])
                            if jobs:
                                job(b, g, *jobs.pop(0))
                            if k % 2 == 1 and k >= 3:
                                values(b, g, k // 2 - 1)
                            for what, n in jobs:
                                job(b, g, what, n)
                        values(b, g, NB - 1)

                with pe.Fori(0, B - 1) as b:
                    body(b)
                body(B - 1)
                job(B - 1, NG, ("out", 0, 0), numbered(B - 1)[1])

            @block.scalar
            def _(act):
                act.nop().then_inc(ex_done, 2)

                def fill_mt(b, g, half, n, at_b):
                    act.wait_ge(bank_made[n % NBK], turns(at_b, n) + 1)
                    if half == 0 and not (isinstance(b, int) and b * NG + g == 0):
                        act.wait_ge(m_in[(g - 1) % NSL], at(b, (g - 1) // NSL * NSL, 16, 64))
                    act.activation(mt[:, half * CH:(half + 1) * CH], ps_m[n % NBK][0:2 * GH, :], ACT.Copy
                                   ).then_inc(bank_read[n % NBK], 1)
                    if half == 1:
                        act.wait_ge(bank_read[n % NBK], turns(at_b, n) + 1)
                        act.wait_ge(bank_read[(n - 1) % NBK], turns(at_b, n - 1) + 1)
                        act.nop().then_inc(mt_done, 1)

                def keep_out(b, g, c):
                    act.wait_ge(pv_done, at(b, g, NB, 3 + TC * c))
                    act.wait_ge(y_done, at(b, g, 2, c + 1))
                    act.activation(ot[:], ps_o[:], ACT.Copy).then_inc(ot_done, 1)

                for n, (kind, _, half) in enumerate(first):
                    if kind == "turn":
                        fill_mt(0, 0, half, n, 0)

                def body(b):
                    for g, steps in enumerate(numbered(b)[0]):
                        for k, (c, j, p) in enumerate(STEPS):
                            blk = k // 2
                            act.wait_ge(st_made, at(b, g, NS, k + 1))
                            act.wait_ge(pv_done, at(b, g, NB, blk + 1))
                            off = max(0, (j - c * TC) * P)
                            act.activation(pt[:, blk % 3, 2 * p:2 * p + 2, off:CH], ps_s[k % 2][:, :, off:CH],
                                           ACT.Exp, scale=HS ** -0.5).then_inc(ex_done, 1)
                            if k == 0:
                                keep_out(b, g, 0)
                            if k == 9:
                                keep_out(b, g, 1)
                            for what, n in steps[k]:
                                if what[0] == "turn":
                                    fill_mt(b, g + 1, what[2], n, b)

                with act.Fori(0, B - 1) as b:
                    body(b)
                body(B - 1)
                keep_out(B, 0, 0)

            @block.vector
            def _(dve):
                dve.nop().then_inc(y_done, 1)
                dve.memset(kg[0][:].bitcast(F32), 0.0).then_inc(init[0], 1)

                def unit(b, g, m, src):
                    i, piece, heads, k0, keys = UNITS[m]
                    src = src[:, 0:len(heads) * keys]
                    h = heads[0]
                    if len(heads) > 1:
                        return dve.tensor_reduce(pm[:, g % 2, i, piece, h:h + 3:2],
                                                 src.rearrange("p (h k) -> p h k", k=keys), AX.X, ALU.max)
                    return dve.tensor_reduce(pm[:, g % 2, i, piece, h:h + 1], src, AX.X, ALU.max)

                def negate(b, g, n, at_b, stage):
                    q = pm[:, g % 2]
                    if stage == 0:
                        for i in range(n - NBK, n):
                            dve.wait_ge(bank_read[i % NBK], turns(at_b, i) + 1)
                        dve.tensor_tensor(q[:, TC:TB, 0], q[:, TC:TB, 0], q[:, TC:TB, 1], ALU.max).then_inc(pm_done, 1)
                    elif stage == 1:
                        dve.wait_ge(pm_done, at(b, g, 1, 1))
                        if not (isinstance(b, int) and b * NG + g == 0):
                            dve.wait_ge(mt_done, at(b, g, 1, 0))
                        dve.tensor_scalar(nh[:, :, :, 0], q[:, :, 0], -1.0, None, ALU.mult).then_inc(nh_hi, 1)
                    else:
                        dve.wait_ge(nh_hi, at(b, g, 1, 1))
                        dve.scalar_tensor_tensor(nh[:, :, :, 1], q[:, :, 0], -1.0, nh[:, :, :, 0],
                                                 ALU.mult, ALU.subtract).then_inc(nh_done, 1)

                def normalise(b, g, c, src, release, released):
                    o = src[:].rearrange("p (t h w) -> p t h w", t=TC, h=GH)
                    dve.reciprocal(rec[:], o[:, :, :, HS]).then_inc(y_rec, 1)
                    dve.wait_ge(y_rec, at(b, g, 2, c + 1))
                    place = b * NG + (g + c)
                    half = 1 - c
                    dst = y[:, bass.ds(place, 1), half * TC:(half + 1) * TC, :].rearrange("p o t (h w) -> p (o t) h w", h=GH)
                    dve.tensor_tensor(dst, o[:, :, :, 0:HS], rec[:].unsqueeze(3).to_broadcast([P, TC, GH, HS]), ALU.mult
                                      ).then_inc(release, 1)
                    dve.wait_ge(release, released)
                    dve.nop().then_inc(y_done, 1)

                def job(b, g, what, n):
                    kind, more, m = what
                    bank = n % NBK
                    if kind == "turn":
                        return
                    dve.wait_ge(bank_made[bank], turns(b, n) + 1)
                    if kind == "unit":
                        unit(b, g + more, m, ps_m[bank]).then_inc(bank_read[bank], 1)
                        if m < 3 and not (isinstance(b, int) and b * NG + g + more == 0):
                            negate(b, g + more - 1, n, b, m)
                        if m == NU - 1 and not ahead(b, g + more, 1):
                            for stage in range(3):
                                negate(b, g + more, n + 1, b, stage)
                    else:
                        normalise(b, g, m, ps_m[bank], bank_read[bank], turns(b, n) + 1)

                for n, what in enumerate(first):
                    job(0, 0, what, n)

                def body(b):
                    for g, steps in enumerate(numbered(b)[0]):
                        for k in range(NS):
                            for what, n in steps[k]:
                                job(b, g, what, n)

                with dve.Fori(0, B - 1) as b:
                    body(b)
                body(B - 1)
                job(B - 1, NG, ("out", 0, 0), numbered(B - 1)[1])


E, K, F = 8, 2, 1024
FT = F // P
XT = 256
NT = K * N // XT + E
MOE_EPS = 1e-6
TILES = N // P


def route(nc, d, keep):
    with ExitStack() as ctx:
        s = Store(nc, ctx, "route")
        ident = keep["ident"]
        y, xf = keep["y"], keep["xf"]
        wgt, slot, base = keep["wgt"], keep["slot"], keep["base"]
        gb = keep["gb"]
        raw1, raw2, w1, w2 = keep["raw1"], keep["raw2"], keep["w1_0"], keep["w2_0"]
        xh = s.sb("xh", [P, TILES, C])
        yn = s.sb("yn", [P, TB, C])
        xb = s.sb("xb", [P, TB, C])
        stats = s.sb("stats", [P, 3, TB, 6])
        mv = s.sb("mv", [P, 3, TB, 2])
        veps = s.sb("veps", [P, 3, TB])
        rstd = s.sb("rstd", [P, 3, TB])
        nmean = s.sb("nmean", [P, 3, TB])
        shift = s.sb("shift", [P, 3, TB])
        mhalf = s.sb("mhalf", [P, TB])
        xfT = s.sb("xfT", [P, 2, CT, P])
        wg = s.sb("wg", [P, CT, E])
        before = s.sb("before", [P, P])
        ones = s.sb("ones", [P, TILES])
        ones_sq = s.sb("ones_sq", [P, P])
        ei = s.sb("ei", [P, E])
        ti = s.sb("ti", [E, NT + 1])
        gam = s.sb("gam", [E, 2, C])
        best = s.sb("best", [P, TILES, 8])
        order = s.sb("order", [P, TILES, 8], mybir.dt.uint32)
        which = s.sb("which", [P, K, TILES])
        pick = s.sb("pick", [P, K, TILES, E])
        taken = s.sb("taken", [P, TILES, E])
        upto = s.sb("upto", [P, E, TILES])
        place = s.sb("place", [P, TILES, E])
        tiles_i = s.sb("tiles_i", [P, E], mybir.dt.int32)
        tiles_f = s.sb("tiles_f", [P, E])
        base_f = s.sb("base_f", [P, E + 1])
        hit = s.sb("hit", [P, TILES, E])
        slot_f = s.sb("slot_f", [P, TILES])
        de = s.sb("de", [P, TILES])
        edge = s.sb("edge", [E, 2, E])
        edges = s.sb("edges", [E, 2])
        own = s.sb("own", [E, 2, NT + 1])

        ps_x = [s.ps(f"ps_x{i}", [P, CT, P]) for i in range(2)]
        ps_g = s.ps("ps_g", [P, TILES, E])
        ps_r = s.ps("ps_r", [P, TILES, E])
        ps_n = s.ps("ps_n", [P, TILES, E])
        ps_b = s.ps("ps_b", [P, 2, CT, NT + 1])

        x_in, c_in, consts = s.sem("x_in"), s.sem("c_in"), s.sem("consts")
        stat, aggr, rs, step = s.sem("stat"), s.sem("aggr"), s.sem("rs"), s.sem("step")
        ve_done, yn_done, x1_done, xf_done, xh_done = (
            s.sem(n) for n in ("ve_done", "yn_done", "x1_done", "xf_done", "xh_done"))
        turned, turn_kept, gated, ranked, weights_in, slots_in, gb_made = (
            s.sem(n) for n in ("turned", "turn_kept", "gated", "ranked", "weights_in", "slots_in", "gb_made"))
        exp_done, scattered, picked, owned, xf_kept, root_done = (
            s.sem(n) for n in ("exp_done", "scattered", "picked", "owned", "xf_kept", "root_done"))
        w0_in, w0_hi, w0_lo = s.sem("w0_in"), s.sem("w0_hi"), s.sem("w0_lo")

        def tile(buf, b, t):
            return buf[:, bass.ds(b * TB + t, 1), :].rearrange("p o c -> p (o c)")

        def head_tile(b, t):
            return y[:, bass.ds(b * NG + 1, NG), t, :]

        def by_group(buf, t):
            return buf[:, t].rearrange("p (g w) -> p g w", g=NG)

        with nc.Block() as block:
            @block.sync
            def _(sp):
                for b in range(B):
                    sp.dma_start(xf[:, b * TB:(b + 1) * TB], d["x"][b * T:(b + 1) * T, :].rearrange("(k p) c -> p k c", p=P)
                                 ).then_inc(x_in, 16)
                for dst, src in ((wg[:], d["wg"].rearrange("(k p) e -> p k e", p=P)), (before[:], d["before"]),
                                 (ei[:], d["ei"]), (ti[:], d["ti"]), (gam[:, 0], d["gamma"]), (gam[:, 1], d["beta"])):
                    sp.dma_start(dst, src).then_inc(c_in, 16)
                sp.dma_start(raw1[:], d["w1"][0].rearrange("(k p) f -> p k f", p=P)).then_inc(w0_in, 16)
                sp.dma_start(raw2[:], d["w2"][0].rearrange("(k p) c -> p k c", p=P)).then_inc(w0_in, 16)

            @block.gpsimd
            def _(pool):
                pool.memset(mhalf[:], -0.5).then_inc(consts, 1)
                pool.memset(ones[:], 1.0).then_inc(consts, 1)
                pool.memset(ones_sq[:], 1.0).then_inc(consts, 1)
                pool.wait_ge(consts, 3)

                def roots(n, call):
                    pool.wait_ge(aggr, call * TB + TB)
                    settle(pool, keep["passed"])
                    pool.tensor_scalar(veps[:, n], mv[:, n, :, 1], MOE_EPS if n == 2 else LN_EPS, None, ALU.add
                                       ).then_inc(ve_done, 1)
                    pool.tensor_scalar(nmean[:, n], mv[:, n, :, 0], -1.0, None, ALU.mult).then_inc(ve_done, 1)
                    pool.wait_ge(ve_done, call * 2 + 2)
                    pool.tensor_tensor(rstd[:, n], veps[:, n], mhalf[:], ALU.pow).then_inc(root_done, 1)
                    pool.wait_ge(root_done, call + 1)
                    pool.tensor_tensor(shift[:, n], nmean[:, n], rstd[:, n], ALU.mult).then_inc(rs, 1)

                roots(0, 0)
                roots(1, 1)
                with pool.Fori(0, B - 1) as b:
                    roots(0, b * 3 + 2)
                    roots(2, b * 3 + 3)
                    roots(1, b * 3 + 4)
                roots(2, 3 * B - 1)
                pool.wait_ge(slots_in, 1)
                pool.wait_ge(xh_done, B)
                for k in range(K):
                    for t in range(TILES):
                        pool.indirect_dma_start(d["xs"], bass.IndirectOffsetOnAxis(ap=slot[:, k, t:t + 1], axis=0),
                                                xh[:, t, :], None).then_inc(scattered, 16)
                pool.wait_ge(scattered, 16 * K * TILES)

            @block.vector
            def _(dve):
                dve.wait_ge(consts, 3)

                def moments(n, src, call):
                    settle(dve, keep["passed"])
                    for t in range(TB):
                        dve.bn_stats(stats[:, n, t], src(t)).then_inc(stat, 1)
                    dve.wait_ge(stat, call * TB + TB)
                    settle(dve, keep["passed"])
                    for t in range(TB):
                        dve.bn_aggr(mv[:, n, t], stats[:, n, t]).then_inc(aggr, 1)

                def residual(b):
                    for t in range(TB):
                        dve.wait_ge(yn_done, b * TB + t + 1)
                        dve.tensor_tensor(head_tile(b, t), tile(xf, b, t).rearrange("p (g w) -> p g w", g=NG),
                                          by_group(yn, t), ALU.add).then_inc(x1_done, 1)
                    dve.wait_ge(x1_done, b * TB + TB)

                def normalise(b, call):
                    dve.wait_ge(rs, call + 1)
                    dve.wait_ge(xf_kept, b + 1)
                    for t in range(TB):
                        dve.tensor_scalar(by_group(xb, t), head_tile(b, t), mv[:, 1, t, 0:1], rstd[:, 1, t:t + 1],
                                          ALU.subtract, ALU.mult).then_inc(xf_done, 1)
                    dve.wait_ge(xf_done, b * TB + TB)

                moments(0, lambda t: head_tile(0, t), 0)
                dve.wait_ge(x_in, 16 * B)
                residual(0)
                moments(1, lambda t: head_tile(0, t), 1)
                with dve.Fori(0, B - 1) as b:
                    moments(0, lambda t: head_tile(b + 1, t), b * 3 + 2)
                    normalise(b, b * 3 + 1)
                    moments(2, lambda t: xb[:, t], b * 3 + 3)
                    residual(b + 1)
                    moments(1, lambda t: head_tile(b + 1, t), b * 3 + 4)
                normalise(B - 1, 3 * B - 2)
                moments(2, lambda t: xb[:, t], 3 * B - 1)

                n = 0

                def then(ins):
                    nonlocal n
                    n += 1
                    ins.then_inc(step, 1)
                    dve.wait_ge(step, n)

                dve.wait_ge(gated, TILES + 2)
                dve.wait_ge(c_in, 16 * 6)
                for t in range(TILES):
                    ins = dve.max(best[:, t], ps_g[:, t])
                then(ins)
                for t in range(TILES):
                    ins = dve.max_index(order[:, t], best[:, t], ps_g[:, t])
                then(ins)
                then(dve.tensor_copy(which[:], order[:, :, 0:K].rearrange("p t k -> p k t")))
                for k in range(K):
                    ins = dve.tensor_tensor(pick[:, k], ei[:].unsqueeze(1).to_broadcast([P, TILES, E]),
                                            which[:, k].unsqueeze(2).to_broadcast([P, TILES, E]), ALU.is_equal)
                then(ins)
                dve.tensor_tensor(taken[:], pick[:, 0], pick[:, 1], ALU.add).then_inc(picked, 1)
                then(dve.tensor_tensor(de[:], best[:, :, 1], best[:, :, 0], ALU.subtract))
                dve.nop().then_inc(weights_in, 1)
                dve.wait_ge(exp_done, 1)
                then(dve.tensor_scalar(de[:], wgt[:, 1], 1.0, None, ALU.add))
                then(dve.reciprocal(wgt[:, 0], de[:]))
                then(dve.tensor_tensor(wgt[:, 1], wgt[:, 1], wgt[:, 0], ALU.mult))
                then(dve.tensor_tensor(wgt[:, 2], wgt[:, 1], wgt[:, 0], ALU.add))
                dve.wait_ge(ranked, 1)
                for e in range(E):
                    ins = dve.tensor_tensor_scan(upto[:, e], ones[:], ps_n[:, :, e], 0.0, ALU.mult, ALU.add)
                then(ins)
                then(dve.tensor_scalar(tiles_f[:], upto[:, :, TILES - 1], float(XT - 1), float(XT), ALU.add, ALU.max))
                then(dve.tensor_copy(tiles_i[:], tiles_f[:]))
                then(dve.tensor_scalar(tiles_i[:], tiles_i[:], XT.bit_length() - 1, None, ALU.logical_shift_right))
                then(dve.tensor_copy(tiles_f[:], tiles_i[:]))
                then(dve.memset(base_f[:, 0:1], 0.0))
                then(dve.tensor_tensor_scan(base_f[:, 1:E + 1], ones[:, 0:E], tiles_f[:], 0.0, ALU.mult, ALU.add))
                then(dve.tensor_copy(base[:], base_f[:]))
                then(dve.tensor_copy(place[:], ps_r[:]))
                then(dve.tensor_tensor(place[:], place[:], upto[:].rearrange("p e t -> p t e"), ALU.add))
                then(dve.tensor_tensor(place[:], place[:], ps_n[:], ALU.subtract))
                then(dve.scalar_tensor_tensor(place[:], base_f[:, 0:E].unsqueeze(1).to_broadcast([P, TILES, E]), float(XT),
                                              place[:], ALU.mult, ALU.add))
                for k in range(K):
                    then(dve.tensor_tensor(hit[:], pick[:, k], place[:], ALU.mult))
                    then(dve.tensor_reduce(slot_f[:], hit[:], AX.X, ALU.add))
                    then(dve.tensor_copy(slot[:, k], slot_f[:]))
                dve.nop().then_inc(slots_in, 1)
                for k in range(2):
                    ins = dve.tensor_tensor(edge[:, k], ident[0:E, 0:E], base_f[0:E, k:k + E], ALU.mult)
                then(ins)
                then(dve.tensor_reduce(edges[:], edge[:], AX.X, ALU.add))
                dve.tensor_scalar(own[:, 0], ti[:], edges[:, 0:1], None, ALU.is_ge)
                then(dve.tensor_scalar(own[:, 1], ti[:], edges[:, 1:2], None, ALU.is_lt))
                dve.tensor_tensor(own[:, 0], own[:, 0], own[:, 1], ALU.mult).then_inc(owned, 1)
                dve.wait_ge(gb_made, 1)
                then(dve.tensor_copy(gb[:], ps_b[:]))
                dve.wait_ge(w0_hi, 2)
                dve.tensor_tensor(w1[1][:], raw1[:], w1[0][:], ALU.subtract).then_inc(w0_lo, 1)
                dve.tensor_tensor(w2[1][:], raw2[:], w2[0][:], ALU.subtract).then_inc(w0_lo, 1)
                dve.wait_ge(w0_lo, 2)

            @block.scalar
            def _(act):
                act.nop().then_inc(turn_kept, 2)
                act.nop().then_inc(xf_kept, 1)

                def norm_y(b, call):
                    act.wait_ge(rs, call + 1)
                    settle(act, keep["passed"])
                    for t in range(TB):
                        act.activation(by_group(yn, t), head_tile(b, t), ACT.Identity, scale=rstd[:, 0, t:t + 1],
                                       bias=shift[:, 0, t:t + 1]).then_inc(yn_done, 1)

                def keep_batch(b, call):
                    for t in range(TB):
                        act.wait_ge(turned, b * TB + t + 1)
                        act.wait_ge(gated, b * TB + t + 1)
                        act.activation(xfT[:, t % 2], ps_x[t % 2][:], ACT.Copy).then_inc(turn_kept, 1)
                    act.wait_ge(rs, call + 1)
                    settle(act, keep["passed"])
                    for t in range(TB):
                        ins = act.activation(tile(xh, b, t), xb[:, t], ACT.Identity, scale=rstd[:, 2, t:t + 1],
                                             bias=shift[:, 2, t:t + 1])
                    ins.then_inc(xh_done, 1)
                    act.wait_ge(xh_done, b + 1)
                    act.activation(xf[:, bass.ds(b * TB, TB), :], xb[:], ACT.Copy).then_inc(xf_kept, 1)

                norm_y(0, 0)
                with act.Fori(0, B - 1) as b:
                    act.wait_ge(x1_done, b * TB + TB)
                    norm_y(b + 1, b * 3 + 2)
                    keep_batch(b, b * 3 + 3)
                keep_batch(B - 1, 3 * B - 1)
                act.wait_ge(weights_in, 1)
                act.activation(wgt[:, 1], de[:], ACT.Exp).then_inc(exp_done, 1)
                act.wait_ge(w0_in, 32)
                act.activation(w1[0][:], raw1[:], ACT.Copy).then_inc(w0_hi, 1)
                act.activation(w2[0][:], raw2[:], ACT.Copy).then_inc(w0_hi, 1)

            @block.tensor
            def _(pe):
                pe.wait_ge(c_in, 16 * 6)
                pe.nop().then_inc(gated, 2)
                with pe.Fori(0, B) as b:
                    for t in range(TB + 1):
                        if t < TB:
                            pe.wait_ge(xf_done, b * TB + t + 1)
                            pe.wait_ge(turn_kept, b * TB + t + 1)
                            for k in range(CT):
                                ins = pe.transpose(ps_x[t % 2][:, k], xb[:, t, k * P:(k + 1) * P], ident[:])
                            ins.then_inc(turned, 1)
                        if t > 0:
                            pe.wait_ge(turn_kept, b * TB + (t - 1) + 1 + 2)
                            for k in range(CT):
                                ins = pe.matmul(ps_g[:, bass.ds(b * TB + (t - 1), 1), :].rearrange("p o e -> p (o e)"),
                                                xfT[:, (t - 1) % 2, k], wg[:, k], start=(k == 0), stop=(k == CT - 1))
                            ins.then_inc(gated, 1)
                pe.wait_ge(picked, 1)
                pe.matmul(ps_r[:].rearrange("p t e -> p (t e)"), before[:], taken[:].rearrange("p t e -> p (t e)"),
                          start=True, stop=True)
                pe.matmul(ps_n[:].rearrange("p t e -> p (t e)"), ones_sq[:], taken[:].rearrange("p t e -> p (t e)"),
                          start=True, stop=True).then_inc(ranked, 1)
                pe.wait_ge(owned, 1)
                for n in range(2):
                    for k in range(CT):
                        ins = pe.matmul(ps_b[:, n, k], gam[:, n, k * P:(k + 1) * P], own[:, 0], start=True, stop=True)
                ins.then_inc(gb_made, 1)


def experts(nc, d, keep):
    with ExitStack() as ctx:
        s = Store(nc, ctx, "moe")
        ident, base, gb = keep["ident"], keep["base"], keep["gb"]
        raw1, raw2 = keep["raw1"], keep["raw2"]
        w1 = [keep["w1_0"], [s.sb(f"w1{p}", [P, CT, F], F32R) for p in "hl"]]
        w2 = [keep["w2_0"], [s.sb(f"w2{p}", [P, FT, C], F32R) for p in "hl"]]
        b1 = [s.sb(f"b1{r}", [P, FT]) for r in range(2)]
        b2 = [s.sb(f"b2{r}", [P, C]) for r in range(2)]
        rows = s.sb("rows", [P, 2, C])
        xg = s.sb("xg", [P, CT, XT])
        xT = [s.sb(f"xT{p}", [P, CT, XT], F32R) for p in "hl"]
        hf = s.sb("hf", [P, 4, XT])
        hT = [s.sb(f"hT{p}", [P, FT, XT], F32R) for p in "hl"]
        o = s.sb("o", [P, 2, C])

        ps_x = s.ps("ps_x", [P, CT, XT])
        ps_h = [s.ps(f"ps_h{i}", [P, XT]) for i in range(4)]
        ps_o = [s.ps(f"ps_o{i}", [P, C]) for i in range(2)]
        NHB = len(ps_h)

        raw_in, raw_used, w_made, w_used = s.sem("raw_in"), s.sem("raw_used"), s.sem("w_made"), s.sem("w_used")
        b_in = [s.sem(f"b_in{r}") for r in range(2)]
        rows_in, turned, xg_done, xh_done, xl_done, h_made, hf_done, hh_done, hl_done, up_done, out_made, o_done, stored = (
            s.sem(n) for n in ("rows_in", "turned", "xg_done", "xh_done", "xl_done", "h_made", "hf_done", "hh_done", "hl_done",
                               "up_done", "out_made", "o_done", "stored"))
        bv, b_used = s.sem("bv"), s.sem("b_used")
        pieces = ((0, 0), (0, 1), (1, 0))

        def each(eng, expert, tile, late=None):
            with eng.Fori(0, E // 2) as q:
                for r in range(2):
                    expert(q, r)
                    first = eng.value_load(base[0:1, bass.ds(q * 2 + r, 1)], min_val=0, max_val=NT - 1)
                    last = eng.value_load(base[0:1, bass.ds(q * 2 + (r + 1), 1)], min_val=1, max_val=NT)
                    with eng.Fori(first, last) as i:
                        tile(r, i)
                    if late:
                        late(last)

        with nc.Block() as block:
            @block.sync
            def _(sp):
                def fetch(i):
                    sp.dma_start(rows[:], d["xs"][bass.ds(i * XT, XT), :].rearrange("(k p) c -> p k c", p=P)
                                 ).then_inc(rows_in, 16)

                fetch(0)
                sp.nop().then_inc(stored, 1)

                def tile(r, i):
                    sp.wait_ge(turned, i + 1)
                    fetch(i + 1)
                    sp.wait_ge(o_done, i * 2 + 4)
                    sp.dma_start(d["xs"][bass.ds(i * XT, XT), :].rearrange("(k p) c -> p k c", p=P), o[:]
                                 ).then_inc(stored, 16)

                each(sp, lambda q, r: None, tile)
                total = sp.value_load(base[0:1, E:E + 1], min_val=1, max_val=NT)
                sp.wait_ge(stored, total * 16 + 1)
                settle(sp, keep["passed"])

            @block.gpsimd
            def _(pool):
                def biases(q, r):
                    pool.dma_start(b1[r][:], d["b1"][:, bass.ds(q * 2 + r, 1), :].rearrange("p o f -> p (o f)")
                                   ).then_inc(b_in[r], 16)
                    pool.dma_start(b2[r][:], d["b2"][bass.ds(q * 2 + r, 1), :].rearrange("o c -> (o c)").partition_broadcast(P)
                                   ).then_inc(b_in[r], 16)

                def fill(q, r):
                    pool.dma_start(raw1[:], d["w1"][bass.ds(q * 2 + r, 1)].rearrange("o (k p) f -> (o p) k f", p=P)
                                   ).then_inc(raw_in, 16)
                    pool.dma_start(raw2[:], d["w2"][bass.ds(q * 2 + r, 1)].rearrange("o (k p) c -> (o p) k c", p=P)
                                   ).then_inc(raw_in, 16)
                    pool.wait_ge(w_used, q * 2 + r + 1)
                    pool.wait_ge(b_used, q * 2 + r + 1)
                    biases(q, r)
                    pool.wait_ge(raw_in, q * 64 + r * 32)
                    settle(pool, keep["passed"])
                    pool.tensor_copy(w1[r][0][:], raw1[:]).then_inc(bv, 1)
                    pool.tensor_copy(w2[r][0][:], raw2[:]).then_inc(bv, 1)
                    pool.wait_ge(bv, q * 4 + r * 2)
                    pool.tensor_tensor(w1[r][1][:], raw1[:], w1[r][0][:], ALU.subtract).then_inc(w_made, 1)
                    pool.tensor_tensor(w2[r][1][:], raw2[:], w2[r][0][:], ALU.subtract).then_inc(w_made, 1)
                    pool.wait_ge(w_made, q * 4 + r * 2 + 2)

                pool.nop().then_inc(w_made, 2)
                biases(0, 0)
                fill(0, 1)
                with pool.Fori(1, E // 2) as q:
                    for r in range(2):
                        fill(q, r)

            @block.tensor
            def _(pe):
                pe.nop().then_inc(w_used, 2)
                pe.nop().then_inc(up_done, 1)
                def turn(n):
                    pe.wait_ge(rows_in, n * 16)
                    pe.wait_ge(xg_done, n)
                    for t in range(XT // P):
                        for k in range(CT):
                            ins = pe.transpose(ps_x[:, k, t * P:(t + 1) * P], rows[:, t, k * P:(k + 1) * P], ident[:])
                    ins.then_inc(turned, 1)

                turn(1)

                def tile(r, i):
                    pe.wait_ge(xl_done, i + 1)
                    for f in range(FT):
                        pe.wait_ge(hf_done, i * FT + (f + 1))
                        n = 0
                        for k in range(CT):
                            for a, m in pieces:
                                ins = pe.matmul(ps_h[f % NHB][:], w1[r][a][:, k, f * P:(f + 1) * P], xT[m][:, k],
                                                start=(n == 0), stop=(n == 3 * CT - 1))
                                n += 1
                        ins.then_inc(h_made, 1)
                    turn(i + 2)
                    pe.wait_ge(o_done, i * 2 + 2)
                    for f in range(FT):
                        pe.wait_ge(hl_done, i * FT + (f + 1 + NHB))
                        for t in range(XT // P):
                            for a, m in pieces:
                                ins = pe.matmul(ps_o[t][:], hT[a][:, f, t * P:(t + 1) * P], w2[r][m][:, f],
                                                start=(f == 0 and (a, m) == pieces[0]),
                                                stop=(f == FT - 1 and (a, m) == pieces[-1]))
                    ins.then_inc(out_made, 1)

                def expert(q, r):
                    pe.wait_ge(w_made, q * 4 + r * 2 + 2)
                    settle(pe, keep["passed"])

                def leave(last):
                    pe.wait_ge(out_made, last)
                    pe.nop().then_inc(w_used, 1)

                each(pe, expert, tile, leave)

            @block.scalar
            def _(act):
                act.nop().then_inc(hf_done, NHB)
                act.nop().then_inc(xg_done, 1)

                def feed(i, n):
                    act.wait_ge(turned, n)
                    for k in range(CT):
                        ins = act.activation(xg[:, k], ps_x[:, k], ACT.Identity, scale=gb[:, 0, k, i], bias=gb[:, 1, k, i])
                    ins.then_inc(xg_done, 1)
                    act.wait_ge(xg_done, n + 1)
                    act.activation(xT[0][:], xg[:], ACT.Copy).then_inc(xh_done, 1)

                feed(slice(0, 1), 1)

                def tile(r, i):
                    for f in range(FT):
                        act.wait_ge(h_made, i * FT + (f + 1))
                        act.wait_ge(hl_done, i * FT + (f + 1))
                        act.activation(hf[:, f % NHB], ps_h[f % NHB][:], ACT.Relu, bias=b1[r][:, f:f + 1]).then_inc(hf_done, 1)
                    feed(bass.ds(i + 1, 1), i + 2)

                def expert(q, r):
                    act.wait_ge(b_in[r], q * 32 + 32)
                    settle(act, keep["passed"])

                each(act, expert, tile)

            @block.vector
            def _(dve):
                dve.nop().then_inc(hl_done, NHB)
                dve.nop().then_inc(o_done, 2)
                dve.nop().then_inc(b_used, 2)

                def feed(n):
                    dve.wait_ge(xh_done, n)
                    dve.tensor_tensor(xT[1][:], xg[:], xT[0][:], ALU.subtract).then_inc(xl_done, 1)

                feed(1)

                def tile(r, i):
                    for f in range(FT):
                        dve.wait_ge(hf_done, i * FT + (f + 1 + NHB))
                        dve.tensor_copy(hT[0][:, f], hf[:, f % NHB]).then_inc(hh_done, 1)
                        dve.wait_ge(hh_done, i * FT + (f + 1))
                        dve.tensor_tensor(hT[1][:, f], hf[:, f % NHB], hT[0][:, f], ALU.subtract).then_inc(hl_done, 1)
                    feed(i + 2)
                    dve.wait_ge(out_made, i + 1)
                    dve.wait_ge(stored, i * 16 + 1)
                    for t in range(XT // P):
                        dve.tensor_tensor(o[:, t], ps_o[t][:], b2[r][:], ALU.add).then_inc(o_done, 1)

                def leave(last):
                    dve.wait_ge(o_done, last * 2 + 2)
                    dve.nop().then_inc(b_used, 1)

                def expert(q, r):
                    dve.wait_ge(b_in[r], q * 32 + 32)
                    settle(dve, keep["passed"])

                each(dve, expert, tile, leave)


def combine(nc, d, keep):
    with ExitStack() as ctx:
        s = Store(nc, ctx, "comb")
        y, xf, wgt, slot = keep["y"], keep["xf"], keep["wgt"], keep["slot"]
        TQ = 4
        NQ = TILES // TQ
        g = s.sb("g", [P, TILES, K, C])
        acc = s.sb("acc", [P, TILES, C])
        stats = s.sb("stats", [P, TILES, 6])
        mv = s.sb("mv", [P, TILES, 2])
        veps = s.sb("veps", [P, TILES])
        nmean = s.sb("nmean", [P, TILES])
        rstd = s.sb("rstd", [P, TILES])
        shift = s.sb("shift", [P, TILES])
        mhalf = s.sb("mhalf", [P, TQ])
        zn = s.sb("zn", [P, TILES, C])
        gathered = [s.sem(f"gathered{q}") for q in range(NQ)]
        consts, w0, w1, w2, st, ag, ve, rt, rs, zd, done, stored = (
            s.sem(n) for n in ("consts", "w0", "w1", "w2", "st", "ag", "ve", "rt", "rs", "zd", "done", "stored"))

        def part(q):
            return range(q * TQ, (q + 1) * TQ)

        with nc.Block() as block:
            @block.gpsimd
            def _(pool):
                pool.memset(mhalf[:], -0.5).then_inc(consts, 1)
                pool.wait_ge(consts, 1)

                def roots(q):
                    tiles = slice(q * TQ, (q + 1) * TQ)
                    pool.wait_ge(ag, (q + 1) * TQ)
                    pool.tensor_scalar(veps[:, tiles], mv[:, tiles, 1], LN_EPS, None, ALU.add).then_inc(ve, 1)
                    pool.tensor_scalar(nmean[:, tiles], mv[:, tiles, 0], -1.0, None, ALU.mult).then_inc(ve, 1)
                    pool.wait_ge(ve, q * 2 + 2)
                    pool.tensor_tensor(rstd[:, tiles], veps[:, tiles], mhalf[:], ALU.pow).then_inc(rt, 1)
                    pool.wait_ge(rt, q + 1)
                    pool.tensor_tensor(shift[:, tiles], nmean[:, tiles], rstd[:, tiles], ALU.mult).then_inc(rs, 1)

                for q in range(NQ):
                    for t in part(q):
                        for k in range(K):
                            pool.indirect_dma_start(g[:, t, k], None, d["xs"],
                                                    bass.IndirectOffsetOnAxis(ap=slot[:, k, t:t + 1], axis=0)
                                                    ).then_inc(gathered[q], 16)
                    if q > 1:
                        roots(q - 2)
                roots(NQ - 2)
                roots(NQ - 1)

            @block.scalar
            def _(act):
                for t in range(TILES):
                    act.activation(acc[:, t], xf[:, t], ACT.Identity, scale=wgt[:, 2, t:t + 1]).then_inc(w0, 1)
                for q in range(NQ):
                    act.wait_ge(rs, q + 1)
                    for t in part(q):
                        act.activation(zn[:, t], acc[:, t], ACT.Identity, scale=rstd[:, t:t + 1], bias=shift[:, t:t + 1]
                                       ).then_inc(zd, 1)

            @block.vector
            def _(dve):
                def attention(q):
                    for t in part(q):
                        dve.wait_ge(zd, t + 1)
                        z = zn[:, t].rearrange("p (g w) -> p g w", g=NG)
                        b = t // TB
                        dve.tensor_tensor(z, z, y[:, b * NG + 1:(b + 1) * NG + 1, t % TB, :], ALU.add).then_inc(done, 1)

                for q in range(NQ):
                    dve.wait_ge(gathered[q], 16 * K * TQ)
                    for t in part(q):
                        dve.wait_ge(w0, t + 1)
                        dve.scalar_tensor_tensor(acc[:, t], g[:, t, 0], wgt[:, 0, t:t + 1], acc[:, t], ALU.mult, ALU.add
                                                 ).then_inc(w1, 1)
                    for t in part(q):
                        dve.wait_ge(w1, t + 1)
                        dve.scalar_tensor_tensor(acc[:, t], g[:, t, 1], wgt[:, 1, t:t + 1], acc[:, t], ALU.mult, ALU.add
                                                 ).then_inc(w2, 1)
                    for t in part(q):
                        dve.wait_ge(w2, t + 1)
                        dve.bn_stats(stats[:, t], acc[:, t]).then_inc(st, 1)
                    for t in part(q):
                        dve.wait_ge(st, t + 1)
                        dve.bn_aggr(mv[:, t], stats[:, t]).then_inc(ag, 1)
                    if q > 2:
                        attention(q - 3)
                for q in range(NQ - 3, NQ):
                    attention(q)

            @block.sync
            def _(sp):
                for q in range(NQ):
                    sp.wait_ge(done, (q + 1) * TQ)
                    sp.dma_start(d["out"][q * TQ * P:(q + 1) * TQ * P, :].rearrange("(k p) c -> p k c", p=P),
                                 zn[:, q * TQ:(q + 1) * TQ]).then_inc(stored, 16)
                sp.wait_ge(stored, 16 * NQ)


_INS = ["x", "wz", "wdq", "wuqT", "wuq", "wuk", "wuv", "woT", "ident", "identb", "mask_ts", "mask_st",
        "wg", "before", "ei", "ti", "gamma", "beta", "w1", "w2", "b1", "b2"]


def build(nc, d):
    with ExitStack() as ctx:
        s = Store(nc, ctx, "keep")
        keep = {"ident": s.sb("ident", [P, P]), "identb": s.sb("identb", [P, P], BF16),
                "passed": s.sem("passed"),
                "mask_ts": s.sb("mask_ts", [P, P], BF16), "mask_st": s.sb("mask_st", [P, P], BF16)}
        project(nc, d, keep)
        keep["y"] = s.sb("y", [P, B * NG + 1, TB, GH * HS])
        attend(nc, d, keep)
        keep["xf"] = s.sb("xf", [P, TILES, C])
        keep["wgt"] = s.sb("wgt", [P, 3, TILES])
        keep["slot"] = s.sb("slot", [P, K, TILES], mybir.dt.uint32)
        keep["base"] = s.sb("base", [P, E + 1], mybir.dt.int32)
        keep["gb"] = s.sb("gb", [P, 2, CT, NT + 1])
        with ExitStack() as inner:
            w = Store(nc, inner, "weights")
            keep["raw1"], keep["raw2"] = w.sb("raw1", [P, CT, F]), w.sb("raw2", [P, FT, C])
            keep["w1_0"] = [w.sb(f"w1_0{p}", [P, CT, F], F32R) for p in "hl"]
            keep["w2_0"] = [w.sb(f"w2_0{p}", [P, FT, C], F32R) for p in "hl"]
            route(nc, d, keep)
            experts(nc, d, keep)
        combine(nc, d, keep)


def kernel(**inputs):
    import concourse.bacc as bacc
    import ml_dtypes
    from concourse.bass_utils import run_bass_kernel_spmd

    w = {k.replace("L0_attn_", "").replace("L0_ffn_", ""): np.asarray(a) for k, a in inputs.items()}
    future = np.triu(np.full((P, P), -1e30, np.float32), 1)
    arrays = {
        "x": w["x"].reshape(N, C),
        "wz": np.concatenate([w["W_dq"].T, w["W_dkv"].T], axis=1),
        "wdq": w["W_dq"], "wuqT": w["W_uq"].T, "wuq": w["W_uq"], "wuk": w["W_uk"], "wuv": w["W_uv"], "woT": w["W_o"].T,
        "ident": np.eye(P, dtype=np.float32), "identb": np.eye(P).astype(ml_dtypes.bfloat16),
        "mask_ts": future.astype(ml_dtypes.bfloat16), "mask_st": future.T.astype(ml_dtypes.bfloat16),
        "wg": w["Wg"], "before": np.triu(np.ones((P, P), np.float32), 1),
        "ei": np.tile(np.arange(E, dtype=np.float32), (P, 1)),
        "ti": np.tile(np.arange(NT + 1, dtype=np.float32), (E, 1)),
        "gamma": w["gamma"], "beta": w["beta"], "w1": w["W1"], "w2": w["W2"],
        "b1": w["b1"].reshape(E, FT, P).transpose(2, 0, 1), "b2": w["b2"],
    }
    nc = bacc.Bacc("TRN2", target_bir_lowering=False, num_devices=1)
    d = {}
    for name in _INS:
        arrays[name] = np.ascontiguousarray(arrays[name])
        d[name] = nc.dram_tensor(f"in_{name}", arrays[name].shape, mybir.dt.from_np(arrays[name].dtype),
                                 kind="ExternalInput").ap()
    d["qs"] = nc.dram_tensor("qs", (B, 2, NH * HS, T), F32, kind=SCRATCH).ap()
    d["ks"] = nc.dram_tensor("ks", (B, 2, NH * HS, T), F32, kind=SCRATCH).ap()
    d["vs"] = nc.dram_tensor("vs", (B * NG, P, TB, GH * VW), F32, kind=SCRATCH).ap()
    d["rows01"] = nc.dram_tensor("rows01", (2, 2, 2, T), F32, kind=SCRATCH).ap()
    d["xs"] = nc.dram_tensor("xs", ((NT + 1) * XT, C), F32, kind=SCRATCH).ap()
    d["out"] = nc.dram_tensor("out_0", (N, C), F32, kind="ExternalOutput").ap()
    build(nc, d)
    r = run_bass_kernel_spmd(nc, [{f"in_{name}": arrays[name] for name in _INS}], core_ids=[0])
    return r.results[0]["out_0"].reshape(B, T, C)
```

```python
from contextlib import ExitStack

import numpy as np

import concourse.bass as bass
from concourse import mybir

F32 = mybir.dt.float32
F32R = mybir.dt.float32r
BF16 = mybir.dt.bfloat16
ALU = mybir.AluOpType
ACT = mybir.ActivationFunctionType
AX = mybir.AxisListType

P = 128
B, T, C = 4, 1024, 256
N = B * T
NH, HS, KVL = 16, 16, 64
CT = C // P
CH = 512
NCH = T // CH
TC = CH // P
TB = T // P
GH = 4
NG = NH // GH
KR = 3 * HS
KM = KR + 2
VW = HS + 1
LN_EPS = 1e-5
SCRATCH = "Internal"


def settle(eng, passed):
    eng.sem_inc(passed, 1)


class Store:

    def __init__(self, nc, ctx, tag):
        self.nc, self.ctx, self.tag = nc, ctx, tag

    def sb(self, name, shape, dt=F32):
        return self.ctx.enter_context(self.nc.sbuf_tensor(f"{self.tag}_{name}", shape, dt))

    def ps(self, name, shape, dt=F32):
        return self.ctx.enter_context(self.nc.psum_tensor(f"{self.tag}_{name}", shape, dt))

    def sem(self, name):
        return self.ctx.enter_context(self.nc.semaphore(f"{self.tag}_{name}"))


NSL = NG


def add_slot(slots, s, g):
    slots["q"].append(s.sb(f"q{g}", [P, 2, T], F32R))
    slots["k"].append(s.sb(f"k{g}", [P, GH, T], F32R))
    slots["v"].append(s.sb(f"v{g}", [P, TB, GH * VW]))
    slots["loaded"].append(s.sem(f"loaded{g}"))
    slots["init"].append(s.sem(f"init{g}"))


LOADS = 16 * (4 * GH + 3) // NSL
ONES = 16 * 2


def load_ones(sp, d, slots, slot):
    for e in range(2):
        sp.dma_start(slots["k"][slot][64 * e + KR:64 * e + KM, e::2, :].bitcast(F32), d["rows01"][1]
                     ).then_inc(slots["loaded"][slot], 16)


def load_group(sp, d, slots, b, g):
    slot = g % NSL
    loaded, qg, kg = slots["loaded"][slot], slots["q"][slot], slots["k"][slot]
    qs, ks = (d[n][bass.ds(b + g // NG, 1)].rearrange("o k c t -> (o k) c t") for n in ("qs", "ks"))
    for h in range(GH):
        head = g % NG * GH + h
        r, c = 64 * (h % 2), slice(head * HS, (head + 1) * HS)
        for dst, src in ((qg[r:r + HS, h // 2, :], qs[0, c]), (qg[r + HS:r + KR, h // 2, :], qs[:, c]),
                         (kg[r:r + 2 * HS, h, :], ks[:, c]), (kg[r + 2 * HS:r + KR, h, :], ks[0, c])):
            sp.dma_start(dst.bitcast(F32), src).then_inc(loaded, 16)
    for e in range(2):
        sp.dma_start(qg[64 * e + KR:64 * e + KM].bitcast(F32), d["rows01"][0]).then_inc(loaded, 16)
    sp.dma_start(slots["v"][slot][:], d["vs"][bass.ds(b * NG + g, 1)].rearrange("o p k w -> (o p) k w")
                 ).then_inc(loaded, 16)


def project(nc, d, keep, slots):
    with ExitStack() as ctx:
        s = Store(nc, ctx, "proj")
        ident = keep["ident"]
        wz = s.sb("wz", [P, CT, P])
        wdq = s.sb("wdq", [KVL, C])
        wuqT = s.sb("wuqT", [P, C])
        wuq = s.sb("wuq", [P, CT, KVL])
        wuk = s.sb("wuk", [P, CT, KVL])
        wuv = s.sb("wuv", [P, CT, KVL])
        woT = s.sb("woT", [P, CT, C])
        amat = s.sb("amat", [KVL, KVL])
        kvw = s.sb("kvw", [P, 2, C])
        x = s.sb("x", [P, 2, TC, C])
        xn = s.sb("xn", [P, 2, TC, C])
        stats = s.sb("stats", [P, 2, TC, 6])
        mv = s.sb("mv", [P, 2, TC, 2])
        veps = s.sb("veps", [P, 2, TC])
        rstd = s.sb("rstd", [P, 2, TC])
        mhalf = s.sb("mhalf", [P, TC])
        xnT = s.sb("xnT", [P, 2, CT, CH])
        z = s.sb("z", [P, 2, CH])
        hi = s.sb("hi", [P, 2, 4, CH], F32R)
        lo = s.sb("lo", [P, 2, 4, CH], F32R)
        v = s.sb("v", [P, 2, TC, NH, VW])

        rows01 = s.sb("rows01", [2, 2, 2 * T], F32R)

        psX = s.ps("psX", [P, CT, CH])
        psZ = s.ps("psZ", [P, CH])
        psQ = s.ps("psQ", [P, 4, CH])
        psV = s.ps("psV", [P, 2, C])

        w_in = s.sem("w_in")
        x_in = [s.sem(f"x_in{u}") for u in range(2)]
        a_made, a_kept, kv_made, kv_kept = (s.sem(n) for n in ("a_made", "a_kept", "kv_made", "kv_kept"))
        stats_done, mv_done, veps_done, rstd_done, xn_done = (
            s.sem(n) for n in ("stats_done", "mv_done", "veps_done", "rstd_done", "xn_done"))
        consts = s.sem("consts")
        xT_made, xT_kept, z_made, z_kept = (s.sem(n) for n in ("xT_made", "xT_kept", "z_made", "z_kept"))
        qk_made, hi_done, lo_done = (s.sem(n) for n in ("qk_made", "hi_done", "lo_done"))
        v_made, v_kept = s.sem("v_made"), s.sem("v_kept")
        rows_made, rows_stored = s.sem("rows_made"), s.sem("rows_stored")
        stored = [s.sem(f"stored{u}") for u in range(2)]

        PER = 16 * (4 + NG)
        NC = B * NCH

        def exists(c):
            return not isinstance(c, int) or c < NC

        with nc.Block() as block:
            @block.sync
            def _(sp):
                for dst, src in ((ident[:], d["ident"]),
                                 (wuq[:], d["wuq"].rearrange("(k p) m -> p k m", p=P)),
                                 (wuk[:], d["wuk"].rearrange("(k p) m -> p k m", p=P)),
                                 (wuv[:], d["wuv"].rearrange("(k p) m -> p k m", p=P)),
                                 (woT[:], d["woT"].rearrange("(k p) m -> p k m", p=P)),
                                 (wdq[:], d["wdq"]),
                                 (wz[:], d["wz"].rearrange("(k p) m -> p k m", p=P)),
                                 (wuqT[0:KVL], d["wuqT"]), (keep["identb"][:], d["identb"]),
                                 (keep["mask_ts"][:], d["mask_ts"]), (keep["mask_st"][:], d["mask_st"])):
                    sp.dma_start(dst, src).then_inc(w_in, 16)

                sp.wait_ge(rows_made, 2)
                for k in range(2):
                    sp.dma_start(d["rows01"][k].rearrange("p h t -> p (h t)"), rows01[:, k].bitcast(F32)
                                 ).then_inc(rows_stored, 16)

                def store(b):
                    for u in range(2):
                        c = b * 2 + u
                        cols = slice(u * CH, (u + 1) * CH)
                        for m, name in ((0, "qs"), (2, "ks")):
                            dst = d[name][bass.ds(b, 1)].rearrange("o k (m p) t -> (o k) p m t", p=P)
                            sp.wait_ge(hi_done, c * 4 + m + 2)
                            sp.dma_start(dst[0, :, :, cols], hi[:, u, m:m + 2].bitcast(F32)).then_inc(stored[u], 16)
                            sp.wait_ge(lo_done, c * 4 + m + 2 + 4)
                            sp.dma_start(dst[1, :, :, cols], lo[:, u, m:m + 2].bitcast(F32)).then_inc(stored[u], 16)
                        sp.wait_ge(v_kept, c * 4 + 4 + 2)
                        for g in range(NG):
                            vs = d["vs"][bass.ds(b * NG + g, 1)].rearrange("o p k w -> (o p) k w")
                            sp.dma_start(vs[:, u * TC:(u + 1) * TC, :],
                                         v[:, u, :, g * GH:(g + 1) * GH, :].rearrange("p k h w -> p k (h w)")
                                         ).then_inc(stored[u], 16)
                with sp.Fori(0, B - 1) as b:
                    store(b)
                sp.wait_ge(rows_stored, 32)
                for u in range(2):
                    sp.wait_ge(stored[u], PER + 1)
                sp.wait_ge(slots["init"][0], 1)
                load_ones(sp, d, slots, 0)
                load_group(sp, d, slots, 0, 0)
                store(B - 1)
                for u in range(2):
                    sp.wait_ge(stored[u], PER * B + 1)

            @block.gpsimd
            def _(pool):
                def load(c, u):
                    pool.dma_start(x[:, u], d["x"][bass.ds(c * CH, CH), :].rearrange("(k p) c -> p k c", p=P)
                                   ).then_inc(x_in[u], 16)

                def deviation(c, u):
                    pool.wait_ge(mv_done, c * TC + TC)
                    settle(pool, keep["passed"])
                    pool.tensor_scalar(veps[:, u], mv[:, u, :, 1], LN_EPS, None, ALU.add).then_inc(veps_done, 1)
                    pool.wait_ge(veps_done, c + 1)
                    pool.tensor_tensor(rstd[:, u], veps[:, u], mhalf[:], ALU.pow).then_inc(rstd_done, 1)

                load(0, 0)
                load(1, 1)
                for n, (dst, value) in enumerate(((mhalf[:], -0.5), (kvw[0:KVL], 0.0), (wuqT[KVL:P], 0.0),
                                                  (v[:, :, :, :, HS:VW], 1.0),
                                                  (slots["q"][0][:].bitcast(F32), 0.0))):
                    pool.memset(dst, value).then_inc(consts, 1)
                    pool.wait_ge(consts, n + 1)
                deviation(0, 0)
                pool.memset(rows01[:, 0].bitcast(F32), 0.0).then_inc(rows_made, 1)
                pool.memset(rows01[:, 1].bitcast(F32), 1.0).then_inc(rows_made, 1)
                with pool.Fori(0, B - 1) as b:
                    for u in range(2):
                        pool.wait_ge(xn_done, b * 2 + u + 1)
                        load(b * 2 + u + 2, u)
                        deviation(b * 2 + u + 1, 1 - u)
                deviation(NC - 1, 1)

            @block.vector
            def _(dve):
                def moments(c, u, n):
                    dve.wait_ge(x_in[u], n * 16)
                    settle(dve, keep["passed"])
                    for t in range(TC):
                        dve.bn_stats(stats[:, u, t], x[:, u, t]).then_inc(stats_done, 1)
                    dve.wait_ge(stats_done, c * TC + TC)
                    settle(dve, keep["passed"])
                    for t in range(TC):
                        dve.bn_aggr(mv[:, u, t], stats[:, u, t]).then_inc(mv_done, 1)

                def normalise(c, u):
                    dve.wait_ge(rstd_done, c + 1)
                    if not (isinstance(c, int) and c < 2):
                        dve.wait_ge(xT_made, c - 1)
                    for t in range(TC):
                        ins = dve.tensor_scalar(xn[:, u, t], x[:, u, t], mv[:, u, t, 0:1], rstd[:, u, t:t + 1],
                                                ALU.subtract, ALU.mult)
                    ins.then_inc(xn_done, 1)

                dve.memset(slots["k"][0][:].bitcast(F32), 0.0).then_inc(slots["init"][0], 1)
                dve.nop().then_inc(lo_done, 4)
                moments(0, 0, 1)
                moments(1, 1, 1)
                normalise(0, 0)
                dve.wait_ge(a_made, 1)
                dve.tensor_copy(amat[:], psZ[0:KVL, 0:KVL]).then_inc(a_kept, 1)
                normalise(1, 1)
                dve.wait_ge(kv_made, 1)
                dve.tensor_copy(kvw[KVL:P], psQ[KVL:P, 0:2, 0:C]).then_inc(kv_kept, 1)

                def body(b):
                    for u in range(2):
                        c = b * 2 + u
                        if exists(c + 2):
                            moments(c + 2, u, b + 2)
                        dve.wait_ge(stored[u], b * PER + 1)
                        for m in range(4):
                            dve.wait_ge(hi_done, c * 4 + m + 1)
                            dve.tensor_tensor(lo[:, u, m], psQ[:, m], hi[:, u, m], ALU.subtract).then_inc(lo_done, 1)
                        if exists(c + 2):
                            normalise(c + 2, u)

                with dve.Fori(0, B - 1) as b:
                    body(b)
                body(B - 1)

            @block.scalar
            def _(act):
                act.nop().then_inc(z_kept, 1)
                act.nop().then_inc(v_kept, 2)
                for u in range(2):
                    act.nop().then_inc(stored[u], 1)

                def keep_xT(c, u):
                    act.wait_ge(xT_made, c + 1)
                    act.activation(xnT[:, u], psX[:], ACT.Copy).then_inc(xT_kept, 1)

                act.wait_ge(consts, 4)
                keep_xT(0, 0)

                def body(b):
                    for u in range(2):
                        c = b * 2 + u
                        act.wait_ge(z_made, c + 1)
                        act.activation(z[:, u], psZ[:], ACT.Copy).then_inc(z_kept, 1)
                        if exists(c + 1):
                            keep_xT(c + 1, 1 - u)
                        act.wait_ge(stored[u], b * PER + 1)
                        for m in range(4):
                            act.wait_ge(qk_made, c * 4 + m + 1)
                            act.activation(hi[:, u, m], psQ[:, m], ACT.Copy).then_inc(hi_done, 1)
                            if m % 2 == 1:
                                act.wait_ge(v_made, c * 2 + m // 2 + 1)
                                for t in range(m - 1, m + 1):
                                    act.activation(v[:, u, t, :, 0:HS], psV[:, t % 2].rearrange("p (h w) -> p h w", h=NH),
                                                   ACT.Copy).then_inc(v_kept, 1)

                with act.Fori(0, B - 1) as b:
                    body(b)
                body(B - 1)

            @block.tensor
            def _(pe):
                def turn(c, u):
                    pe.wait_ge(xn_done, c + 1)
                    if not (isinstance(c, int) and c == 0):
                        pe.wait_ge(xT_kept, c)
                    for t in range(TC):
                        for k in range(CT):
                            ins = pe.transpose(psX[:, k, t * P:(t + 1) * P], xn[:, u, t, k * P:(k + 1) * P], ident[:])
                    ins.then_inc(xT_made, 1)

                pe.wait_ge(w_in, 16 * 11)
                pe.wait_ge(consts, 4)
                for k in range(CT):
                    ins = pe.matmul(psZ[0:KVL, 0:KVL], wuq[:, k], wuk[:, k], start=(k == 0), stop=(k == CT - 1))
                ins.then_inc(a_made, 1)
                for k in range(CT):
                    pe.matmul(psQ[KVL:P, 1, 0:C], wuv[:, k], woT[:, k], start=(k == 0), stop=(k == CT - 1))
                pe.wait_ge(a_kept, 1)
                pe.matmul(psQ[KVL:P, 0, 0:C], amat[:], wdq[:], start=True, stop=True).then_inc(kv_made, 1)
                turn(0, 0)
                pe.wait_ge(kv_kept, 1)

                def body(b):
                    for u in range(2):
                        c = b * 2 + u
                        pe.wait_ge(xT_kept, c + 1)
                        pe.wait_ge(z_kept, c + 1)
                        for k in range(CT):
                            ins = pe.matmul(psZ[:], wz[:, k], xnT[:, u, k], start=(k == 0), stop=(k == CT - 1))
                        ins.then_inc(z_made, 1)
                        if exists(c + 1):
                            turn(c + 1, 1 - u)
                        pe.wait_ge(z_kept, c + 2)
                        for m in range(4):
                            pe.wait_ge(lo_done, c * 4 + m + 1)
                            w = wuqT[:, m * P:(m + 1) * P] if m < 2 else kvw[:, 0, (m - 2) * P:(m - 1) * P]
                            pe.matmul(psQ[:, m], w, z[:, u], start=True, stop=True).then_inc(qk_made, 1)
                            if m % 2 == 1:
                                pe.wait_ge(v_kept, c * 4 + (m - 1) + 2)
                                for t in range(m - 1, m + 1):
                                    ins = pe.matmul(psV[:, t % 2], z[:, u, t * P:(t + 1) * P], kvw[:, 1], start=True, stop=True)
                                ins.then_inc(v_made, 1)

                with pe.Fori(0, B - 1) as b:
                    body(b)
                body(B - 1)


BLOCKS = [(c, j) for c in range(NCH) for j in range((c + 1) * TC)]
STEPS = [(c, j, p) for c, j in BLOCKS for p in range(2)]
NB, NS = len(BLOCKS), len(STEPS)


def max_units():
    out = []
    for i in range(TB):
        keys = (i + 1) * P
        if 2 * keys <= CH:
            out += [(i, 0, (e, e + 2), 0, keys) for e in range(2)]
        else:
            out += [(i, k, (h,), k * CH, min(CH, keys - k * CH)) for k in range(-(-keys // CH)) for h in range(GH)]
    return out


UNITS = max_units()
NU = len(UNITS)
HALF = NU // 2
NBK = 3


def bank_jobs():
    work = [("unit", 1, m) for m in range(HALF, NU)] + [("unit", 2, m) for m in range(HALF)]
    cost = [len(UNITS[m][2]) * UNITS[m][4] + 64 for _, _, m in work]
    width = [CH - max(0, (j - c * TC) * P) + 96 for c, j, _ in STEPS]
    out, step, done = [[] for _ in STEPS], 0, 0
    for job, c in zip(work, cost):
        while step < NS - 1 and (done + c / 2) / sum(cost) > sum(width[:step + 1]) / sum(width):
            step += 1
        out[step].append(job)
        done += c
    out[4].insert(0, ("out", 0, 0))
    out[13].insert(0, ("out", 0, 1))
    out[15].insert(0, ("turn", 1, 0))
    out[17].insert(0, ("turn", 1, 1))
    return out


AFTER = bank_jobs()
JOBS = sum(len(x) for x in AFTER)
assert JOBS % NBK == 0 and NB % 3 == 0


def attend(nc, d, keep, slots):
    with ExitStack() as ctx:
        s = Store(nc, ctx, "att")
        ident, identb = keep["ident"], keep["identb"]
        y = keep["y"]
        for g in range(1, NSL):
            add_slot(slots, s, g)
        qg, kg, vg, loaded = slots["q"], slots["k"], slots["v"], slots["loaded"]
        pt = s.sb("pt", [P, 3, GH, CH])
        pm = s.sb("pm", [P, 2, TB, 2, GH])
        nh = s.sb("nh", [P, TB, GH, 2], F32R)
        mt = s.sb("mt", [2 * GH, T], F32R)
        ot = s.sb("ot", [P, CH])
        rec = s.sb("rec", [P, TC, GH])
        onesb = s.sb("onesb", [1, CH], BF16)
        zeros = s.sb("zeros", [P, C])

        ps_s = [s.ps(f"ps_s{i}", [P, 2, CH]) for i in range(2)]
        ps_m = [s.ps(f"ps_m{i}", [P, CH]) for i in range(NBK)]
        ps_o = s.ps("ps_o", [P, CH])

        m_in = [s.sem(f"m_in{g}") for g in range(NSL)]
        started, blank, blank_made = s.sem("started"), s.sem("blank"), s.sem("blank_made")
        st_made, ex_done, pv_done, ot_done, y_rec, y_done = (
            s.sem(n) for n in ("st_made", "ex_done", "pv_done", "ot_done", "y_rec", "y_done"))
        bank_made = [s.sem(f"bank_made{i}") for i in range(NBK)]
        bank_read = [s.sem(f"bank_read{i}") for i in range(NBK)]
        pm_done, nh_hi, nh_done, mtp_made, mt_done = (
            s.sem(n) for n in ("pm_done", "nh_hi", "nh_done", "mtp_made", "mt_done"))

        def at(b, g, per, more):
            return b * (NG * per) + (g * per + more)

        def ahead(b, g, n):
            return not isinstance(b, int) or b * NG + g + n < B * NG

        first = [("unit", 0, m) for m in range(NU)] + [("unit", 1, m) for m in range(HALF)]
        first[NU + 5:NU + 5] = [("turn", 0, 0), ("turn", 0, 1)]

        def numbered(b):
            out, n = [], len(first)
            for g in range(NG):
                steps = []
                for k in range(NS):
                    here = [j for j in AFTER[k] if ahead(b, g, j[1])]
                    steps.append([(j, n + i) for i, j in enumerate(here)])
                    n += len(here)
                out.append(steps)
            return out, n

        def turns(b, n):
            return b * (JOBS * NG // NBK) + n // NBK

        with nc.Block() as block:
            @block.sync
            def _(sp):
                def max_rows(b, g):
                    sp.wait_ge(mt_done, at(b, g, 1, 1))
                    slot = g % NSL
                    for h in range(GH):
                        r = 64 * (h % 2) + KR
                        sp.dma_start(qg[slot][r:r + 2, h // 2, :].bitcast(F32), mt[2 * h:2 * h + 2, :].bitcast(F32)
                                     ).then_inc(m_in[slot], 16)

                for g in range(1, NSL):
                    sp.wait_ge(slots["init"][g], 2)
                    load_ones(sp, d, slots, g)
                    if g < 3:
                        load_group(sp, d, slots, 0, g)
                max_rows(0, 0)

                def body(b):
                    for g in range(NG):
                        if ahead(b, g, 3):
                            sp.wait_ge(pv_done, at(b, g, NB, 3))
                            load_group(sp, d, slots, b, g + 3)
                        if ahead(b, g, 1):
                            max_rows(b, g + 1)

                with sp.Fori(0, B - 1) as b:
                    body(b)
                body(B - 1)

            @block.gpsimd
            def _(pool):
                pool.memset(onesb[:], 1.0).then_inc(started, 1)
                for g in range(1, NSL):
                    pool.memset(qg[g][:].bitcast(F32), 0.0).then_inc(slots["init"][g], 1)
                    pool.memset(kg[g][:].bitcast(F32), 0.0).then_inc(slots["init"][g], 1)
                pool.memset(zeros[:], 0.0).then_inc(blank_made, 1)
                pool.wait_ge(blank_made, 1)
                parts = NT * XT // (8 * P)
                assert parts + B <= B * NG
                for n in range(parts):
                    pool.wait_ge(pv_done, 3 + 2 + NB * n)
                    pool.dma_start(d["ys"][n * 8 * P:(n + 1) * 8 * P, :].rearrange("(p k) c -> p k c", p=P),
                                   zeros[:].unsqueeze(1).to_broadcast([P, 8, C])).then_inc(blank, 16)
                for b in range(B):
                    pool.wait_ge(pv_done, 3 + 2 + NB * (parts + b))
                    pool.dma_start(keep["xf"][:, b * TB:(b + 1) * TB],
                                   d["x"][b * T:(b + 1) * T, :].rearrange("(k p) c -> p k c", p=P)).then_inc(blank, 16)
                pool.wait_ge(blank, 16 * (parts + B))

            @block.tensor
            def _(pe):
                pe.nop().then_inc(pv_done, 3)
                pe.wait_ge(started, 1)
                pe.matmul(ps_o[:], onesb[:, 0:P], onesb[:], start=True, stop=True)

                def unit(b, g, m, out):
                    i, piece, heads, k0, keys = UNITS[m]
                    slot = g % NSL
                    if m == 0:
                        pe.wait_ge(loaded[slot], at(b, g // NSL * NSL, LOADS, NSL * LOADS + ONES))
                    for n, h in enumerate(heads):
                        diag = k0 + keys == (i + 1) * P
                        ins = pe.matmul(out[:, n * keys:(n + 1) * keys], qg[slot][:, h // 2, i * P:(i + 1) * P],
                                        kg[slot][:, h, k0:k0 + keys], start=True, stop=not diag)
                        if diag:
                            ins = pe.matmul(out[:, (n + 1) * keys - P:(n + 1) * keys], identb[:], keep["mask_ts"][:],
                                            start=False, stop=True)
                    return ins

                def max_turn(b, g, half, out):
                    pe.wait_ge(nh_done, at(b, g, 1, 1))
                    for i in range(TC):
                        ins = pe.transpose(out[0:2 * GH, i * P:(i + 1) * P], nh[:, half * TC + i].rearrange("p h k -> p (h k)").bitcast(F32), ident[:])
                    return ins

                def turn_out(b, g, c, out):
                    pe.wait_ge(ot_done, at(b, g, 2, c + 1))
                    for t in range(TC):
                        ins = pe.transpose(out[:, t * P:(t + 1) * P], ot[:, t * P:(t + 1) * P], ident[:])
                    return ins

                def job(b, g, what, n):
                    kind, more, m = what
                    bank = n % NBK
                    if not (isinstance(b, int) and n < NBK):
                        pe.wait_ge(bank_read[bank], turns(b, n))
                    do = {"unit": unit, "turn": max_turn, "out": turn_out}[kind]
                    do(b, g + more, m, ps_m[bank]).then_inc(bank_made[bank], 1)

                def scores(b, g, k):
                    c, j, p = STEPS[k]
                    slot, out = g % NSL, ps_s[k % 2]
                    if k == 0:
                        pe.wait_ge(m_in[slot], at(b, g // NSL * NSL, 16, 64))
                    pe.wait_ge(ex_done, at(b, g, NS, k + 1))
                    off = max(0, (j - c * TC) * P)
                    diag = j >= c * TC
                    for e in range(2):
                        ins = pe.matmul(out[:, e, off:CH], kg[slot][:, 2 * p + e, j * P:(j + 1) * P],
                                        qg[slot][:, p, c * CH + off:(c + 1) * CH], start=True, stop=not diag)
                    if diag:
                        for e in range(2):
                            ins = pe.matmul(out[:, e, off:off + P], identb[:], keep["mask_st"][:], start=False, stop=True)
                    ins.then_inc(st_made, 1)

                def values(b, g, blk):
                    c, j = BLOCKS[blk]
                    slot = g % NSL
                    pe.wait_ge(ex_done, at(b, g, NS, 2 * blk + 2 + 2))
                    if j == 0:
                        pe.wait_ge(ot_done, at(b, g, 2, 1 + c))
                    off = max(0, (j - c * TC) * P)
                    for h in range(GH):
                        ins = pe.matmul(ps_o[32 * h:32 * h + VW, off:CH], vg[slot][:, j, h * VW:(h + 1) * VW],
                                        pt[:, blk % 3, h, off:CH], start=(j == 0), stop=(j == (c + 1) * TC - 1))
                    ins.then_inc(pv_done, 1)

                for n, what in enumerate(first):
                    job(0, 0, what, n)

                def body(b):
                    for g, steps in enumerate(numbered(b)[0]):
                        for k in range(NS):
                            scores(b, g, k)
                            jobs = list(steps[k])
                            if jobs:
                                job(b, g, *jobs.pop(0))
                            if k % 2 == 1 and k >= 3:
                                values(b, g, k // 2 - 1)
                            for what, n in jobs:
                                job(b, g, what, n)
                        values(b, g, NB - 1)

                with pe.Fori(0, B - 1) as b:
                    body(b)
                body(B - 1)
                job(B - 1, NG, ("out", 0, 0), numbered(B - 1)[1])

            @block.scalar
            def _(act):
                act.nop().then_inc(ex_done, 2)

                def fill_mt(b, g, half, n, at_b):
                    act.wait_ge(bank_made[n % NBK], turns(at_b, n) + 1)
                    if half == 0 and not (isinstance(b, int) and b * NG + g == 0):
                        act.wait_ge(m_in[(g - 1) % NSL], at(b, (g - 1) // NSL * NSL, 16, 64))
                    act.activation(mt[:, half * CH:(half + 1) * CH], ps_m[n % NBK][0:2 * GH, :], ACT.Copy
                                   ).then_inc(bank_read[n % NBK], 1)
                    if half == 1:
                        act.wait_ge(bank_read[n % NBK], turns(at_b, n) + 1)
                        act.wait_ge(bank_read[(n - 1) % NBK], turns(at_b, n - 1) + 1)
                        act.nop().then_inc(mt_done, 1)

                def keep_out(b, g, c):
                    act.wait_ge(pv_done, at(b, g, NB, 3 + TC * c))
                    act.wait_ge(y_done, at(b, g, 2, c + 1))
                    act.activation(ot[:], ps_o[:], ACT.Copy).then_inc(ot_done, 1)

                for n, (kind, _, half) in enumerate(first):
                    if kind == "turn":
                        fill_mt(0, 0, half, n, 0)

                def body(b):
                    for g, steps in enumerate(numbered(b)[0]):
                        for k, (c, j, p) in enumerate(STEPS):
                            blk = k // 2
                            act.wait_ge(st_made, at(b, g, NS, k + 1))
                            act.wait_ge(pv_done, at(b, g, NB, blk + 1))
                            off = max(0, (j - c * TC) * P)
                            act.activation(pt[:, blk % 3, 2 * p:2 * p + 2, off:CH], ps_s[k % 2][:, :, off:CH],
                                           ACT.Exp, scale=HS ** -0.5).then_inc(ex_done, 1)
                            if k == 0:
                                keep_out(b, g, 0)
                            if k == 9:
                                keep_out(b, g, 1)
                            for what, n in steps[k]:
                                if what[0] == "turn":
                                    fill_mt(b, g + 1, what[2], n, b)

                with act.Fori(0, B - 1) as b:
                    body(b)
                body(B - 1)
                keep_out(B, 0, 0)

            @block.vector
            def _(dve):
                dve.nop().then_inc(y_done, 1)

                def unit(b, g, m, src):
                    i, piece, heads, k0, keys = UNITS[m]
                    src = src[:, 0:len(heads) * keys]
                    h = heads[0]
                    if len(heads) > 1:
                        return dve.tensor_reduce(pm[:, g % 2, i, piece, h:h + 3:2],
                                                 src.rearrange("p (h k) -> p h k", k=keys), AX.X, ALU.max)
                    return dve.tensor_reduce(pm[:, g % 2, i, piece, h:h + 1], src, AX.X, ALU.max)

                def negate(b, g, n, at_b, stage):
                    q = pm[:, g % 2]
                    if stage == 0:
                        for i in range(n - NBK, n):
                            dve.wait_ge(bank_read[i % NBK], turns(at_b, i) + 1)
                        dve.tensor_tensor(q[:, TC:TB, 0], q[:, TC:TB, 0], q[:, TC:TB, 1], ALU.max).then_inc(pm_done, 1)
                    elif stage == 1:
                        dve.wait_ge(pm_done, at(b, g, 1, 1))
                        if not (isinstance(b, int) and b * NG + g == 0):
                            dve.wait_ge(mt_done, at(b, g, 1, 0))
                        dve.tensor_scalar(nh[:, :, :, 0], q[:, :, 0], -1.0, None, ALU.mult).then_inc(nh_hi, 1)
                    else:
                        dve.wait_ge(nh_hi, at(b, g, 1, 1))
                        dve.scalar_tensor_tensor(nh[:, :, :, 1], q[:, :, 0], -1.0, nh[:, :, :, 0],
                                                 ALU.mult, ALU.subtract).then_inc(nh_done, 1)

                def normalise(b, g, c, src, release, released):
                    o = src[:].rearrange("p (t h w) -> p t h w", t=TC, h=GH)
                    dve.reciprocal(rec[:], o[:, :, :, HS]).then_inc(y_rec, 1)
                    dve.wait_ge(y_rec, at(b, g, 2, c + 1))
                    place = b * NG + (g + c)
                    half = 1 - c
                    dst = y[:, bass.ds(place, 1), half * TC:(half + 1) * TC, :].rearrange("p o t (h w) -> p (o t) h w", h=GH)
                    dve.tensor_tensor(dst, o[:, :, :, 0:HS], rec[:].unsqueeze(3).to_broadcast([P, TC, GH, HS]), ALU.mult
                                      ).then_inc(release, 1)
                    dve.wait_ge(release, released)
                    dve.nop().then_inc(y_done, 1)

                def job(b, g, what, n):
                    kind, more, m = what
                    bank = n % NBK
                    if kind == "turn":
                        return
                    dve.wait_ge(bank_made[bank], turns(b, n) + 1)
                    if kind == "unit":
                        unit(b, g + more, m, ps_m[bank]).then_inc(bank_read[bank], 1)
                        if m < 3 and not (isinstance(b, int) and b * NG + g + more == 0):
                            negate(b, g + more - 1, n, b, m)
                        if m == NU - 1 and not ahead(b, g + more, 1):
                            for stage in range(3):
                                negate(b, g + more, n + 1, b, stage)
                    else:
                        normalise(b, g, m, ps_m[bank], bank_read[bank], turns(b, n) + 1)

                for n, what in enumerate(first):
                    job(0, 0, what, n)

                def body(b):
                    for g, steps in enumerate(numbered(b)[0]):
                        for k in range(NS):
                            for what, n in steps[k]:
                                job(b, g, what, n)

                with dve.Fori(0, B - 1) as b:
                    body(b)
                body(B - 1)
                job(B - 1, NG, ("out", 0, 0), numbered(B - 1)[1])


E, K, F = 8, 2, 1024
FT = F // P
XT = 256
NT = K * N // XT + E
CAP = N + XT
MOE_EPS = 1e-6
TILES = N // P


def route(nc, d, keep):
    with ExitStack() as ctx:
        s = Store(nc, ctx, "route")
        ident = keep["ident"]
        y, xf = keep["y"], keep["xf"]
        wgt, slot, base = keep["wgt"], keep["slot"], keep["base"]
        gb = keep["gb"]
        raw1, raw2, w1, w2 = keep["raw1"], keep["raw2"], keep["w1_0"], keep["w2_0"]
        xh = s.sb("xh", [P, TILES, C])
        yn = s.sb("yn", [P, TB, C])
        xb = s.sb("xb", [P, TB, C])
        stats = s.sb("stats", [P, 3, TB, 6])
        mv = s.sb("mv", [P, 3, TB, 2])
        veps = s.sb("veps", [P, 3, TB])
        rstd = s.sb("rstd", [P, 3, TB])
        nmean = s.sb("nmean", [P, 3, TB])
        shift = s.sb("shift", [P, 3, TB])
        mhalf = s.sb("mhalf", [P, TB])
        xfT = s.sb("xfT", [P, 2, CT, P])
        wg = s.sb("wg", [P, CT, E])
        before = s.sb("before", [P, P], BF16)
        ones = s.sb("ones", [P, TILES])
        ones_sq = s.sb("ones_sq", [P, P], BF16)
        ei = s.sb("ei", [P, E])
        ti = s.sb("ti", [E, NT + 2])
        gam = s.sb("gam", [E, 2, C])
        etile = s.sb("etile", [E, 1])
        best = s.sb("best", [P, TB, 8])
        order = s.sb("order", [P, TB, 8], mybir.dt.uint32)
        which = s.sb("which", [P, K, TB])
        pick = s.sb("pick", [P, K, TB, E])
        taken = s.sb("taken", [P, TB, E], BF16)
        part = s.sb("part", [P, E])
        total = s.sb("total", [P, E], BF16)
        assert TILES <= 256
        efirst = s.sb("efirst", [P, E])
        place = s.sb("place", [P, TB, E])
        pad_f = s.sb("pad_f", [P, E])
        pad = s.sb("pad", [P, E], mybir.dt.int32)
        zeros = s.sb("zeros", [P, C])
        pick_all = s.sb("pick_all", [P, K, TILES, E])
        slot_all = s.sb("slot_all", [P, K, TILES])
        hit_all = s.sb("hit_all", [P, K, TILES, E])
        moved = s.sb("moved", [P, K, TILES])
        apart = s.sb("apart", [P, E])
        tiles_i = s.sb("tiles_i", [P, E], mybir.dt.int32)
        tiles_f = s.sb("tiles_f", [P, E])
        base_f = s.sb("base_f", [P, E + 1])
        hit = s.sb("hit", [P, K, TB, E])
        slot_f = s.sb("slot_f", [P, K, TB])
        de = s.sb("de", [P, TILES])
        edge = s.sb("edge", [E, 2, E])
        edges = s.sb("edges", [E, 2])
        own = s.sb("own", [E, 2, NT + 2])
        shift_e = s.sb("shift_e", [E, 1])
        row_e = s.sb("row_e", [E, NT + 2], BF16)
        assert E * CAP // XT <= 256

        ps_x = [s.ps(f"ps_x{i}", [P, CT, P]) for i in range(2)]
        ps_g = s.ps("ps_g", [P, TB, E])
        ps_r = s.ps("ps_r", [P, TB, E])
        ps_n = s.ps("ps_n", [P, E])
        ps_t = s.ps("ps_t", [1, NT + 2])
        ps_b = s.ps("ps_b", [P, 2, CT, NT + 2])

        c_in, consts = s.sem("c_in"), s.sem("consts")
        stat, aggr, rs, step = s.sem("stat"), s.sem("aggr"), s.sem("rs"), s.sem("step")
        ve_done, yn_done, x1_done, xf_done, xh_done = (
            s.sem(n) for n in ("ve_done", "yn_done", "x1_done", "xf_done", "xh_done"))
        turned, turn_kept, gated, ranked, weights_in, slots_in, gb_made = (
            s.sem(n) for n in ("turned", "turn_kept", "gated", "ranked", "weights_in", "slots_in", "gb_made"))
        exp_done, scattered, picked, owned, xf_kept, root_done = (
            s.sem(n) for n in ("exp_done", "scattered", "picked", "owned", "xf_kept", "root_done"))
        w0_in, w0_hi, w0_lo = s.sem("w0_in"), s.sem("w0_hi"), s.sem("w0_lo")
        counting, counted, pad_known, padded, rows_known = (
            s.sem(n) for n in ("counting", "counted", "pad_known", "padded", "rows_known"))

        def tile(buf, b, t):
            return buf[:, bass.ds(b * TB + t, 1), :].rearrange("p o c -> p (o c)")

        def head_tile(b, t):
            return y[:, bass.ds(b * NG + 1, NG), t, :]

        def by_group(buf, t):
            return buf[:, t].rearrange("p (g w) -> p g w", g=NG)

        with nc.Block() as block:
            @block.sync
            def _(sp):
                for dst, src in ((wg[:], d["wg"].rearrange("(k p) e -> p k e", p=P)), (before[:], d["before"]),
                                 (ei[:], d["ei"]), (ti[:], d["ti"]), (gam[:, 0], d["gamma"]), (gam[:, 1], d["beta"]),
                                 (etile[:], d["etile"])):
                    sp.dma_start(dst, src).then_inc(c_in, 16)
                sp.dma_start(raw1[:], d["w1"][0].rearrange("(k p) f -> p k f", p=P)).then_inc(w0_in, 16)
                sp.dma_start(raw2[:], d["w2"][0].rearrange("(k p) c -> p k c", p=P)).then_inc(w0_in, 16)
                sp.wait_ge(consts, 4)
                sp.wait_ge(pad_known, 1)
                settle(sp, keep["passed"])
                for e in range(E):
                    row = sp.value_load(pad[0:1, e:e + 1], min_val=e * CAP, max_val=e * CAP + N)
                    sp.dma_start(d["xs"][bass.ds(row, XT), :].rearrange("(k p) c -> p k c", p=P),
                                 zeros[:].unsqueeze(1).to_broadcast([P, XT // P, C])).then_inc(padded, 16)
                sp.wait_ge(padded, 16 * E)

            @block.gpsimd
            def _(pool):
                pool.memset(mhalf[:], -0.5).then_inc(consts, 1)
                pool.memset(ones[:], 1.0).then_inc(consts, 1)
                pool.memset(ones_sq[:], 1.0).then_inc(consts, 1)
                pool.memset(zeros[:], 0.0).then_inc(consts, 1)
                pool.wait_ge(consts, 4)

                def roots(n, call):
                    pool.wait_ge(aggr, call * TB + TB)
                    settle(pool, keep["passed"])
                    pool.tensor_scalar(veps[:, n], mv[:, n, :, 1], MOE_EPS if n == 2 else LN_EPS, None, ALU.add
                                       ).then_inc(ve_done, 1)
                    pool.tensor_scalar(nmean[:, n], mv[:, n, :, 0], -1.0, None, ALU.mult).then_inc(ve_done, 1)
                    pool.wait_ge(ve_done, call * 2 + 2)
                    pool.tensor_tensor(rstd[:, n], veps[:, n], mhalf[:], ALU.pow).then_inc(root_done, 1)
                    pool.wait_ge(root_done, call + 1)
                    pool.tensor_tensor(shift[:, n], nmean[:, n], rstd[:, n], ALU.mult).then_inc(rs, 1)

                def scatter(b, first, last):
                    pool.wait_ge(slots_in, b + 1)
                    pool.wait_ge(xh_done, b + 1)
                    for n in range(first, last):
                        t, k = b * TB + n // K, n % K
                        pool.indirect_dma_start(d["xs"], bass.IndirectOffsetOnAxis(ap=slot[:, k, t:t + 1], axis=0),
                                                xh[:, t, :], None).then_inc(scattered, 16)

                roots(0, 0)
                roots(1, 1)
                cuts = (0, 5, 10, K * TB)
                for b in range(-1, B - 1):
                    for n, (norm, ahead) in enumerate(((0, 2), (2, 1), (1, 2))):
                        if b + ahead < B:
                            roots(norm, 3 * (b + 1) + 2 + n if b + 2 < B else 3 * B - 1)
                        if b >= 0:
                            scatter(b, cuts[n], cuts[n + 1])
                scatter(B - 1, 0, K * TB)
                pool.wait_ge(scattered, 16 * K * TILES)

            @block.vector
            def _(dve):
                dve.wait_ge(consts, 3)

                def moments(n, src, call):
                    settle(dve, keep["passed"])
                    for t in range(TB):
                        dve.bn_stats(stats[:, n, t], src(t)).then_inc(stat, 1)
                    dve.wait_ge(stat, call * TB + TB)
                    settle(dve, keep["passed"])
                    for t in range(TB):
                        dve.bn_aggr(mv[:, n, t], stats[:, n, t]).then_inc(aggr, 1)

                def residual(b):
                    for t in range(TB):
                        dve.wait_ge(yn_done, b * TB + t + 1)
                        dve.tensor_tensor(head_tile(b, t), tile(xf, b, t).rearrange("p (g w) -> p g w", g=NG),
                                          by_group(yn, t), ALU.add).then_inc(x1_done, 1)
                    dve.wait_ge(x1_done, b * TB + TB)

                def normalise(b, call):
                    dve.wait_ge(rs, call + 1)
                    dve.wait_ge(xf_kept, b + 1)
                    for t in range(TB):
                        dve.tensor_scalar(by_group(xb, t), head_tile(b, t), mv[:, 1, t, 0:1], rstd[:, 1, t:t + 1],
                                          ALU.subtract, ALU.mult).then_inc(xf_done, 1)
                    dve.wait_ge(xf_done, b * TB + TB)

                STEPS_B = 10

                def pick_experts(b):
                    n = 0

                    def then(ins):
                        nonlocal n
                        n += 1
                        ins.then_inc(step, 1)
                        dve.wait_ge(step, b * STEPS_B + (n + START))

                    dve.wait_ge(gated, b * TB + TB + 2)
                    settle(dve, keep["passed"])
                    for t in range(TB):
                        ins = dve.max(best[:, t], ps_g[:, t])
                    then(ins)
                    settle(dve, keep["passed"])
                    for t in range(TB):
                        ins = dve.max_index(order[:, t], best[:, t], ps_g[:, t])
                    then(ins)
                    dve.tensor_tensor(de[:, bass.ds(b * TB, TB)], best[:, :, 1], best[:, :, 0], ALU.subtract)
                    then(dve.tensor_copy(which[:], order[:, :, 0:K].rearrange("p t k -> p k t")))
                    for k in range(K):
                        ins = dve.tensor_tensor(pick[:, k], ei[:].unsqueeze(1).to_broadcast([P, TB, E]),
                                                which[:, k].unsqueeze(2).to_broadcast([P, TB, E]), ALU.is_equal)
                    then(ins)
                    then(dve.tensor_tensor(taken[:], pick[:, 0], pick[:, 1], ALU.add))
                    dve.nop().then_inc(picked, 1)
                    dve.wait_ge(ranked, b + 1)
                    then(dve.tensor_tensor(place[:], ps_r[:], efirst[:].unsqueeze(1).to_broadcast([P, TB, E]), ALU.add))
                    for k in range(K):
                        ins = dve.tensor_tensor(hit[:, k], pick[:, k], place[:], ALU.mult)
                    then(ins)
                    then(dve.tensor_reduce(slot_f[:], hit[:], AX.X, ALU.add))
                    dve.tensor_copy(slot[:, :, bass.ds(b * TB, TB)], slot_f[:]).then_inc(slots_in, 1)
                    dve.tensor_copy(slot_all[:, :, bass.ds(b * TB, TB)], slot_f[:])
                    for k in range(K):
                        dve.tensor_copy(pick_all[:, k, bass.ds(b * TB, TB), :], pick[:, k])
                    then(dve.tensor_reduce(part[:], taken[:].rearrange("p t e -> p e t"), AX.X, ALU.add))
                    then(dve.tensor_tensor(total[:], total[:], part[:], ALU.add))
                    assert n == STEPS_B
                    dve.nop().then_inc(counting, 1)

                START = 2
                moments(0, lambda t: head_tile(0, t), 0)
                residual(0)
                moments(1, lambda t: head_tile(0, t), 1)

                def body(b):
                    moments(0, lambda t: head_tile(b + 1, t), b * 3 + 2)
                    if not isinstance(b, int):
                        pick_experts(b - 1)
                    normalise(b, b * 3 + 1)
                    moments(2, lambda t: xb[:, t], b * 3 + 3)
                    residual(b + 1)
                    moments(1, lambda t: head_tile(b + 1, t), b * 3 + 4)

                body(0)
                dve.wait_ge(c_in, 16 * 7)
                dve.memset(total[:], 0.0).then_inc(step, 1)
                dve.tensor_scalar(efirst[:], ei[:], float(CAP), None, ALU.mult).then_inc(step, 1)
                dve.wait_ge(step, START)
                with dve.Fori(1, B - 1) as b:
                    body(b)
                pick_experts(B - 2)
                normalise(B - 1, 3 * B - 2)
                moments(2, lambda t: xb[:, t], 3 * B - 1)
                pick_experts(B - 1)

                n = START + STEPS_B * B

                def then(ins):
                    nonlocal n
                    n += 1
                    ins.then_inc(step, 1)
                    dve.wait_ge(step, n)

                dve.wait_ge(counted, 1)
                then(dve.tensor_tensor(pad_f[:], ps_n[:], efirst[:], ALU.add))
                then(dve.tensor_copy(pad[:], pad_f[:]))
                dve.nop().then_inc(pad_known, 1)
                dve.nop().then_inc(weights_in, 1)
                dve.wait_ge(exp_done, 1)
                then(dve.tensor_scalar(de[:], wgt[:, 1], 1.0, None, ALU.add))
                then(dve.reciprocal(wgt[:, 0], de[:]))
                then(dve.tensor_tensor(wgt[:, 1], wgt[:, 1], wgt[:, 0], ALU.mult))
                then(dve.tensor_tensor(wgt[:, 2], wgt[:, 1], wgt[:, 0], ALU.add))
                then(dve.tensor_scalar(tiles_f[:], ps_n[:], float(XT - 1), float(XT), ALU.add, ALU.max))
                then(dve.tensor_copy(tiles_i[:], tiles_f[:]))
                then(dve.tensor_scalar(tiles_i[:], tiles_i[:], XT.bit_length() - 1, None, ALU.logical_shift_right))
                then(dve.tensor_copy(tiles_f[:], tiles_i[:]))
                then(dve.memset(base_f[:, 0:1], 0.0))
                then(dve.tensor_tensor_scan(base_f[:, 1:E + 1], ones[:, 0:E], tiles_f[:], 0.0, ALU.mult, ALU.add))
                then(dve.tensor_copy(base[:], base_f[:]))
                then(dve.scalar_tensor_tensor(apart[:], base_f[:, 0:E], float(XT), efirst[:], ALU.mult, ALU.subtract))
                for k in range(K):
                    ins = dve.tensor_tensor(hit_all[:, k], pick_all[:, k], apart[:].unsqueeze(1).to_broadcast([P, TILES, E]),
                                            ALU.mult)
                then(ins)
                then(dve.tensor_reduce(moved[:], hit_all[:], AX.X, ALU.add))
                then(dve.tensor_tensor(moved[:], moved[:], slot_all[:], ALU.add))
                then(dve.tensor_copy(keep["out_slot"][:], moved[:]))
                for k in range(2):
                    ins = dve.tensor_tensor(edge[:, k], ident[0:E, 0:E], base_f[0:E, k:k + E], ALU.mult)
                then(ins)
                then(dve.tensor_reduce(edges[:], edge[:], AX.X, ALU.add))
                dve.tensor_scalar(own[:, 0], ti[:], edges[:, 0:1], None, ALU.is_ge)
                then(dve.tensor_scalar(own[:, 1], ti[:], edges[:, 1:2], None, ALU.is_lt))
                dve.tensor_tensor(own[:, 0], own[:, 0], own[:, 1], ALU.mult).then_inc(owned, 1)
                dve.wait_ge(owned, 1)
                then(dve.tensor_tensor(shift_e[:], etile[:], edges[:, 0:1], ALU.subtract))
                then(dve.tensor_scalar(own[:, 1], ti[:], shift_e[:, 0:1], None, ALU.add))
                then(dve.tensor_tensor(row_e[:], own[:, 1], own[:, 0], ALU.mult))
                dve.nop().then_inc(rows_known, 1)
                dve.wait_ge(gb_made, 2)
                then(dve.tensor_copy(gb[:], ps_b[:]))
                then(dve.tensor_copy(keep["tile_row"][:], ps_t[:]))
                dve.wait_ge(w0_hi, 2)
                dve.tensor_tensor(w1[1][:], raw1[:], w1[0][:], ALU.subtract).then_inc(w0_lo, 1)
                dve.tensor_tensor(w2[1][:], raw2[:], w2[0][:], ALU.subtract).then_inc(w0_lo, 1)
                dve.wait_ge(w0_lo, 2)

            @block.scalar
            def _(act):
                act.nop().then_inc(turn_kept, 2)
                act.nop().then_inc(xf_kept, 1)

                def norm_y(b, call):
                    act.wait_ge(rs, call + 1)
                    settle(act, keep["passed"])
                    for t in range(TB):
                        act.activation(by_group(yn, t), head_tile(b, t), ACT.Identity, scale=rstd[:, 0, t:t + 1],
                                       bias=shift[:, 0, t:t + 1]).then_inc(yn_done, 1)

                def keep_batch(b, call):
                    for t in range(TB):
                        act.wait_ge(turned, b * TB + t + 1)
                        act.wait_ge(gated, b * TB + t + 1)
                        act.activation(xfT[:, t % 2], ps_x[t % 2][:], ACT.Copy).then_inc(turn_kept, 1)
                    act.wait_ge(rs, call + 1)
                    settle(act, keep["passed"])
                    for t in range(TB):
                        ins = act.activation(tile(xh, b, t), xb[:, t], ACT.Identity, scale=rstd[:, 2, t:t + 1],
                                             bias=shift[:, 2, t:t + 1])
                    ins.then_inc(xh_done, 1)
                    act.wait_ge(xh_done, b + 1)
                    act.activation(xf[:, bass.ds(b * TB, TB), :], xb[:], ACT.Copy).then_inc(xf_kept, 1)

                norm_y(0, 0)
                with act.Fori(0, B - 1) as b:
                    act.wait_ge(x1_done, b * TB + TB)
                    norm_y(b + 1, b * 3 + 2)
                    keep_batch(b, b * 3 + 3)
                keep_batch(B - 1, 3 * B - 1)
                act.wait_ge(weights_in, 1)
                act.activation(wgt[:, 1], de[:], ACT.Exp).then_inc(exp_done, 1)
                act.wait_ge(w0_in, 32)
                act.activation(w1[0][:], raw1[:], ACT.Copy).then_inc(w0_hi, 1)
                act.activation(w2[0][:], raw2[:], ACT.Copy).then_inc(w0_hi, 1)

            @block.tensor
            def _(pe):
                pe.wait_ge(c_in, 16 * 7)
                pe.nop().then_inc(gated, 2)
                with pe.Fori(0, B) as b:
                    for t in range(TB + 1):
                        if t < TB:
                            pe.wait_ge(xf_done, b * TB + t + 1)
                            pe.wait_ge(turn_kept, b * TB + t + 1)
                            for k in range(CT):
                                ins = pe.transpose(ps_x[t % 2][:, k], xb[:, t, k * P:(k + 1) * P], ident[:])
                            ins.then_inc(turned, 1)
                        if t > 0:
                            pe.wait_ge(turn_kept, b * TB + (t - 1) + 1 + 2)
                            for k in range(CT):
                                ins = pe.matmul(ps_g[:, t - 1], xfT[:, (t - 1) % 2, k], wg[:, k], start=(k == 0), stop=(k == CT - 1))
                            ins.then_inc(gated, 1)
                    pe.wait_ge(picked, b + 1)
                    pe.matmul(ps_r[:].rearrange("p t e -> p (t e)"), before[:], taken[:].rearrange("p t e -> p (t e)"),
                              start=True, stop=False)
                    for t in range(TB - 1):
                        pe.matmul(ps_r[:, t + 1:TB], ones_sq[:], taken[:, t:t + 1].to_broadcast([P, TB - 1 - t, E]),
                                  start=False, stop=False)
                    pe.matmul(ps_r[:], ones_sq[:], total[:].unsqueeze(1).to_broadcast([P, TB, E]), start=False, stop=True
                              ).then_inc(ranked, 1)
                pe.wait_ge(counting, B)
                pe.matmul(ps_n[:], ones_sq[:], total[:], start=True, stop=True).then_inc(counted, 1)
                pe.wait_ge(owned, 1)
                for n in range(2):
                    for k in range(CT):
                        ins = pe.matmul(ps_b[:, n, k], gam[:, n, k * P:(k + 1) * P], own[:, 0], start=True, stop=True)
                ins.then_inc(gb_made, 1)
                pe.wait_ge(rows_known, 1)
                pe.matmul(ps_t[:], ones_sq[0:E, 0:1], row_e[:], start=True, stop=True).then_inc(gb_made, 1)


def experts(nc, d, keep):
    with ExitStack() as ctx:
        s = Store(nc, ctx, "moe")
        ident, base, gb = keep["ident"], keep["base"], keep["gb"]
        raw1, raw2 = keep["raw1"], keep["raw2"]
        w1 = [keep["w1_0"], [s.sb(f"w1{p}", [P, CT, F], F32R) for p in "hl"]]
        w2 = [keep["w2_0"], [s.sb(f"w2{p}", [P, FT, C], F32R) for p in "hl"]]
        b1 = [s.sb(f"b1{r}", [P, FT]) for r in range(2)]
        b2 = [s.sb(f"b2{r}", [P, C]) for r in range(2)]
        rows = s.sb("rows", [P, 2, C])
        xg = s.sb("xg", [P, CT, XT])
        xT = [s.sb(f"xT{p}", [P, CT, XT], F32R) for p in "hl"]
        hf = s.sb("hf", [P, 4, XT])
        hT = [s.sb(f"hT{p}", [P, FT, XT], F32R) for p in "hl"]
        o = s.sb("o", [P, 2, C])

        ps_x = s.ps("ps_x", [P, CT, XT])
        ps_h = [s.ps(f"ps_h{i}", [P, XT]) for i in range(4)]
        ps_o = [s.ps(f"ps_o{i}", [P, C]) for i in range(2)]
        NHB = len(ps_h)

        raw_in, raw_used, w_made, w_used = s.sem("raw_in"), s.sem("raw_used"), s.sem("w_made"), s.sem("w_used")
        b_in = [s.sem(f"b_in{r}") for r in range(2)]
        rows_in, turned, xg_done, xh_done, xl_done, h_made, hf_done, hh_done, hl_done, up_done, out_made, o_done, stored = (
            s.sem(n) for n in ("rows_in", "turned", "xg_done", "xh_done", "xl_done", "h_made", "hf_done", "hh_done", "hl_done",
                               "up_done", "out_made", "o_done", "stored"))
        bv, b_used = s.sem("bv"), s.sem("b_used")
        pieces = ((0, 0), (0, 1), (1, 0))

        def each(eng, expert, tile, late=None):
            with eng.Fori(0, E // 2) as q:
                bounds = [eng.value_load(base[0:1, bass.ds(q * 2 + r, 1)], min_val=min(r, 1), max_val=NT - 1 if r == 0 else NT)
                          for r in range(3)]
                for r in range(2):
                    expert(q, r)
                    with eng.Fori(bounds[r], bounds[r + 1]) as i:
                        tile(r, i)
                    if late:
                        late(bounds[r + 1])

        with nc.Block() as block:
            @block.sync
            def _(sp):
                def tile_slots(i):
                    place = sp.value_load(keep["tile_row"][0:1, bass.ds(i, 1)], min_val=0, max_val=E * CAP // XT - 1)
                    return d["xs"][bass.ds(place * XT, XT), :].rearrange("(k p) c -> p k c", p=P)

                def fetch(slots):
                    sp.dma_start(rows[:], slots).then_inc(rows_in, 16)

                fetch(d["xs"][0:XT, :].rearrange("(k p) c -> p k c", p=P))
                second = tile_slots(1)
                sp.wait_ge(turned, 1)
                fetch(second)
                sp.nop().then_inc(stored, 1)

                def tile(r, i):
                    ahead = tile_slots(i + 2)
                    sp.wait_ge(turned, i + 2)
                    fetch(ahead)
                    sp.wait_ge(o_done, i * 2 + 4)
                    sp.dma_start(d["ys"][bass.ds(i * XT, XT), :].rearrange("(k p) c -> p k c", p=P), o[:]
                                 ).then_inc(stored, 16)

                each(sp, lambda q, r: None, tile)
                total = sp.value_load(base[0:1, E:E + 1], min_val=1, max_val=NT)
                sp.wait_ge(stored, total * 16 + 1)
                settle(sp, keep["passed"])
                sp.wait_ge(rows_in, total * 16 + 32)
                settle(sp, keep["passed"])

            @block.gpsimd
            def _(pool):
                def biases(q, r):
                    pool.dma_start(b1[r][:], d["b1"][:, bass.ds(q * 2 + r, 1), :].rearrange("p o f -> p (o f)")
                                   ).then_inc(b_in[r], 16)
                    pool.dma_start(b2[r][:], d["b2"][bass.ds(q * 2 + r, 1), :].rearrange("o c -> (o c)").partition_broadcast(P)
                                   ).then_inc(b_in[r], 16)

                def fill(q, r):
                    pool.dma_start(raw1[:], d["w1"][bass.ds(q * 2 + r, 1)].rearrange("o (k p) f -> (o p) k f", p=P)
                                   ).then_inc(raw_in, 16)
                    pool.dma_start(raw2[:], d["w2"][bass.ds(q * 2 + r, 1)].rearrange("o (k p) c -> (o p) k c", p=P)
                                   ).then_inc(raw_in, 16)
                    pool.wait_ge(w_used, q * 2 + r + 1)
                    pool.wait_ge(b_used, q * 2 + r + 1)
                    biases(q, r)
                    pool.wait_ge(raw_in, q * 64 + r * 32)
                    settle(pool, keep["passed"])
                    pool.tensor_copy(w1[r][0][:], raw1[:]).then_inc(bv, 1)
                    pool.tensor_copy(w2[r][0][:], raw2[:]).then_inc(bv, 1)
                    pool.wait_ge(bv, q * 4 + r * 2)
                    pool.tensor_tensor(w1[r][1][:], raw1[:], w1[r][0][:], ALU.subtract).then_inc(w_made, 1)
                    pool.tensor_tensor(w2[r][1][:], raw2[:], w2[r][0][:], ALU.subtract).then_inc(w_made, 1)
                    pool.wait_ge(w_made, q * 4 + r * 2 + 2)

                pool.nop().then_inc(w_made, 2)
                biases(0, 0)
                fill(0, 1)
                with pool.Fori(1, E // 2) as q:
                    for r in range(2):
                        fill(q, r)

            @block.tensor
            def _(pe):
                pe.nop().then_inc(w_used, 2)
                pe.nop().then_inc(up_done, 1)
                def turn(n):
                    pe.wait_ge(rows_in, n * 16)
                    pe.wait_ge(xg_done, n)
                    for t in range(XT // P):
                        for k in range(CT):
                            ins = pe.transpose(ps_x[:, k, t * P:(t + 1) * P], rows[:, t, k * P:(k + 1) * P], ident[:])
                    ins.then_inc(turned, 1)

                turn(1)

                def tile(r, i):
                    pe.wait_ge(xl_done, i + 1)
                    for f in range(FT):
                        pe.wait_ge(hf_done, i * FT + (f + 1))
                        n = 0
                        for k in range(CT):
                            for a, m in pieces:
                                ins = pe.matmul(ps_h[f % NHB][:], w1[r][a][:, k, f * P:(f + 1) * P], xT[m][:, k],
                                                start=(n == 0), stop=(n == 3 * CT - 1))
                                n += 1
                        ins.then_inc(h_made, 1)
                    turn(i + 2)
                    pe.wait_ge(o_done, i * 2 + 2)
                    for f in range(FT):
                        pe.wait_ge(hl_done, i * FT + (f + 1 + NHB))
                        for t in range(XT // P):
                            for a, m in pieces:
                                ins = pe.matmul(ps_o[t][:], hT[a][:, f, t * P:(t + 1) * P], w2[r][m][:, f],
                                                start=(f == 0 and (a, m) == pieces[0]),
                                                stop=(f == FT - 1 and (a, m) == pieces[-1]))
                    ins.then_inc(out_made, 1)

                def expert(q, r):
                    pe.wait_ge(w_made, q * 4 + r * 2 + 2)
                    settle(pe, keep["passed"])

                def leave(last):
                    pe.wait_ge(out_made, last)
                    pe.nop().then_inc(w_used, 1)

                each(pe, expert, tile, leave)

            @block.scalar
            def _(act):
                act.nop().then_inc(hf_done, NHB)
                act.nop().then_inc(xg_done, 1)

                def feed(i, n):
                    act.wait_ge(turned, n)
                    for k in range(CT):
                        ins = act.activation(xg[:, k], ps_x[:, k], ACT.Identity, scale=gb[:, 0, k, i], bias=gb[:, 1, k, i])
                    ins.then_inc(xg_done, 1)
                    act.wait_ge(xg_done, n + 1)
                    act.activation(xT[0][:], xg[:], ACT.Copy).then_inc(xh_done, 1)

                feed(slice(0, 1), 1)

                def tile(r, i):
                    for f in range(FT):
                        act.wait_ge(h_made, i * FT + (f + 1))
                        act.wait_ge(hl_done, i * FT + (f + 1))
                        act.activation(hf[:, f % NHB], ps_h[f % NHB][:], ACT.Relu, bias=b1[r][:, f:f + 1]).then_inc(hf_done, 1)
                    feed(bass.ds(i + 1, 1), i + 2)

                def expert(q, r):
                    act.wait_ge(b_in[r], q * 32 + 32)
                    settle(act, keep["passed"])

                each(act, expert, tile)

            @block.vector
            def _(dve):
                dve.nop().then_inc(hl_done, NHB)
                dve.nop().then_inc(o_done, 2)
                dve.nop().then_inc(b_used, 2)

                def feed(n):
                    dve.wait_ge(xh_done, n)
                    dve.tensor_tensor(xT[1][:], xg[:], xT[0][:], ALU.subtract).then_inc(xl_done, 1)

                feed(1)

                def tile(r, i):
                    for f in range(FT):
                        dve.wait_ge(hf_done, i * FT + (f + 1 + NHB))
                        dve.tensor_copy(hT[0][:, f], hf[:, f % NHB]).then_inc(hh_done, 1)
                        dve.wait_ge(hh_done, i * FT + (f + 1))
                        dve.tensor_tensor(hT[1][:, f], hf[:, f % NHB], hT[0][:, f], ALU.subtract).then_inc(hl_done, 1)
                    feed(i + 2)
                    dve.wait_ge(out_made, i + 1)
                    dve.wait_ge(stored, i * 16 + 1)
                    for t in range(XT // P):
                        dve.tensor_tensor(o[:, t], ps_o[t][:], b2[r][:], ALU.add).then_inc(o_done, 1)

                def leave(last):
                    dve.wait_ge(o_done, last * 2 + 2)
                    dve.nop().then_inc(b_used, 1)

                def expert(q, r):
                    dve.wait_ge(b_in[r], q * 32 + 32)
                    settle(dve, keep["passed"])

                each(dve, expert, tile, leave)


def combine(nc, d, keep):
    with ExitStack() as ctx:
        s = Store(nc, ctx, "comb")
        y, xf, wgt, slot = keep["y"], keep["xf"], keep["wgt"], keep["out_slot"]
        SIZES = (8, 8, 6, 6, 4)
        NQ, ENDS = len(SIZES), [sum(SIZES[:q]) for q in range(len(SIZES) + 1)]
        assert ENDS[-1] == TILES
        g = s.sb("g", [P, TILES, K, C])
        acc = s.sb("acc", [P, TILES, C])
        stats = s.sb("stats", [P, TILES, 6])
        mv = s.sb("mv", [P, TILES, 2])
        veps = s.sb("veps", [P, TILES])
        nmean = s.sb("nmean", [P, TILES])
        rstd = s.sb("rstd", [P, TILES])
        shift = s.sb("shift", [P, TILES])
        mhalf = s.sb("mhalf", [P, max(SIZES)])
        zn = s.sb("zn", [P, TILES, C])
        gathered = [s.sem(f"gathered{q}") for q in range(NQ)]
        consts, w0, w1, w2, st, ag, ve, rt, rs, zd, done, stored = (
            s.sem(n) for n in ("consts", "w0", "w1", "w2", "st", "ag", "ve", "rt", "rs", "zd", "done", "stored"))

        def part(q):
            return range(ENDS[q], ENDS[q + 1])

        with nc.Block() as block:
            @block.gpsimd
            def _(pool):
                pool.memset(mhalf[:], -0.5).then_inc(consts, 1)
                pool.wait_ge(consts, 1)

                def roots(q):
                    tiles = slice(ENDS[q], ENDS[q + 1])
                    pool.wait_ge(ag, ENDS[q + 1])
                    pool.tensor_scalar(veps[:, tiles], mv[:, tiles, 1], LN_EPS, None, ALU.add).then_inc(ve, 1)
                    pool.tensor_scalar(nmean[:, tiles], mv[:, tiles, 0], -1.0, None, ALU.mult).then_inc(ve, 1)
                    pool.wait_ge(ve, q * 2 + 2)
                    pool.tensor_tensor(rstd[:, tiles], veps[:, tiles], mhalf[:, 0:SIZES[q]], ALU.pow).then_inc(rt, 1)
                    pool.wait_ge(rt, q + 1)
                    pool.tensor_tensor(shift[:, tiles], nmean[:, tiles], rstd[:, tiles], ALU.mult).then_inc(rs, 1)

                for q in range(NQ):
                    for t in part(q):
                        for k in range(K):
                            pool.indirect_dma_start(g[:, t, k], None, d["ys"],
                                                    bass.IndirectOffsetOnAxis(ap=slot[:, k, t:t + 1], axis=0)
                                                    ).then_inc(gathered[q], 16)
                    if q > 0:
                        roots(q - 1)
                roots(NQ - 1)

            @block.scalar
            def _(act):
                for t in range(TILES):
                    act.activation(acc[:, t], xf[:, t], ACT.Identity, scale=wgt[:, 2, t:t + 1]).then_inc(w0, 1)
                for q in range(NQ):
                    act.wait_ge(rs, q + 1)
                    for t in part(q):
                        act.activation(zn[:, t], acc[:, t], ACT.Identity, scale=rstd[:, t:t + 1], bias=shift[:, t:t + 1]
                                       ).then_inc(zd, 1)

            @block.vector
            def _(dve):
                def attention(q):
                    for t in part(q):
                        dve.wait_ge(zd, t + 1)
                        z = zn[:, t].rearrange("p (g w) -> p g w", g=NG)
                        b = t // TB
                        dve.tensor_tensor(z, z, y[:, b * NG + 1:(b + 1) * NG + 1, t % TB, :], ALU.add).then_inc(done, 1)

                for q in range(NQ):
                    dve.wait_ge(gathered[q], 16 * K * SIZES[q])
                    for t in part(q):
                        dve.wait_ge(w0, t + 1)
                        dve.scalar_tensor_tensor(acc[:, t], g[:, t, 0], wgt[:, 0, t:t + 1], acc[:, t], ALU.mult, ALU.add
                                                 ).then_inc(w1, 1)
                    for t in part(q):
                        dve.wait_ge(w1, t + 1)
                        dve.scalar_tensor_tensor(acc[:, t], g[:, t, 1], wgt[:, 1, t:t + 1], acc[:, t], ALU.mult, ALU.add
                                                 ).then_inc(w2, 1)
                    for t in part(q):
                        dve.wait_ge(w2, t + 1)
                        dve.bn_stats(stats[:, t], acc[:, t]).then_inc(st, 1)
                    for t in part(q):
                        dve.wait_ge(st, t + 1)
                        dve.bn_aggr(mv[:, t], stats[:, t]).then_inc(ag, 1)
                    if q > 1:
                        attention(q - 2)
                for q in range(NQ - 2, NQ):
                    attention(q)

            @block.sync
            def _(sp):
                for q in range(NQ):
                    sp.wait_ge(done, ENDS[q + 1])
                    sp.dma_start(d["out"][ENDS[q] * P:ENDS[q + 1] * P, :].rearrange("(k p) c -> p k c", p=P),
                                 zn[:, ENDS[q]:ENDS[q + 1]]).then_inc(stored, 16)
                sp.wait_ge(stored, 16 * NQ)


_INS = ["x", "wz", "wdq", "wuqT", "wuq", "wuk", "wuv", "woT", "ident", "identb", "mask_ts", "mask_st",
        "wg", "before", "ei", "ti", "etile", "gamma", "beta", "w1", "w2", "b1", "b2"]


def build(nc, d):
    with ExitStack() as ctx:
        s = Store(nc, ctx, "keep")
        keep = {"ident": s.sb("ident", [P, P]), "identb": s.sb("identb", [P, P], BF16),
                "passed": s.sem("passed"),
                "mask_ts": s.sb("mask_ts", [P, P], BF16), "mask_st": s.sb("mask_st", [P, P], BF16)}
        keep["y"] = s.sb("y", [P, B * NG + 1, TB, GH * HS])
        keep["xf"] = s.sb("xf", [P, TILES, C])
        with ExitStack() as inner:
            slots = {part: [] for part in ("q", "k", "v", "loaded", "init")}
            add_slot(slots, Store(nc, inner, "slots"), 0)
            project(nc, d, keep, slots)
            attend(nc, d, keep, slots)
        keep["wgt"] = s.sb("wgt", [P, 3, TILES])
        keep["slot"] = s.sb("slot", [P, K, TILES], mybir.dt.uint32)
        keep["out_slot"] = s.sb("out_slot", [P, K, TILES], mybir.dt.uint32)
        keep["base"] = s.sb("base", [P, E + 1], mybir.dt.int32)
        keep["tile_row"] = s.sb("tile_row", [1, NT + 2], mybir.dt.int32)
        keep["gb"] = s.sb("gb", [P, 2, CT, NT + 2])
        with ExitStack() as inner:
            w = Store(nc, inner, "weights")
            keep["raw1"], keep["raw2"] = w.sb("raw1", [P, CT, F]), w.sb("raw2", [P, FT, C])
            keep["w1_0"] = [w.sb(f"w1_0{p}", [P, CT, F], F32R) for p in "hl"]
            keep["w2_0"] = [w.sb(f"w2_0{p}", [P, FT, C], F32R) for p in "hl"]
            route(nc, d, keep)
            experts(nc, d, keep)
        combine(nc, d, keep)


def kernel(**inputs):
    import concourse.bacc as bacc
    import ml_dtypes
    from concourse.bass_utils import run_bass_kernel_spmd

    w = {k.replace("L0_attn_", "").replace("L0_ffn_", ""): np.asarray(a) for k, a in inputs.items()}
    future = np.triu(np.full((P, P), -1e30, np.float32), 1)
    arrays = {
        "x": w["x"].reshape(N, C),
        "wz": np.concatenate([w["W_dq"].T, w["W_dkv"].T], axis=1),
        "wdq": w["W_dq"], "wuqT": w["W_uq"].T, "wuq": w["W_uq"], "wuk": w["W_uk"], "wuv": w["W_uv"], "woT": w["W_o"].T,
        "ident": np.eye(P, dtype=np.float32), "identb": np.eye(P).astype(ml_dtypes.bfloat16),
        "mask_ts": future.astype(ml_dtypes.bfloat16), "mask_st": future.T.astype(ml_dtypes.bfloat16),
        "wg": w["Wg"], "before": np.triu(np.ones((P, P)), 1).astype(ml_dtypes.bfloat16),
        "ei": np.tile(np.arange(E, dtype=np.float32), (P, 1)),
        "ti": np.tile(np.arange(NT + 2, dtype=np.float32), (E, 1)),
        "etile": (np.arange(E, dtype=np.float32) * (CAP // XT)).reshape(E, 1),
        "gamma": w["gamma"], "beta": w["beta"], "w1": w["W1"], "w2": w["W2"],
        "b1": w["b1"].reshape(E, FT, P).transpose(2, 0, 1), "b2": w["b2"],
    }
    nc = bacc.Bacc("TRN2", target_bir_lowering=False, num_devices=1)
    d = {}
    for name in _INS:
        arrays[name] = np.ascontiguousarray(arrays[name])
        d[name] = nc.dram_tensor(f"in_{name}", arrays[name].shape, mybir.dt.from_np(arrays[name].dtype),
                                 kind="ExternalInput").ap()
    d["qs"] = nc.dram_tensor("qs", (B, 2, NH * HS, T), F32, kind=SCRATCH).ap()
    d["ks"] = nc.dram_tensor("ks", (B, 2, NH * HS, T), F32, kind=SCRATCH).ap()
    d["vs"] = nc.dram_tensor("vs", (B * NG, P, TB, GH * VW), F32, kind=SCRATCH).ap()
    d["rows01"] = nc.dram_tensor("rows01", (2, 2, 2, T), F32, kind=SCRATCH).ap()
    d["xs"] = nc.dram_tensor("xs", (E * CAP, C), F32, kind=SCRATCH).ap()
    d["ys"] = nc.dram_tensor("ys", (NT * XT, C), F32, kind=SCRATCH).ap()
    d["out"] = nc.dram_tensor("out_0", (N, C), F32, kind="ExternalOutput").ap()
    build(nc, d)
    r = run_bass_kernel_spmd(nc, [{f"in_{name}": arrays[name] for name in _INS}], core_ids=[0])
    return r.results[0]["out_0"].reshape(B, T, C)
```
